# Optimizing a Trainium2 kernel written in Bass

```python
import numpy as np
import jax
import jax.numpy as jnp

def _softmax(x, axis=-1):
    return jax.nn.softmax(x, axis=axis)

def _gelu(x):
    return jax.nn.gelu(x, approximate=True)

def _silu(x):
    return jax.nn.silu(x)

def _sigmoid(x):
    return jax.nn.sigmoid(x)

def _layernorm(x, axis=-1, eps=1e-05):
    m = jnp.mean(x, axis=axis, keepdims=True)
    v = jnp.var(x, axis=axis, keepdims=True)
    return (x - m) / jnp.sqrt(v + eps)

def _scatter_add(tgt, idx, src, axis=0):
    return tgt.at[idx].add(src)

def _segment_sum(src, seg, n):
    return jax.ops.segment_sum(src, seg, n)
kernel_name = 'mk_seq_postln_d1_jaxref_r8_838479'

def setup_inputs(seed: int=0):
    np.random.seed(seed)
    _w = jnp.asarray

    def _L0_attn_setup():
        import jax, jax.numpy as jnp
        import numpy as np
        HIDDEN = 512
        N_HEADS = 32
        KV_HEADS = 8
        HEAD_DIM = 128
        LOW_RANK = 64
        TOP_K_ROPE = 32
        ROPE_THETA = 10000.0
        B, S = (2, 256)
        GROUPS = N_HEADS // KV_HEADS
        _half = HEAD_DIM // 2
        _m = np.ones(_half, dtype=bool)
        _m[:TOP_K_ROPE] = False
        _m = np.concatenate([_m, _m])
        NOPE_MASK = np.tile(_m, KV_HEADS)
        ROPE_IDX = jnp.asarray(np.where(~NOPE_MASK)[0])
        NOPE_IDX = jnp.asarray(np.where(NOPE_MASK)[0])
        R_DIM = int((~NOPE_MASK).sum())
        C_DIM = LOW_RANK * KV_HEADS

        def _rope_tables(seq_len, dtype):
            inv_freq = 1.0 / ROPE_THETA ** (np.arange(0, HEAD_DIM, 2, dtype=np.float32) / HEAD_DIM)
            pos = np.arange(seq_len, dtype=np.float32)
            freqs = np.outer(pos, inv_freq)
            emb = np.concatenate([freqs, freqs], axis=-1)
            return (jnp.asarray(np.cos(emb), dtype), jnp.asarray(np.sin(emb), dtype))

        def _rotate_half(x):
            x1, x2 = (x[..., :HEAD_DIM // 2], x[..., HEAD_DIM // 2:])
            return jnp.concatenate([-x2, x1], axis=-1)
        key = jax.random.key(seed)
        ks = jax.random.split(key, 7)
        s = 0.02
        return {'hidden_states': jax.random.normal(ks[0], (B, S, HIDDEN), jnp.float32), 'Wq': jax.random.normal(ks[1], (N_HEADS * HEAD_DIM, HIDDEN), jnp.float32) * s, 'Wkr': jax.random.normal(ks[2], (R_DIM, HIDDEN), jnp.float32) * s, 'Wdk': jax.random.normal(ks[3], (C_DIM, HIDDEN), jnp.float32) * s, 'Wupk': jax.random.normal(ks[4], (KV_HEADS * HEAD_DIM - R_DIM, C_DIM), jnp.float32) * s, 'Wupv': jax.random.normal(ks[5], (KV_HEADS * HEAD_DIM, C_DIM), jnp.float32) * s, 'Wo': jax.random.normal(ks[6], (HIDDEN, N_HEADS * HEAD_DIM), jnp.float32) * s}
    _L0_attn_in = _L0_attn_setup()

    def _L0_ffn_setup():
        import jax, jax.numpy as jnp
        import numpy as np
        GROUP = 64

        def dequant_q40(w, s, out_features, in_features):
            msb = w >> 4
            lsb = (w & 15 ^ 8) - 8
            g = jnp.concatenate([msb, lsb], axis=1).reshape(-1, GROUP)
            deq = g.astype(s.dtype) * s[:, None]
            return deq.reshape(out_features, in_features)
        key = jax.random.key(seed)
        ks = jax.random.split(key, 7)
        dim, hidden = (512, 1376)
        B, S = (2, 256)

        def packed(k, din, dout):
            return jax.random.randint(k, (din * dout // GROUP // 2, GROUP), -128, 128, dtype=jnp.int32)

        def scales(k, din, dout):
            return (jax.random.uniform(k, (din * dout // GROUP,), dtype=jnp.float32) + 0.5) * 0.01
        x = jax.random.normal(ks[0], (B, S, dim), dtype=jnp.float32)
        w1 = packed(ks[1], dim, hidden)
        s1 = scales(ks[2], dim, hidden)
        w2 = packed(ks[3], hidden, dim)
        s2 = scales(ks[4], hidden, dim)
        w3 = packed(ks[5], dim, hidden)
        s3 = scales(ks[6], dim, hidden)
        return {'x': x, 'w1': w1, 's1': s1, 'w2': w2, 's2': s2, 'w3': w3, 's3': s3}
    _L0_ffn_in = _L0_ffn_setup()
    _d = {'L0_attn_hidden_states': _L0_attn_in['hidden_states'], 'L0_attn_Wq': _L0_attn_in['Wq'], 'L0_attn_Wkr': _L0_attn_in['Wkr'], 'L0_attn_Wdk': _L0_attn_in['Wdk'], 'L0_attn_Wupk': _L0_attn_in['Wupk'], 'L0_attn_Wupv': _L0_attn_in['Wupv'], 'L0_attn_Wo': _L0_attn_in['Wo'], 'L0_ffn_w1': _L0_ffn_in['w1'], 'L0_ffn_s1': _L0_ffn_in['s1'], 'L0_ffn_w2': _L0_ffn_in['w2'], 'L0_ffn_s2': _L0_ffn_in['s2'], 'L0_ffn_w3': _L0_ffn_in['w3'], 'L0_ffn_s3': _L0_ffn_in['s3']}
    _x0 = _d['L0_attn_hidden_states']
    _d['L0_attn_hidden_states'] = jax.random.normal(jax.random.fold_in(jax.random.key(seed), 1), (2, 1024, 512), dtype=_x0.dtype)
    del _x0
    return _d

def reference(L0_attn_hidden_states, L0_attn_Wq, L0_attn_Wkr, L0_attn_Wdk, L0_attn_Wupk, L0_attn_Wupv, L0_attn_Wo, L0_ffn_w1, L0_ffn_s1, L0_ffn_w2, L0_ffn_s2, L0_ffn_w3, L0_ffn_s3):

    def _L0_attn_ref(hidden_states, Wq, Wkr, Wdk, Wupk, Wupv, Wo):
        import jax, jax.numpy as jnp
        import numpy as np
        HIDDEN = 512
        N_HEADS = 32
        KV_HEADS = 8
        HEAD_DIM = 128
        LOW_RANK = 64
        TOP_K_ROPE = 32
        ROPE_THETA = 10000.0
        B, S = (2, 256)
        GROUPS = N_HEADS // KV_HEADS
        _half = HEAD_DIM // 2
        _m = np.ones(_half, dtype=bool)
        _m[:TOP_K_ROPE] = False
        _m = np.concatenate([_m, _m])
        NOPE_MASK = np.tile(_m, KV_HEADS)
        ROPE_IDX = jnp.asarray(np.where(~NOPE_MASK)[0])
        NOPE_IDX = jnp.asarray(np.where(NOPE_MASK)[0])
        R_DIM = int((~NOPE_MASK).sum())
        C_DIM = LOW_RANK * KV_HEADS

        def _rope_tables(seq_len, dtype):
            inv_freq = 1.0 / ROPE_THETA ** (np.arange(0, HEAD_DIM, 2, dtype=np.float32) / HEAD_DIM)
            pos = np.arange(seq_len, dtype=np.float32)
            freqs = np.outer(pos, inv_freq)
            emb = np.concatenate([freqs, freqs], axis=-1)
            return (jnp.asarray(np.cos(emb), dtype), jnp.asarray(np.sin(emb), dtype))

        def _rotate_half(x):
            x1, x2 = (x[..., :HEAD_DIM // 2], x[..., HEAD_DIM // 2:])
            return jnp.concatenate([-x2, x1], axis=-1)
        bsz, q_len, _ = hidden_states.shape
        dt = hidden_states.dtype
        q = (hidden_states @ Wq.T).reshape(bsz, q_len, N_HEADS, HEAD_DIM).transpose(0, 2, 1, 3)
        k_r0 = hidden_states @ Wkr.T
        key_flat = jnp.zeros((bsz, q_len, KV_HEADS * HEAD_DIM), dt).at[..., ROPE_IDX].set(k_r0)
        k = key_flat.reshape(bsz, q_len, KV_HEADS, HEAD_DIM).transpose(0, 2, 1, 3)
        cos, sin = _rope_tables(q_len, dt)
        cos, sin = (cos[None, None], sin[None, None])
        q = q * cos + _rotate_half(q) * sin
        k = k * cos + _rotate_half(k) * sin
        k_r = k.transpose(0, 2, 1, 3).reshape(bsz, q_len, KV_HEADS * HEAD_DIM)[..., ROPE_IDX]
        c_kv = hidden_states @ Wdk.T
        k_c = c_kv @ Wupk.T
        v = (c_kv @ Wupv.T).reshape(bsz, q_len, KV_HEADS, HEAD_DIM).transpose(0, 2, 1, 3)
        key_full = jnp.zeros((bsz, q_len, KV_HEADS * HEAD_DIM), dt).at[..., NOPE_IDX].set(k_c).at[..., ROPE_IDX].set(k_r)
        k = key_full.reshape(bsz, q_len, KV_HEADS, HEAD_DIM).transpose(0, 2, 1, 3)
        k = jnp.repeat(k, GROUPS, axis=1)
        v = jnp.repeat(v, GROUPS, axis=1)
        scale = 1.0 / jnp.sqrt(jnp.asarray(HEAD_DIM, dt))
        scores = jnp.einsum('bhqd,bhkd->bhqk', q, k) * scale
        causal = jnp.tril(jnp.ones((q_len, q_len), bool))
        scores = jnp.where(causal[None, None], scores, jnp.asarray(-1000000000.0, dt))
        attn = jax.nn.softmax(scores, axis=-1)
        out = jnp.einsum('bhqk,bhkd->bhqd', attn, v)
        out = out.transpose(0, 2, 1, 3).reshape(bsz, q_len, N_HEADS * HEAD_DIM)
        return out @ Wo.T

    def _L0_ffn_ref(x, w1, s1, w2, s2, w3, s3):
        import jax, jax.numpy as jnp
        import numpy as np
        GROUP = 64

        def dequant_q40(w, s, out_features, in_features):
            msb = w >> 4
            lsb = (w & 15 ^ 8) - 8
            g = jnp.concatenate([msb, lsb], axis=1).reshape(-1, GROUP)
            deq = g.astype(s.dtype) * s[:, None]
            return deq.reshape(out_features, in_features)
        dim = x.shape[-1]
        hidden = w1.shape[0] * w1.shape[1] * 2 // dim
        W1 = dequant_q40(w1, s1, hidden, dim)
        W3 = dequant_q40(w3, s3, hidden, dim)
        W2 = dequant_q40(w2, s2, dim, hidden)
        a = jnp.einsum('bsd,hd->bsh', x, W1)
        b = jnp.einsum('bsd,hd->bsh', x, W3)
        h = jax.nn.silu(a) * b
        return jnp.einsum('bsh,dh->bsd', h, W2)
    x = L0_attn_hidden_states
    x = _layernorm(x + _L0_attn_ref(x, L0_attn_Wq, L0_attn_Wkr, L0_attn_Wdk, L0_attn_Wupk, L0_attn_Wupv, L0_attn_Wo), axis=-1)
    x = _layernorm(x + _L0_ffn_ref(x, L0_ffn_w1, L0_ffn_s1, L0_ffn_w2, L0_ffn_s2, L0_ffn_w3, L0_ffn_s3), axis=-1)
    return x

_drawn_inputs = setup_inputs


def setup_inputs(seed=0):
    import zlib

    import numpy as np

    out = dict(_drawn_inputs(seed))
    spreads = {}
    factors = {'L0_attn_Wq': 8.0, 'L0_attn_Wkr': 8.0, 'L0_attn_Wupk': 8.0}
    for name, (base, spread) in spreads.items():
        noise = np.random.default_rng([zlib.crc32(name.encode()), seed]).standard_normal(out[name].shape)
        drawn = base * np.exp(spread * noise) if base else spread * noise
        out[name] = jnp.asarray(drawn.astype(out[name].dtype))
    for name, factor in factors.items():
        out[name] = (out[name] * factor).astype(out[name].dtype)
    return out
```

```python
from contextlib import ExitStack

import numpy as np
import concourse.bass as bass
from concourse import mybir

F32 = mybir.dt.float32
F32R = mybir.dt.float32r
I32 = mybir.dt.int32
ALU = mybir.AluOpType
ACT = mybir.ActivationFunctionType

B, S, D = 2, 1024, 512
HEADS, KV, HD = 32, 8, 128
GQ = HEADS // KV
GROUPS = B * KV
C = 512
F = 1376
P = 128
DC = D // P
TB = 512
NBLK = B * S // TB
QT = S // P
FT = (F + P - 1) // P
HI, LO = 0, 1
PASSES = ((HI, HI), (HI, LO), (LO, HI))
SCALE = float(1.0 / np.sqrt(np.float32(HD)))
MASKED = -1.0e30
EPS = 1e-5

CELLS = QT * GQ
LAG = 3
STEPS = 40
S_RING = 4
PT_UNITS = 3


def pieces(c):
    i = c // GQ
    first = c if i < 4 else 16 + 2 * (c - 16)
    out = [(first, 0, min(4, i + 1))]
    if i >= 4:
        out.append((first + 1, 4, i - 3))
    return out


PIECES = 48


def unit_of(i, j0):
    return i if i < 4 else 4 + 2 * (i - 4) + j0 // 4


UNITS = 12
UNIT_TILE = [0, 1, 2, 3, 4, 4, 5, 5, 6, 6, 7, 7]


def bank_uses(step, last):
    out = []
    for h, s in enumerate((1, 3, 5, 8)):
        if s == step:
            out.append(("q", 1, h))
    if step >= 7 and (step - 7) % 4 == 0 and (step - 7) // 4 < QT:
        out.append(("pv", (step - 7) // 4, 0))
    if step >= 9 and (step - 9) % 4 == 0 and (step - 9) // 4 < QT:
        out.append(("wo", (step - 9) // 4, 0))
    if not last:
        for h, s in enumerate((32, 33, 34, 36)):
            if s == step:
                out.append(("q", 0, h))
    return out


def use_numbers(last):
    n, out = 0, {}
    for s in range(STEPS):
        for k, _ in enumerate(bank_uses(s, last)):
            out[s, k] = n
            n += 1
    return out, n


USES = use_numbers(False)[1]


def acts(step, last):
    numbers = use_numbers(last)[0]
    return [(numbers[step, k], *u) for k, u in enumerate(bank_uses(step, last))] if step >= 0 else []


def use_of(kind, a, last):
    return next(n for s in range(STEPS) for n, k, b, _ in acts(s, last) if (k, b) == (kind, a))


def program(nc, x, xT, wqT, wkrT, wdkT, wupkT, wupvT, woT, w1p, s1p, w3p, s3p, w2p, s2p, cosT, sinT, shifts, out):
    xs_d = nc.dram_tensor("xs_d", [NBLK, P, 2, DC, TB], F32).ap()
    k_d = nc.dram_tensor("k_d", [GROUPS // 4, 4, P, 2, S], F32).ap()
    v_d = nc.dram_tensor("v_d", [GROUPS, P, QT, 2, HD], F32).ap()
    y_d = nc.dram_tensor("y_d", [B, QT, P, D], F32).ap()
    x1_d = nc.dram_tensor("x1_d", [NBLK, 4, P, D], F32).ap()
    x1s_d = nc.dram_tensor("x1s_d", [NBLK, P, 2, DC, TB], F32).ap()

    stage_a(nc, x, xT, wkrT, wdkT, wupkT, wupvT, cosT, sinT, xs_d, k_d, v_d, y_d)
    stage_b(nc, wqT, woT, cosT, sinT, xs_d, k_d, v_d, y_d)
    stage_c(nc, y_d, x1_d, x1s_d)
    stage_d(nc, w1p, s1p, w3p, s3p, w2p, s2p, shifts, x1_d, x1s_d, out)


def words(ap):
    return ap.bitcast(F32)


def three_pass(nc, out, pairs, split=PASSES):
    n, last = 0, len(pairs) * len(split)
    for lhsT, rhs in pairs:
        for a, b in split:
            ins = nc.tensor.matmul(out, lhsT(a), rhs(b), start=(n == 0), stop=(n == last - 1))
            n += 1
    return ins


def stage_a(nc, x, xT, wkrT, wdkT, wupkT, wupvT, cosT, sinT, xs_d, k_d, v_d, y_d):
    with ExitStack() as ctx:
        def sb(name, shape, dt):
            return ctx.enter_context(nc.sbuf_tensor(name, shape, dt))

        def sem(name):
            return ctx.enter_context(nc.semaphore(name))

        raw = sb("a_raw", [P, 2, DC, 512], F32)
        wdk = sb("a_wdk", [P, 2, DC, 512], F32R)
        wkr = sb("a_wkr", [P, 2, DC, 512], F32R)
        wupk = sb("a_wupk", [P, 2, DC, 512], F32R)
        wupv = sb("a_wupv", [P, 2, 2, DC, 512], F32R)
        xraw = sb("a_xraw", [P, DC, TB], F32)
        xs = sb("a_xs", [P, 2, DC, TB], F32R)
        cs = sb("a_cs", [P, 2, DC, TB], F32R)
        cosk = sb("a_cos", [P, S], F32)
        sink = sb("a_sin", [P, S], F32)
        rt = sb("a_rt", [P, 4, TB], F32)
        kf = sb("a_kf", [P, 2, TB], F32)
        ks = sb("a_ks", [P, 4, 2, TB], F32R)
        vs = sb("a_vs", [P, 2, 4, 2, HD], F32R)
        RING = 5
        bank = [ctx.enter_context(nc.psum_tensor(f"a_ps{i}", [P, TB], F32)) for i in range(RING)]

        w_in = [sem("a_w_in0"), sem("a_w_in1")]
        tab_in, x_in = sem("a_tab_in"), sem("a_x_in")
        w_hi, w_lo = sem("a_w_hi"), sem("a_w_lo")
        x_hi, x_lo = sem("a_x_hi"), sem("a_x_lo")
        mm = sem("a_mm")
        bank_free = sem("a_bank_free")
        part_hi = sem("a_part_hi")
        rope_t, rope_done = sem("a_rope_t"), sem("a_rope_done")
        kr_lo = sem("a_kr_lo")
        k_out, xs_out, y_out = sem("a_k_out"), sem("a_xs_out"), sem("a_y_out")
        v_out = [sem("a_v_out0"), sem("a_v_out1")]

        MM0, FREE0, KRLO0, XLO0, OUT0 = 20, RING, 2, 1, 1
        WEIGHTS = [(wdkT, None, wdk), (wkrT, None, wkr), (wupkT, None, wupk), (wupvT, 0, wupv), (wupvT, 1, wupv)]
        NW = len(WEIGHTS)
        CG, RG, NG, VG, GROUPS_A = 0, 4, 8, 12, 20

        def weight_part(n):
            _s, half, w = WEIGHTS[n]
            return (lambda p: w[:, p]) if half is None else (lambda p: w[:, half, p])

        block = ctx.enter_context(nc.Block())

        @block.sync
        def _(sp):
            for g in range(4):
                sp.dma_start(cosk[32 * g:32 * g + 32, :], cosT[0:32, :]).then_inc(tab_in, 16)
                sp.dma_start(sink[32 * g:32 * g + 32, :], sinT[64:96, :]).then_inc(tab_in, 16)
            for n, (src, half, _w) in enumerate(WEIGHTS):
                if n >= 2:
                    sp.wait_ge(w_lo, n - 1)
                s = src if half is None else src[:, :, half * 512:half * 512 + 512]
                sp.dma_start(raw[:, n % 2], s).then_inc(w_in[n % 2], 16)
            sp.dma_start(y_d.rearrange("b i p d -> (b i p) d"), x.rearrange("b s d -> (b s) d")).then_inc(y_out, 16)
            with sp.Fori(0, NBLK) as t:
                sp.wait_ge(x_lo, t + 1 + XLO0)
                sp.dma_start(xs_d[t], words(xs[:])).then_inc(xs_out, 16)
                for n in range(8):
                    quad, part = n // 2 % 2, 2 * (n % 2) + n // 4
                    if n < 4:
                        sp.wait_ge(kr_lo, 4 * t + n + 1 + KRLO0)
                    else:
                        sp.wait_ge(bank_free, GROUPS_A * t + NG + (n - 4) + 1 + FREE0)
                    sp.dma_start(k_d[(t // 2) * 2 + quad, part, :, :, bass.ds((t % 2) * TB, TB)],
                                 words(ks[:, n % 4])).then_inc(k_out, 16)
                for n in range(8):
                    sp.wait_ge(bank_free, GROUPS_A * t + VG + n + 1 + FREE0)
                    sp.dma_start(
                        v_d[bass.ds((t // 2) * KV + 4 * (n % 2), 4), :, (t % 2) * 4 + n // 2]
                        .rearrange("g p l d -> p g (l d)"),
                        words(vs[:, n % 2]).rearrange("p g l d -> p g (l d)")).then_inc(v_out[n % 2], 16)
            sp.wait_ge(xs_out, 16 * NBLK + OUT0)
            sp.wait_ge(k_out, 16 * 8 * NBLK + OUT0)
            for p in range(2):
                sp.wait_ge(v_out[p], 16 * 4 * NBLK + OUT0)
            sp.wait_ge(y_out, 16)

        @block.gpsimd
        def _(pool):
            pool.sem_inc(x_lo, XLO0)
            pool.sem_inc(kr_lo, KRLO0)
            pool.dma_start(xraw[:], xT[0]).then_inc(x_in, 16)
            for n in range(NW):
                pool.wait_ge(w_hi, n + 1)
                w = weight_part(n)
                nc.gpsimd.tensor_tensor(w(LO), raw[:, n % 2], w(HI), ALU.subtract).then_inc(w_lo, 1)

            def rope_lo(t):
                for n in range(4):
                    pool.wait_ge(part_hi, GROUPS_A * t + RG + n + 1)
                    nc.gpsimd.tensor_tensor(ks[:, n, LO], kf[:, n % 2], ks[:, n, HI], ALU.subtract).then_inc(kr_lo, 1)

            with pool.Fori(0, NBLK - 1) as t:
                rope_lo(t)
                pool.wait_ge(x_lo, t + 1 + XLO0)
                pool.dma_start(xraw[:], xT[t + 1]).then_inc(x_in, 16)
            rope_lo(NBLK - 1)

        @block.scalar
        def _(act):
            act.sem_inc(xs_out, OUT0)
            act.sem_inc(k_out, OUT0)
            act.sem_inc(v_out[0], OUT0)
            act.sem_inc(v_out[1], OUT0)
            for n in range(NW):
                act.wait_ge(w_in[n % 2], 16 * (n // 2 + 1))
                w = weight_part(n)
                nc.scalar.activation(w(HI), raw[:, n % 2], ACT.Copy).then_inc(w_hi, 1)
            with act.Fori(0, NBLK) as t:
                act.wait_ge(x_in, 16 * t + 16)
                act.wait_ge(mm, GROUPS_A * t + NG)
                act.wait_ge(xs_out, 16 * t + OUT0)
                nc.scalar.activation(xs[:, HI], xraw[:], ACT.Copy).then_inc(x_hi, 1)
                for m in range(DC):
                    act.wait_ge(mm, GROUPS_A * t + CG + m + 1 + MM0)
                    nc.scalar.activation(cs[:, HI, m], bank[(CG + m) % RING][:], ACT.Copy).then_inc(part_hi, 1)
                act.wait_ge(k_out, 16 * 8 * t + OUT0)
                for n in range(4):
                    act.wait_ge(rope_done, 4 * t + n + 1)
                    nc.scalar.activation(ks[:, n, HI], kf[:, n % 2], ACT.Copy).then_inc(part_hi, 1)
                act.wait_ge(k_out, 16 * (8 * t + 4) + OUT0)
                for n in range(4):
                    act.wait_ge(mm, GROUPS_A * t + NG + n + 1 + MM0)
                    nc.scalar.activation(ks[:, n, HI], bank[(NG + n) % RING][:], ACT.Copy).then_inc(part_hi, 1)
                for n in range(8):
                    act.wait_ge(mm, GROUPS_A * t + VG + n + 1 + MM0)
                    act.wait_ge(v_out[n % 2], 16 * (4 * t + n // 2) + OUT0)
                    nc.scalar.activation(vs[:, n % 2, :, HI, :], bank[(VG + n) % RING][:].rearrange("p (g d) -> p g d", g=4),
                                         ACT.Copy).then_inc(part_hi, 1)

        @block.vector
        def _(dve):
            dve.sem_inc(bank_free, FREE0)
            dve.wait_ge(tab_in, 16 * 8)
            with dve.Fori(0, NBLK) as t:
                dve.wait_ge(x_hi, t + 1)
                nc.vector.tensor_tensor(xs[:, LO], xraw[:], xs[:, HI], ALU.subtract).then_inc(x_lo, 1)
                for m in range(DC):
                    dve.wait_ge(part_hi, GROUPS_A * t + CG + m + 1)
                    nc.vector.tensor_tensor(cs[:, LO, m], bank[(CG + m) % RING][:], cs[:, HI, m],
                                            ALU.subtract).then_inc(bank_free, 1)
                cos_t, sin_t = (w[:, bass.ds((t % 2) * TB, TB)] for w in (cosk, sink))
                for quad in range(2):
                    if quad == 1:
                        dve.wait_ge(rope_done, 4 * t + 2)
                    for k in range(2):
                        g = RG + 2 * quad + k
                        dve.wait_ge(mm, GROUPS_A * t + g + 1 + MM0)
                        nc.vector.tensor_tensor(rt[:, 2 * k], bank[g % RING][:], cos_t, ALU.mult).then_inc(rope_t, 1)
                        nc.vector.tensor_tensor(rt[:, 2 * k + 1], bank[g % RING][:], sin_t, ALU.mult).then_inc(bank_free, 1)
                    dve.wait_ge(rope_t, 4 * t + 2 * quad + 2)
                    dve.wait_ge(bank_free, GROUPS_A * t + RG + 2 * quad + 2 + FREE0)
                    for k, (a, b, op) in enumerate(((0, 3, ALU.subtract), (2, 1, ALU.add))):
                        dve.wait_ge(kr_lo, 4 * t + 2 * quad + k + 1)
                        nc.vector.tensor_tensor(kf[:, k], rt[:, a], rt[:, b], op).then_inc(rope_done, 1)
                for n in range(4):
                    dve.wait_ge(part_hi, GROUPS_A * t + NG + n + 1)
                    nc.vector.tensor_tensor(ks[:, n, LO], bank[(NG + n) % RING][:], ks[:, n, HI],
                                            ALU.subtract).then_inc(bank_free, 1)
                for n in range(8):
                    dve.wait_ge(part_hi, GROUPS_A * t + VG + n + 1)
                    nc.vector.tensor_tensor(vs[:, n % 2, :, LO, :], bank[(VG + n) % RING][:].rearrange("p (g d) -> p g d", g=4),
                                            vs[:, n % 2, :, HI, :], ALU.subtract).then_inc(bank_free, 1)

        @block.tensor
        def _(pe):
            pe.sem_inc(mm, MM0)

            def group(t, g, pairs):
                pe.wait_ge(bank_free, GROUPS_A * t + g + 1)
                three_pass(nc, bank[g % RING][:], pairs).then_inc(mm, 1)

            def project(w, m, src):
                return [(lambda p, k=k: w(p)[:, k, m * P:(m + 1) * P], lambda p, k=k: src[:, p, k]) for k in range(DC)]

            with pe.Fori(0, NBLK) as t:
                pe.wait_ge(x_lo, t + 1 + XLO0)
                pe.wait_ge(w_lo, 1)
                for m in range(4):
                    group(t, CG + m, project(weight_part(0), m, xs))
                pe.wait_ge(w_lo, 2)
                for m in range(4):
                    group(t, RG + m, project(weight_part(1), m, xs))
                pe.wait_ge(w_lo, 3)
                pe.wait_ge(bank_free, GROUPS_A * t + CG + 4 + FREE0)
                for m in range(4):
                    group(t, NG + m, project(weight_part(2), m, cs))
                pe.wait_ge(w_lo, NW)
                for n in range(8):
                    w, tt = weight_part(3 + n % 2), n // 2
                    group(t, VG + n, [(lambda p, k=k: cs[:, p, k, tt * P:(tt + 1) * P], lambda p, k=k: w(p)[:, k])
                                      for k in range(DC)])


def stage_b(nc, wqT, woT, cosT, sinT, xs_d, k_d, v_d, y_d):
    with ExitStack() as ctx:
        def sb(name, shape, dt):
            return ctx.enter_context(nc.sbuf_tensor(name, shape, dt))

        def sem(name):
            return ctx.enter_context(nc.semaphore(name))

        xs = sb("b_xs", [P, 2, DC, TB], F32R)
        kt = sb("b_kt", [P, 2, S], F32R)
        vt = sb("b_vt", [P, QT, 2, HD], F32R)
        wraw = sb("b_wraw", [P, 2, 512], F32)
        wq = sb("b_wq", [P, GQ, 2, DC, HD], F32R)
        wo = sb("b_wo", [P, GQ, 2, D], F32R)
        qs = sb("b_qs", [P, 2, GQ, 2, TB], F32R)
        sw = sb("b_sw", [P, TB], F32)
        qf = sb("b_qf", [P, TB], F32)
        cosq = sb("b_cos", [P, S], F32)
        sinq = sb("b_sin", [P, S], F32)
        mask = sb("b_mask", [P, S], F32)
        ident = sb("b_ident", [P, P], F32)
        sc = sb("b_sc", [P, S_RING, S], F32)
        spare = sb("b_spare", [P, LAG + 1], F32)
        nmax = sb("b_nmax", [P, S_RING], F32)
        rsum = sb("b_rsum", [P, S_RING], F32)
        rinv = sb("b_rinv", [P, S_RING], F32)
        pt = sb("b_pt", [P, PT_UNITS, 2, 4, GQ * P], F32R)
        ot = sb("b_ot", [P, 2, 2, GQ * P], F32R)
        ys = sb("b_ys", [P, 2, D], F32)
        sps = [ctx.enter_context(nc.psum_tensor(f"b_sps{i}", [P, S], F32)) for i in range(2)]
        tps = [ctx.enter_context(nc.psum_tensor(f"b_tps{i}", [P, 4, P], F32)) for i in range(2)]
        bank = [ctx.enter_context(nc.psum_tensor(f"b_ps{i}", [P, 512], F32)) for i in range(2)]

        tab_in, masked = sem("b_tab_in"), sem("b_masked")
        k_in, v_in, xs_in = sem("b_k_in"), sem("b_v_in"), sem("b_xs_in")
        w_in = [sem("b_w_in0"), sem("b_w_in1")]
        w_hi, w_lo = sem("b_w_hi"), sem("b_w_lo")
        y_in, y_out = [sem("b_y_in0"), sem("b_y_in1")], [sem("b_y_out0"), sem("b_y_out1")]
        s_done = sem("b_s_done")
        sc_done = sem("b_sc_done")
        exp_done, rinv_done, norm_done = sem("b_exp_done"), sem("b_rinv_done"), sem("b_norm_done")
        t_done = sem("b_t_done")
        pt_hi, pt_lo = sem("b_pt_hi"), sem("b_pt_lo")
        q_mm = sem("b_q_mm")
        sw_done, sin_done, add_done = sem("b_sw_done"), sem("b_sin_done"), sem("b_add_done")
        q_hi, q_lo = sem("b_q_hi"), sem("b_q_lo")
        pv_done, ot_hi, wo_done = sem("b_pv_done"), sem("b_ot_hi"), sem("b_wo_done")
        bank_free = sem("b_bank_free")

        SC0, TD0, PTLO0, PV0, WO0, ADD0, QLO0, FREE0, YO0, WL0 = 2, 8, 2, 2, 8, 1, 1, 2, 1, 2
        LAST = GROUPS - 1
        WPG = 8

        def thru(c):
            return pieces(c)[-1][0] + 1 if c >= 0 else pieces(c + CELLS)[-1][0] + 1 - PIECES

        def scores_width(i):
            w = P * (i + 1)
            return [(0, max(w, 256))] if w <= 512 else [(0, 512), (512, max(w, 768))]

        def q_number(blk, h):
            return 4 * blk + h

        FIRST_USES = GQ

        block = ctx.enter_context(nc.Block())

        @block.sync
        def _(sp):
            def load_wq(it, h, par):
                sp.wait_ge(w_lo, WPG * it + h + 1)
                sp.dma_start(wraw[:, par].rearrange("p (k m) -> p k m", k=DC), wqT[(it % KV) * GQ + h])\
                    .then_inc(w_in[par], 16)

            def load_wo(it, h, par):
                sp.wait_ge(w_lo, WPG * it + 4 + h + 1)
                sp.dma_start(wraw[:, par], woT[(it % KV) * GQ + h]).then_inc(w_in[par], 16)

            def load_k(it):
                for part in range(4):
                    sp.dma_start(words(kt[32 * part:32 * part + 32]), k_d[it // 4, part, bass.ds((it % 4) * 32, 32)])\
                        .then_inc(k_in, 16)

            def load_xs(it, blk):
                sp.dma_start(words(xs[:]), xs_d[(it // KV) * 2 + blk]).then_inc(xs_in, 16)

            def load_y(it, i):
                sp.wait_ge(y_out[i % 2], 16 * (4 * it + i // 2) + YO0)
                sp.dma_start(ys[:, i % 2], y_d[it // KV, i]).then_inc(y_in[i % 2], 16)

            def store_y(it, i, last):
                n = use_of("wo", i, last)
                sp.wait_ge(bank_free, USES * it + FIRST_USES + n + 1 + FREE0)
                sp.dma_start(y_d[it // KV, i], ys[:, i % 2]).then_inc(y_out[i % 2], 16)

            def load_v(it):
                sp.dma_start(words(vt[:]), v_d[it]).then_inc(v_in, 16)

            def load_rest(it):
                sp.wait_ge(q_mm, 8 * it + 4)
                load_xs(it, 1)
                load_wo(it, 0, 0)
                load_wo(it, 1, 1)
                load_y(it, 0)
                load_y(it, 1)

            def group(it, last):
                for step in range(STEPS):
                    if step in (1, 2):
                        load_wo(it, step + 1, (step + 1) % 2)
                    if not last:
                        if step == 12:
                            sp.wait_ge(q_mm, 8 * it + 8)
                            load_xs(it + 1, 0)
                        if 12 <= step < 16:
                            load_wq(it + 1, step - 12, step % 2)
                        if step == 32:
                            sp.wait_ge(s_done, CELLS * (it + 1))
                            load_k(it + 1)
                        if step == 36:
                            sp.wait_ge(pv_done, QT * (it + 1) + PV0)
                            load_v(it + 1)
                    i = (step - 10) // 4
                    if step >= 10 and (step - 10) % 4 == 0 and i < QT:
                        store_y(it, i, last)
                        if i + 2 < QT:
                            load_y(it, i + 2)
                if not last:
                    load_rest(it + 1)

            sp.dma_start(cosq[:], cosT).then_inc(tab_in, 16)
            sp.dma_start(sinq[:], sinT).then_inc(tab_in, 16)
            load_xs(0, 0)
            for h in range(GQ):
                load_wq(0, h, h % 2)
            load_k(0)
            load_v(0)
            load_rest(0)
            group(0, False)
            with sp.Fori(1, LAST) as it:
                group(it, False)
            group(LAST, True)
            for p in range(2):
                sp.wait_ge(y_out[p], 16 * 4 * GROUPS + YO0)

        @block.gpsimd
        def _(pool):
            pool.sem_inc(w_lo, WL0)
            pool.sem_inc(q_lo, QLO0)
            nc.gpsimd.memset(mask[:], 0.0).then_inc(masked, 1)
            nc.gpsimd.memset(ident[:], 0.0).then_inc(masked, 1)
            pool.wait_ge(masked, 2)
            nc.gpsimd.affine_select(out=mask[:, S - P:S], in_=mask[:, S - P:S], compare_op=ALU.is_ge, fill=MASKED,
                                    base=0, pattern=[[-1, P]], channel_multiplier=1).then_inc(masked, 1)
            nc.gpsimd.affine_select(out=ident[:], in_=ident[:], compare_op=ALU.not_equal, fill=1.0,
                                    base=0, pattern=[[-1, P]], channel_multiplier=1).then_inc(masked, 1)
            pool.wait_ge(tab_in, 32)

            def times_sin(it, blk, h):
                pool.wait_ge(sw_done, 2 * (8 * it + q_number(blk, h) + 1))
                nc.gpsimd.tensor_tensor(sw[:], sw[:], sinq[:, blk % 2 * TB:blk % 2 * TB + TB], ALU.mult)\
                    .then_inc(sin_done, 1)

            def split_q(it, blk, h):
                pool.wait_ge(q_hi, 8 * it + q_number(blk, h) + 1)
                nc.gpsimd.tensor_tensor(qs[:, blk % 2, h, LO], qf[:], qs[:, blk % 2, h, HI], ALU.subtract)\
                    .then_inc(q_lo, 1)

            def split_wq(it, h, par):
                pool.wait_ge(w_hi, WPG * it + h + 1)
                nc.gpsimd.tensor_tensor(wq[:, h, LO].rearrange("p k m -> p (k m)"), wraw[:, par],
                                        wq[:, h, HI].rearrange("p k m -> p (k m)"), ALU.subtract).then_inc(w_lo, 1)

            def split_wo(it, h, par):
                pool.wait_ge(w_hi, WPG * it + 4 + h + 1)
                nc.gpsimd.tensor_tensor(wo[:, h, LO], wraw[:, par], wo[:, h, HI], ALU.subtract).then_inc(w_lo, 1)

            def group(it, last):
                for step in range(STEPS):
                    if step < GQ:
                        split_wo(it, step, step % 2)
                    if not last and 13 <= step < 17:
                        split_wq(it + 1, step - 13, (step - 13) % 2)
                    for _n, kind, blk, h in acts(step - 2, last):
                        if kind == "q":
                            split_q(it, blk if blk else 2, h)
                    for _n, kind, blk, h in acts(step - 1, last):
                        if kind == "q":
                            times_sin(it, blk if blk else 2, h)

            for h in range(GQ):
                split_wq(0, h, h % 2)
            for h in range(GQ):
                times_sin(0, 0, h)
                split_q(0, 0, h)
            group(0, False)
            with pool.Fori(1, LAST) as it:
                group(it, False)
            group(LAST, True)

        @block.scalar
        def _(act):
            act.sem_inc(y_out[0], YO0)
            act.sem_inc(y_out[1], YO0)

            def swap_q(it, blk, h, bk):
                n = 8 * it + q_number(blk, h)
                act.wait_ge(q_mm, n + 1)
                act.wait_ge(add_done, n + 1)
                nc.scalar.activation(sw[0:64], bank[bk][64:128], ACT.Copy).then_inc(sw_done, 1)
                nc.scalar.activation(sw[64:128], bank[bk][0:64], ACT.Copy).then_inc(sw_done, 1)

            def hi_q(it, blk, h):
                n = 8 * it + q_number(blk, h)
                act.wait_ge(add_done, n + 1 + ADD0)
                nc.scalar.activation(qs[:, blk % 2, h, HI], qf[:], ACT.Copy).then_inc(q_hi, 1)

            def hi_wq(it, h, par, prev_uses):
                act.wait_ge(w_in[par], 16 * (4 * it + h // 2 + 1))
                if prev_uses is not None:
                    act.wait_ge(q_mm, prev_uses)
                nc.scalar.activation(wq[:, h, HI].rearrange("p k m -> p (k m)"), wraw[:, par], ACT.Copy).then_inc(w_hi, 1)

            def hi_wo(it, h, par):
                act.wait_ge(w_in[par], 16 * (4 * it + 2 + h // 2 + 1))
                act.wait_ge(wo_done, QT * it + WO0)
                nc.scalar.activation(wo[:, h, HI], wraw[:, par], ACT.Copy).then_inc(w_hi, 1)

            def exp(it, c):
                slot, w = c % S_RING, P * (c // GQ + 1)
                act.wait_ge(sc_done, CELLS * it + c + 1 + SC0)
                nc.scalar.activation(sc[:, slot, 0:w], sc[:, slot, 0:w], ACT.Exp, bias=nmax[:, slot:slot + 1], scale=-1.0,
                                     accum_out=rsum[:, slot:slot + 1]).then_inc(exp_done, 1)

            def normalise(it, c):
                slot, w = c % S_RING, P * (c // GQ + 1)
                act.wait_ge(rinv_done, CELLS * it + c + 1)
                nc.scalar.activation(sc[:, slot, 0:w], sc[:, slot, 0:w], ACT.Copy, scale=rinv[:, slot:slot + 1])\
                    .then_inc(norm_done, 1)

            def hi_pt(it, c):
                i, h = c // GQ, c % GQ
                for n, j0, nj in pieces(c):
                    u = unit_of(i, j0)
                    act.wait_ge(t_done, PIECES * it + n + 1 + TD0)
                    if h == 0:
                        tile = UNIT_TILE[(u - PT_UNITS) % UNITS] - (QT if u < PT_UNITS else 0)
                        act.wait_ge(pv_done, QT * it + tile + 1 + PV0)
                    nc.scalar.activation(pt[:, u % PT_UNITS, HI, 0:nj, h * P:(h + 1) * P], tps[n % 2][:, 0:nj], ACT.Copy)\
                        .then_inc(pt_hi, 1)

            def hi_ot(it, i, bk):
                act.wait_ge(pv_done, QT * it + i + 1 + PV0)
                act.wait_ge(wo_done, QT * it + i - 1 + WO0)
                nc.scalar.activation(ot[:, i % 2, HI], bank[bk][:], ACT.Copy).then_inc(ot_hi, 1)

            def group(it, last):
                for step in range(STEPS):
                    if 0 <= step - LAG - 1 < CELLS:
                        hi_pt(it, step - LAG - 1)
                    if step < CELLS:
                        exp(it, step)
                    if step < GQ:
                        hi_wo(it, step, step % 2)
                    if 0 <= step - 1 < CELLS:
                        normalise(it, step - 1)
                    if not last and 13 <= step < 17:
                        hi_wq(it + 1, step - 13, (step - 13) % 2, 8 * it + 4 + step - 13 + 1)
                    for _n, kind, a, h in acts(step - 2, last):
                        if kind == "q":
                            hi_q(it, a if a else 2, h)
                    for n, kind, a, h in acts(step - 1, last):
                        if kind == "q":
                            swap_q(it, a if a else 2, h, n % 2)
                        elif kind == "pv":
                            hi_ot(it, a, n % 2)

            for h in range(GQ):
                hi_wq(0, h, h % 2, None)
            for h in range(GQ):
                swap_q(0, 0, h, h % 2)
                hi_q(0, 0, h)
            group(0, False)
            with act.Fori(1, LAST) as it:
                group(it, False)
            group(LAST, True)

        @block.vector
        def _(dve):
            dve.sem_inc(sc_done, SC0)
            dve.sem_inc(pt_lo, PTLO0)
            dve.sem_inc(bank_free, FREE0)
            dve.sem_inc(add_done, ADD0)
            dve.wait_ge(tab_in, 32)
            dve.wait_ge(masked, 4)

            def cos_q(it, blk, h, bk):
                n = 8 * it + q_number(blk, h)
                dve.wait_ge(sw_done, 2 * (n + 1))
                dve.wait_ge(q_lo, n + 1)
                nc.vector.tensor_tensor(qf[:], bank[bk][:], cosq[:, blk % 2 * TB:blk % 2 * TB + TB], ALU.mult)\
                    .then_inc(bank_free, 1)

            def add_q(it, blk, h, use):
                dve.wait_ge(sin_done, 8 * it + q_number(blk, h) + 1)
                dve.wait_ge(bank_free, use + 1 + FREE0)
                nc.vector.tensor_tensor(qf[:], qf[:], sw[:], ALU.add).then_inc(add_done, 1)

            def scores_there(it, c):
                dve.wait_ge(s_done, CELLS * it + c + 1)
                dve.wait_ge(t_done, PIECES * it + thru(c - S_RING) + TD0)

            def mask_max(it, c):
                i, slot = c // GQ, c % S_RING
                w = P * (i + 1)
                nc.vector.tensor_tensor_reduce(out=sc[:, slot, 0:w], in0=sps[c % 2][:, 0:w], in1=mask[:, S - w:S],
                                               scale=-SCALE, scalar=3.0e38, op0=ALU.add, op1=ALU.min,
                                               accum_out=nmax[:, slot:slot + 1]).then_inc(sc_done, 1)

            def reciprocal(it, c):
                slot = c % S_RING
                dve.wait_ge(exp_done, CELLS * it + c + 1)
                nc.vector.reciprocal(rinv[:, slot:slot + 1], rsum[:, slot:slot + 1]).then_inc(rinv_done, 1)

            def lo_pt(it, c):
                i, h = c // GQ, c % GQ
                for n, j0, nj in pieces(c):
                    u = unit_of(i, j0) % PT_UNITS
                    dve.wait_ge(pt_hi, PIECES * it + n + 1)
                    nc.vector.tensor_tensor(pt[:, u, LO, 0:nj, h * P:(h + 1) * P], tps[n % 2][:, 0:nj],
                                            pt[:, u, HI, 0:nj, h * P:(h + 1) * P], ALU.subtract).then_inc(pt_lo, 1)

            def lo_ot(it, i, bk):
                dve.wait_ge(ot_hi, QT * it + i + 1)
                nc.vector.tensor_tensor(ot[:, i % 2, LO], bank[bk][:], ot[:, i % 2, HI], ALU.subtract)\
                    .then_inc(bank_free, 1)

            def add_y(it, i, bk):
                dve.wait_ge(wo_done, QT * it + i + 1 + WO0)
                dve.wait_ge(y_in[i % 2], 16 * (4 * it + i // 2 + 1))
                nc.vector.tensor_tensor(ys[:, i % 2], bank[bk][:], ys[:, i % 2], ALU.add).then_inc(bank_free, 1)

            def group(it, last):
                base = USES * it + FIRST_USES
                for step in range(STEPS):
                    if step < CELLS:
                        scores_there(it, step)
                    if 0 <= step - LAG - 1 < CELLS:
                        lo_pt(it, step - LAG - 1)
                    elif step < CELLS:
                        nc.vector.memset(spare[:, step:step + 1], 0.0)
                    if step < CELLS:
                        mask_max(it, step)
                    if 0 <= step - 1 < CELLS:
                        reciprocal(it, step - 1)
                    for n, kind, a, h in acts(step - 2, last):
                        if kind == "q":
                            add_q(it, a if a else 2, h, base + n)
                    for n, kind, a, h in acts(step - 1, last):
                        if kind == "q":
                            cos_q(it, a if a else 2, h, n % 2)
                        elif kind == "pv":
                            lo_ot(it, a, n % 2)
                        else:
                            add_y(it, a, n % 2)

            for h in range(GQ):
                cos_q(0, 0, h, h % 2)
                add_q(0, 0, h, h)
            group(0, False)
            with dve.Fori(1, LAST) as it:
                group(it, False)
            group(LAST, True)

        @block.tensor
        def _(pe):
            pe.sem_inc(t_done, TD0)
            pe.sem_inc(pv_done, PV0)
            pe.sem_inc(wo_done, WO0)
            pe.wait_ge(masked, 4)

            def scores(it, c):
                i, h = c // GQ, c % GQ
                if c == 0:
                    pe.wait_ge(k_in, 64 * (it + 1))
                pe.wait_ge(q_lo, 8 * it + q_number(i // 4, h) + 1 + QLO0)
                pe.wait_ge(sc_done, CELLS * it + c + 1)
                q = (i % 4) * P
                for a, b in scores_width(i):
                    last = three_pass(nc, sps[c % 2][:, a:b], [(lambda p: qs[:, i // 4, h, p, q:q + P], lambda p: kt[:, p, a:b])])
                last.then_inc(s_done, 1)

            def transposes(it, c):
                pe.wait_ge(norm_done, CELLS * it + c + 1)
                for n, j0, nj in pieces(c):
                    pe.wait_ge(pt_lo, PIECES * it + n + 1)
                    for j in range(nj):
                        last = nc.tensor.transpose(tps[n % 2][:, j], sc[:, c % S_RING, (j0 + j) * P:(j0 + j + 1) * P], ident[:])
                    last.then_inc(t_done, 1)

            def take_bank(use):
                pe.wait_ge(bank_free, use + 1)

            def queries(it, blk, h, n, use, weights, blocks):
                pe.wait_ge(xs_in, 16 * blocks)
                pe.wait_ge(w_lo, weights + WL0)
                take_bank(use)
                three_pass(nc, bank[n % 2][:], [(lambda p, k=k: wq[:, h, p, k], lambda p, k=k: xs[:, p, k]) for k in range(DC)])\
                    .then_inc(q_mm, 1)

            def values(it, i, n, use):
                if i == 0:
                    pe.wait_ge(v_in, 16 * (it + 1))
                pe.wait_ge(pt_lo, PIECES * it + thru(GQ * i + GQ - 1) + PTLO0)
                take_bank(use)
                three_pass(nc, bank[n % 2][:],
                           [(lambda p, j=j: vt[:, j, p], lambda p, j=j: pt[:, unit_of(i, j) % PT_UNITS, p, j % 4])
                            for j in range(i + 1)]).then_inc(pv_done, 1)

            def project(it, i, n, use, pv_use):
                if i == 0:
                    pe.wait_ge(w_lo, WPG * (it + 1) + WL0)
                pe.wait_ge(bank_free, pv_use + 1 + FREE0)
                take_bank(use)
                three_pass(nc, bank[n % 2][:], [(lambda p, h=h: ot[:, i % 2, p, h * P:(h + 1) * P], lambda p, h=h: wo[:, h, p])
                                                for h in range(GQ)]).then_inc(wo_done, 1)

            def group(it, last):
                base = USES * it + FIRST_USES
                for step in range(STEPS):
                    if step < CELLS:
                        scores(it, step)
                    for n, kind, a, h in acts(step, last):
                        if kind == "q" and a == 1:
                            queries(it, 1, h, n, base + n, WPG * it + 4, 2 * it + 2)
                        elif kind == "q":
                            queries(it + 1, 0, h, n, base + n, WPG * (it + 1) + h + 1, 2 * it + 3)
                        elif kind == "pv":
                            values(it, a, n, base + n)
                        else:
                            project(it, a, n, base + n, base + use_of("pv", a, last))
                    if 0 <= step - LAG < CELLS:
                        transposes(it, step - LAG)

            for h in range(GQ):
                queries(0, 0, h, h, h, h + 1, 1)
            group(0, False)
            with pe.Fori(1, LAST) as it:
                group(it, False)
            group(LAST, True)


def rstd_steps(nc, dve, chain, var, sd, rs, tmp, sqrt_asked, sqrt_done, asked, done):
    def link(ins):
        chain[0] = chain[0] + 1
        ins.then_inc(chain[1], 1)
        dve.wait_ge(chain[1], chain[0])

    nc.vector.tensor_scalar(var, var, EPS, None, ALU.add).then_inc(sqrt_asked, 1)
    dve.wait_ge(sqrt_asked, asked)
    dve.wait_ge(sqrt_done, done)
    link(nc.vector.reciprocal(rs, sd))
    link(nc.vector.tensor_tensor(tmp, rs, rs, ALU.mult))
    link(nc.vector.tensor_tensor(tmp, tmp, var, ALU.mult))
    link(nc.vector.tensor_scalar(tmp, tmp, -0.5, 1.5, ALU.mult, ALU.add))
    link(nc.vector.tensor_tensor(rs, rs, tmp, ALU.mult))


def stage_c(nc, y_d, x1_d, x1s_d):
    NT = B * QT
    with ExitStack() as ctx:
        def sb(name, shape, dt):
            return ctx.enter_context(nc.sbuf_tensor(name, shape, dt))

        def sem(name):
            return ctx.enter_context(nc.semaphore(name))

        y = sb("c_y", [P, NT, D], F32)
        stats = sb("c_stats", [P, NT, 6], F32)
        mv = sb("c_mv", [P, NT, 2], F32)
        var, sd, rs, tmp = (sb(f"c_{n}", [P, NT], F32) for n in ("var", "sd", "rs", "tmp"))
        ident = sb("c_ident", [P, P], F32)
        xs = sb("c_xs", [P, 2, 2, DC, TB], F32R)
        tps = [ctx.enter_context(nc.psum_tensor(f"c_tps{i}", [P, DC, P], F32)) for i in range(4)]

        y_in = [sem(f"c_y_in{b}") for b in range(NBLK)]
        ids, st, ag = sem("c_ids"), sem("c_st"), sem("c_ag")
        link = sem("c_link")
        sqrt_asked, sqrt_done = sem("c_sqrt_asked"), sem("c_sqrt_done")
        norm, t_done, t_hi, t_lo = sem("c_norm"), sem("c_t_done"), sem("c_t_hi"), sem("c_t_lo")
        x1_out = sem("c_x1_out")
        xs_out = [sem("c_xs_out0"), sem("c_xs_out1")]

        block = ctx.enter_context(nc.Block())

        @block.sync
        def _(sp):
            for b in range(NBLK):
                sp.dma_start(y[:, 4 * b:4 * b + 4], y_d[b // 2, (b % 2) * 4:(b % 2) * 4 + 4].rearrange("i p d -> p i d"))\
                    .then_inc(y_in[b], 16)
            for b in range(NBLK):
                sp.wait_ge(norm, 4 * b + 4)
                sp.dma_start(x1_d[b].rearrange("i p d -> p i d"), y[:, 4 * b:4 * b + 4]).then_inc(x1_out, 16)
                sp.wait_ge(t_lo, 4 * b + 4)
                sp.dma_start(x1s_d[b], words(xs[:, b % 2])).then_inc(xs_out[b % 2], 16)
            sp.wait_ge(x1_out, 16 * NBLK)
            for p in range(2):
                sp.wait_ge(xs_out[p], 16 * NBLK // 2)

        @block.gpsimd
        def _(pool):
            nc.gpsimd.memset(ident[:], 0.0).then_inc(ids, 1)
            pool.wait_ge(ids, 1)
            nc.gpsimd.affine_select(out=ident[:], in_=ident[:], compare_op=ALU.not_equal, fill=1.0,
                                    base=0, pattern=[[-1, P]], channel_multiplier=1).then_inc(ids, 1)

        @block.vector
        def _(dve):
            for n in range(NT):
                dve.wait_ge(y_in[n // 4], 16)
                nc.vector.bn_stats(stats[:, n], y[:, n]).then_inc(st, 1)
            for n in range(NT):
                dve.wait_ge(st, n + 1)
                nc.vector.bn_aggr(mv[:, n], stats[:, n]).then_inc(ag, 1)
            dve.wait_ge(ag, NT)
            nc.vector.tensor_copy(var[:], mv[:, :, 1]).then_inc(ag, 1)
            dve.wait_ge(ag, NT + 1)
            rstd_steps(nc, dve, [0, link], var[:], sd[:], rs[:], tmp[:], sqrt_asked, sqrt_done, 1, 1)
            for n in range(NT + 1):
                if n < NT:
                    nc.vector.tensor_scalar(y[:, n], y[:, n], mv[:, n, 0:1], rs[:, n:n + 1], ALU.subtract, ALU.mult)\
                        .then_inc(norm, 1)
                if n >= 1:
                    m, t = n - 1, (n - 1) % 4 * P
                    dve.wait_ge(t_hi, m + 1)
                    b = m // 4 % 2
                    nc.vector.tensor_tensor(xs[:, b, LO, :, t:t + P], tps[m % 4][:], xs[:, b, HI, :, t:t + P], ALU.subtract)\
                        .then_inc(t_lo, 1)

        @block.scalar
        def _(act):
            act.wait_ge(sqrt_asked, 1)
            nc.scalar.activation(sd[:], var[:], ACT.Sqrt).then_inc(sqrt_done, 1)
            for n in range(NT):
                act.wait_ge(t_done, n + 1)
                if n % 4 == 0 and n >= 8:
                    act.wait_ge(xs_out[n // 4 % 2], 16)
                t = n % 4 * P
                nc.scalar.activation(xs[:, n // 4 % 2, HI, :, t:t + P], tps[n % 4][:], ACT.Copy).then_inc(t_hi, 1)

        @block.tensor
        def _(pe):
            pe.wait_ge(ids, 2)
            for n in range(NT):
                pe.wait_ge(norm, n + 1)
                if n >= 4:
                    pe.wait_ge(t_lo, n - 3)
                for k in range(DC):
                    last = nc.tensor.transpose(tps[n % 4][:, k], y[:, n, k * P:(k + 1) * P], ident[:])
                last.then_inc(t_done, 1)


def stage_d(nc, w1p, s1p, w3p, s3p, w2p, s2p, shifts, x1_d, x1s_d, out):
    with ExitStack() as ctx:
        def sb(name, shape, dt):
            return ctx.enter_context(nc.sbuf_tensor(name, shape, dt))

        def sem(name):
            return ctx.enter_context(nc.semaphore(name))

        w1 = sb("d_w1", [P, 2, DC, F], F32R)
        w3 = sb("d_w3", [P, 2, DC, F], F32R)
        w2 = sb("d_w2", [P, 2, FT, D], F32R)
        pk = sb("d_pk", [P, 2, 3, 512], I32)
        sl = sb("d_sl", [P, 2, 3, 512], F32)
        sh = sb("d_sh", [P, 5, 2], I32)
        xs = sb("d_xs", [P, 2, 2, DC, TB], F32R)
        x1 = sb("d_x1", [P, 4, D], F32)
        hb = sb("d_hb", [P, 2, TB], F32)
        hs = sb("d_hs", [P, 2, 2, TB], F32R)
        stats = sb("d_stats", [P, 4, 6], F32)
        mv = sb("d_mv", [P, 4, 2], F32)
        var, sd, rs, tmp = (sb(f"d_{n}", [P, 4], F32) for n in ("var", "sd", "rs", "tmp"))
        aps = [ctx.enter_context(nc.psum_tensor(f"d_a{i}", [P, TB], F32)) for i in range(2)]
        bps = [ctx.enter_context(nc.psum_tensor(f"d_b{i}", [P, TB], F32)) for i in range(2)]
        yps = [ctx.enter_context(nc.psum_tensor(f"d_y{i}", [P, D], F32)) for i in range(4)]

        sh_in = sem("d_sh_in")
        pk_in = [sem("d_pk_in0"), sem("d_pk_in1")]
        shifted, unpacked, w_hi, w_lo = sem("d_shifted"), sem("d_unpacked"), sem("d_w_hi"), sem("d_w_lo")
        xs_in, x1_in, o_out = sem("d_xs_in"), sem("d_x1_in"), sem("d_o_out")
        a_done, b_done, ab_free = sem("d_a_done"), sem("d_b_done"), sem("d_ab_free")
        exp_done, link = sem("d_exp_done"), sem("d_link")
        h_hi, h_lo, h_used = sem("d_h_hi"), sem("d_h_lo"), sem("d_h_used")
        z_done, st, rlink = sem("d_z_done"), sem("d_st"), sem("d_rlink")
        sqrt_asked, sqrt_done, o_ready = sem("d_sqrt_asked"), sem("d_sqrt_done"), sem("d_o_ready")

        AB0, HLO0, HU0, Z0, O0 = 2, 2, 2, 1, 1
        LOADS = 2 * 2 + 2 * 2 + 1 + 4

        def width(f):
            return min(P, F - f * P)

        block = ctx.enter_context(nc.Block())

        @block.sync
        def _(sp):
            sp.dma_start(sh[:], shifts).then_inc(sh_in, 16)
            for f in range(FT):
                if f == 1:
                    sp.dma_start(words(xs[:, 0]), x1s_d[0]).then_inc(xs_in, 16)
                if f >= 2:
                    sp.wait_ge(w_lo, 3 * (f - 1))
                n, b = width(f), f % 2
                cols = slice(f * P, f * P + n)
                for m, (w, s) in enumerate(((w1p, s1p), (w3p, s3p))):
                    pv = pk[:, b, m, 0:DC * n].rearrange("p (k c) -> p k c", k=DC)
                    sv = sl[:, b, m, 0:DC * n].rearrange("p (k c) -> p k c", k=DC)
                    for half in range(2):
                        rows = slice(64 * half, 64 * half + 64)
                        sp.dma_start(pv[rows], w[:, :, cols]).then_inc(pk_in[b], 16)
                        sp.dma_start(sv[rows], s[half:half + 1, :, cols].broadcast_to((64, DC, n))).then_inc(pk_in[b], 16)
                sp.dma_start(pk[0:n, b, 2], w2p[f * P:f * P + n]).then_inc(pk_in[b], 16)
                for q in range(n // 32):
                    sp.dma_start(sl[32 * q:32 * q + 32, b, 2], s2p[4 * f + q:4 * f + q + 1].broadcast_to((32, D)))\
                        .then_inc(pk_in[b], 16)

            def block_io(n, last):
                if not last:
                    sp.wait_ge(a_done, FT * n + 1)
                    sp.dma_start(words(xs[:, (n + 1) % 2]), x1s_d[n + 1]).then_inc(xs_in, 16)
                sp.wait_ge(o_out, 16 * n + O0)
                sp.dma_start(x1[:], x1_d[n].rearrange("i p d -> p i d")).then_inc(x1_in, 16)
                sp.wait_ge(o_ready, 4 * n + 4)
                sp.dma_start(out[n].rearrange("i p d -> p i d"), x1[:]).then_inc(o_out, 16)

            with sp.Fori(0, NBLK - 1) as n:
                block_io(n, False)
            block_io(NBLK - 1, True)
            sp.wait_ge(o_out, 16 * NBLK + O0)

        def split_views(m, f, p):
            n, b = width(f), f % 2
            if m < 2:
                w = (w1, w3)[m]
                return w[:, p, :, f * P:f * P + n], sl[:, b, m, 0:DC * n].rearrange("p (k c) -> p k c", k=DC)
            return w2[0:n, p, f].rearrange("p (m c) -> p c m", c=4), sl[0:n, b, 2].rearrange("p (c m) -> p c m", c=4)

        @block.gpsimd
        def _(pool):
            for f in range(FT):
                for m in range(3):
                    pool.wait_ge(w_hi, 3 * f + m + 1)
                    lo, src = split_views(m, f, LO)
                    nc.gpsimd.tensor_tensor(lo, src, split_views(m, f, HI)[0], ALU.subtract).then_inc(w_lo, 1)

        @block.scalar
        def _(act):
            act.sem_inc(o_out, O0)

            def weights_hi(f):
                for m in range(3):
                    act.wait_ge(unpacked, 3 * f + m + 1)
                    hi, src = split_views(m, f, HI)
                    nc.scalar.activation(hi, src, ACT.Copy).then_inc(w_hi, 1)

            def hidden(n, f, first):
                k, w = FT * n + f, width(f)
                act.wait_ge(a_done, k + 1)
                act.wait_ge(h_lo, k + 1)
                nc.scalar.activation(hb[0:w, f % 2], aps[f % 2][0:w], ACT.Exp, scale=-1.0).then_inc(exp_done, 1)
                if first and f + 2 < FT:
                    weights_hi(f + 2)
                act.wait_ge(ab_free, k + 1 + AB0)
                act.wait_ge(h_used, k + 1)
                nc.scalar.activation(hs[0:w, f % 2, HI], hb[0:w, f % 2], ACT.Copy).then_inc(h_hi, 1)

            def block_of(n, first):
                for f in range(FT):
                    hidden(n, f, first)
                act.wait_ge(sqrt_asked, n + 1)
                nc.scalar.activation(sd[:], var[:], ACT.Sqrt).then_inc(sqrt_done, 1)

            weights_hi(0)
            weights_hi(1)
            block_of(0, True)
            with act.Fori(1, NBLK) as n:
                block_of(n, False)

        @block.vector
        def _(dve):
            dve.sem_inc(ab_free, AB0)
            dve.sem_inc(h_lo, HLO0)
            dve.sem_inc(z_done, Z0)
            dve.wait_ge(sh_in, 16)

            def unpack(f):
                n, b = width(f), f % 2
                dve.wait_ge(pk_in[b], 16 * ((LOADS * (f // 2)) + LOADS - (4 - n // 32)))
                for m in range(2):
                    v = pk[:, b, m, 0:DC * n]
                    nc.vector.tensor_scalar(v, v, sh[:, 0, 0:1], sh[:, 0, 1:2], ALU.logical_shift_left,
                                            ALU.arith_shift_right).then_inc(shifted, 1)
                for c in range(4):
                    v = pk[0:n, b, 2, c * P:(c + 1) * P]
                    nc.vector.tensor_scalar(v, v, sh[0:n, 1 + c, 0:1], sh[0:n, 1 + c, 1:2], ALU.logical_shift_left,
                                            ALU.arith_shift_right).then_inc(shifted, 1)
                for m, (rows, cols) in enumerate(((P, DC * n), (P, DC * n), (n, D))):
                    dve.wait_ge(shifted, 6 * f + (1, 2, 6)[m])
                    v = sl[0:rows, b, m, 0:cols]
                    nc.vector.tensor_tensor(v, pk[0:rows, b, m, 0:cols], v, ALU.mult).then_inc(unpacked, 1)

            def hidden(n, f, first):
                k, w = FT * n + f, width(f)
                v = hb[0:w, f % 2]
                dve.wait_ge(exp_done, k + 1)
                nc.vector.tensor_scalar(v, v, 1.0, None, ALU.add).then_inc(link, 1)
                dve.wait_ge(link, 3 * k + 1)
                nc.vector.reciprocal(v, v).then_inc(link, 1)
                dve.wait_ge(link, 3 * k + 2)
                nc.vector.tensor_tensor(v, aps[f % 2][0:w], v, ALU.mult).then_inc(link, 1)
                dve.wait_ge(link, 3 * k + 3)
                dve.wait_ge(b_done, k + 1)
                nc.vector.tensor_tensor(v, bps[f % 2][0:w], v, ALU.mult).then_inc(ab_free, 1)
                if first and f + 2 < FT:
                    unpack(f + 2)
                dve.wait_ge(h_hi, k + 1)
                nc.vector.tensor_tensor(hs[0:w, f % 2, LO], v, hs[0:w, f % 2, HI], ALU.subtract).then_inc(h_lo, 1)

            def finish(n):
                dve.wait_ge(x1_in, 16 * n + 16)
                dve.wait_ge(h_used, FT * (n + 1) + HU0)
                for t in range(4):
                    nc.vector.tensor_tensor(x1[:, t], yps[t][:], x1[:, t], ALU.add).then_inc(z_done, 1)
                for t in range(4):
                    dve.wait_ge(z_done, 4 * n + t + 1 + Z0)
                    nc.vector.bn_stats(stats[:, t], x1[:, t]).then_inc(st, 1)
                dve.wait_ge(st, 9 * n + 4)
                nc.vector.memset(tmp[:], 0.0)
                for t in range(4):
                    nc.vector.bn_aggr(mv[:, t], stats[:, t]).then_inc(st, 1)
                dve.wait_ge(st, 9 * n + 8)
                nc.vector.tensor_copy(var[:], mv[:, :, 1]).then_inc(st, 1)
                dve.wait_ge(st, 9 * n + 9)
                rstd_steps(nc, dve, [5 * n, rlink], var[:], sd[:], rs[:], tmp[:], sqrt_asked, sqrt_done, n + 1, n + 1)
                for t in range(4):
                    nc.vector.tensor_scalar(x1[:, t], x1[:, t], mv[:, t, 0:1], rs[:, t:t + 1], ALU.subtract, ALU.mult)\
                        .then_inc(o_ready, 1)

            unpack(0)
            unpack(1)
            for f in range(FT):
                hidden(0, f, True)
            finish(0)
            with dve.Fori(1, NBLK) as n:
                for f in range(FT):
                    hidden(n, f, False)
                finish(n)

        @block.tensor
        def _(pe):
            pe.sem_inc(h_used, HU0)

            def up(n, f):
                w = width(f)
                cols = slice(f * P, f * P + w)
                pe.wait_ge(ab_free, FT * n + f + 1)
                for m, (ps, wt, done) in enumerate(((aps, w1, a_done), (bps, w3, b_done))):
                    pe.wait_ge(w_lo, 3 * f + m + 1)
                    three_pass(nc, ps[f % 2][0:w], [(lambda p, k=k: wt[:, p, k, cols], lambda p, k=k: xs[:, n % 2, p, k])
                                                    for k in range(DC)]).then_inc(done, 1)

            def down(n, f):
                w = width(f)
                pe.wait_ge(w_lo, 3 * f + 3)
                pe.wait_ge(h_lo, FT * n + f + 1 + HLO0)
                if f == 0:
                    pe.wait_ge(z_done, 4 * n + Z0)
                for t in range(4):
                    for k, (a, b) in enumerate(PASSES):
                        last = nc.tensor.matmul(yps[t][:], hs[0:w, f % 2, a, t * P:(t + 1) * P], w2[0:w, b, f],
                                                start=(f == 0 and k == 0), stop=(f == FT - 1 and k == 2))
                last.then_inc(h_used, 1)

            with pe.Fori(0, NBLK) as n:
                pe.wait_ge(xs_in, 16 * n + 16)
                for f in range(FT + 1):
                    if f < FT:
                        up(n, f)
                    if f >= 1:
                        down(n, f - 1)


def kernel(L0_attn_hidden_states, L0_attn_Wq, L0_attn_Wkr, L0_attn_Wdk, L0_attn_Wupk, L0_attn_Wupv, L0_attn_Wo,
           L0_ffn_w1, L0_ffn_s1, L0_ffn_w2, L0_ffn_s2, L0_ffn_w3, L0_ffn_s3):
    import concourse.bacc as bacc
    from concourse.bass_utils import run_bass_kernel_spmd

    x = np.asarray(L0_attn_hidden_states)

    def chunked(wT, n):
        return wT.reshape(DC, P, n).transpose(1, 0, 2)

    def quads(w):
        w = np.asarray(w).reshape(2, 4, 2, 32, D).transpose(0, 2, 1, 3, 4).reshape(512, D)
        return chunked(w.T, 512)

    def packed_up(w):
        return np.asarray(w).reshape(F, 4, 64).transpose(2, 1, 0)

    def scales_up(s):
        return np.asarray(s).reshape(F, 4, 2).transpose(2, 1, 0)

    d = np.arange(D).reshape(P, 4).T.reshape(-1)
    flat = F * d[None, :] + np.arange(F)[:, None]
    w2p = np.asarray(L0_ffn_w2)[flat // P, flat % 64]
    s2p = np.asarray(L0_ffn_s2)[(F * d[None, :] + 32 * np.arange(F // 32)[:, None]) // 64]

    inv_freq = 1.0 / 10000.0 ** (np.arange(0, HD, 2, dtype=np.float32) / HD)
    emb = np.outer(np.arange(S, dtype=np.float32), inv_freq)
    emb = np.concatenate([emb, emb], axis=-1)
    cosT = np.cos(emb).astype(np.float32).T
    sinT = np.sin(emb).astype(np.float32).T.copy()
    sinT[:HD // 2] *= -1
    shifts = np.zeros((P, 5, 2), np.int32)
    p = np.arange(P)
    for k in range(5):
        low = (p if k == 0 else (F % P * (k - 1) + p) % P) >= 64
        shifts[:, k, 0] = np.where(low, 28, 0)
        shifts[:, k, 1] = np.where(low, 28, 4)

    arrays = {
        "x": x,
        "xT": x.reshape(NBLK, TB, DC, P).transpose(0, 3, 2, 1),
        "wqT": np.asarray(L0_attn_Wq).reshape(HEADS, HD, DC, P).transpose(0, 3, 2, 1),
        "wkrT": quads(L0_attn_Wkr),
        "wdkT": chunked(np.asarray(L0_attn_Wdk).T, C),
        "wupkT": quads(L0_attn_Wupk),
        "wupvT": chunked(np.asarray(L0_attn_Wupv).T, KV * HD),
        "woT": np.asarray(L0_attn_Wo).T.reshape(HEADS, HD, D),
        "w1p": packed_up(L0_ffn_w1), "s1p": scales_up(L0_ffn_s1),
        "w3p": packed_up(L0_ffn_w3), "s3p": scales_up(L0_ffn_s3),
        "w2p": w2p, "s2p": s2p,
        "cosT": cosT, "sinT": sinT, "shifts": shifts,
    }
    nc = bacc.Bacc("TRN2", target_bir_lowering=False, num_devices=1)
    feeds, args = {}, []
    for name, a in arrays.items():
        a = np.ascontiguousarray(a)
        feeds[f"in_{name}"] = a
        args.append(nc.dram_tensor(f"in_{name}", a.shape, mybir.dt.from_np(a.dtype), kind="ExternalInput").ap())
    args.append(nc.dram_tensor("out", (NBLK, 4, P, D), F32, kind="ExternalOutput").ap())
    program(nc, *args)
    result = run_bass_kernel_spmd(nc, [feeds], core_ids=[0])
    return result.results[0]["out"].reshape(B, S, D)
```

```python
from contextlib import ExitStack

import numpy as np
import concourse.bass as bass
from concourse import mybir

F32 = mybir.dt.float32
F32R = mybir.dt.float32r
BF16 = mybir.dt.bfloat16
I32 = mybir.dt.int32
ALU = mybir.AluOpType
ACT = mybir.ActivationFunctionType

B, S, D = 2, 1024, 512
HEADS, KV, HD = 32, 8, 128
GQ = HEADS // KV
GROUPS = B * KV
C = 512
F = 1376
P = 128
DC = D // P
TB = 512
NBLK = B * S // TB
QT = S // P
FT = (F + P - 1) // P
HI, LO = 0, 1
PASSES = ((HI, HI), (HI, LO), (LO, HI))
SCALE = float(1.0 / np.sqrt(np.float32(HD)))
MASKED = -1.0e30
EPS = 1e-5

CELLS = QT * GQ
LAG = 3
S_RING = 4
PT_UNITS = 4
UNITS = 12


def pieces(c):
    i = c // GQ
    first = c if i < 4 else 16 + 2 * (c - 16)
    out = [(first, 0, min(4, i + 1))]
    if i >= 4:
        out.append((first + 1, 4, i - 3))
    return out


PIECES = 48


def unit_of(i, j0):
    return i if i < 4 else 4 + 2 * (i - 4) + j0 // 4


UNIT_TILE = [0, 1, 2, 3, 4, 4, 5, 5, 6, 6, 7, 7]

FILL = [('pv', 6, -1, 0), ('wo', 5, -1, 0), ('q1', 0, 0, 1), ('pv', 7, -1, 3), ('wo', 6, -1, 5), ('wo', 7, -1, 6), ('q1', 1, 0, 2), ('pv', 0, 0, 9), ('q1', 2, 0, 2), ('pv', 1, 0, 12), ('q1', 3, 0, 2), ('wo', 0, 0, 14), ('wo', 1, 0, 14), ('pv', 2, 0, 16), ('wo', 2, 0, 17), ('pv', 3, 0, 20), ('q0', 0, 1, 20), ('wo', 3, 0, 21), ('q0', 1, 1, 21), ('pv', 4, 0, 24), ('q0', 2, 1, 24), ('wo', 4, 0, 25), ('q0', 3, 1, 25), ('pv', 5, 0, 28)]
ROOM = [29] + 15 * [8] + 4 * [9] + 12 * [11]


def products(kind, a):
    return 3 * (a + 1) if kind == "pv" else 12


def done_of(done, kind, a):
    return next((s for n, s in done.items() if FILL[n][:2] == (kind, a)), None)


def spread():
    steps, n, at, done = [[] for _ in range(CELLS)], 0, 0, {}
    for s in range(CELLS):
        room = ROOM[s] if s < CELLS - 1 else 10 ** 6
        while n < len(FILL) and FILL[n][3] <= s and room:
            kind, a, _g, _s = FILL[n]
            if at == 0 and (done.get(n - 2, -1) == s or kind == "wo" and done_of(done, "pv", a) == s):
                break
            take = min(room, products(kind, a) - at)
            steps[s].append((n, at, at + take))
            room, at = room - take, at + take
            if at == products(kind, a):
                done[n] = s
                n, at = n + 1, 0
    assert n == len(FILL)
    return steps


SPREAD = spread()
DONE_AT = {n: s for s in range(CELLS) for n, _a, b in SPREAD[s] if b == products(*FILL[n][:2])}


def cut(parts, k, n):
    total = sum(b - a for _n, a, b in parts)
    lo, hi, at, out = total * k // n, total * (k + 1) // n, 0, []
    for place, a, b in parts:
        x, y = max(lo, at), min(hi, at + b - a)
        if x < y:
            out.append((place, a + x - at, a + y - at))
        at += b - a
    return out


def valid(n, turn):
    g = FILL[n][2]
    return {"first": g >= 0, "loop": True, "last": g <= 0, "end": g < 0}[turn]


def finished(step, turn, ago):
    s, before = step - ago, {"first": None, "loop": "loop", "last": "loop", "end": "last"}[turn]
    shift = 0
    if s < 0:
        if before is None:
            return []
        s, turn, shift = s + CELLS, before, -1
    if s >= CELLS:
        return []
    return [(n, FILL[n][0], FILL[n][1], FILL[n][2] + shift) for n in sorted(DONE_AT) if DONE_AT[n] == s and valid(n, turn)]


def bank_before(n, turn):
    shift, bank = 0, n % 2
    while True:
        n -= 1
        if n < 0:
            turn = {"first": None, "loop": "loop", "last": "loop", "end": "last"}[turn]
            if turn is None:
                return None
            n, shift = len(FILL) - 1, shift - 1
        if n % 2 == bank and valid(n, turn):
            return FILL[n][0], FILL[n][1], FILL[n][2] + shift


def program(nc, x, xT, wqT, wkrT, wdkT, wupkT, wupvT, woT, w1p, s1p, w3p, s3p, w2p, s2p, cosT, sinT, shifts, out):
    xs_d = nc.dram_tensor("xs_d", [NBLK, P, 2, DC, TB], F32).ap()
    k_d = nc.dram_tensor("k_d", [GROUPS // 4, 4, P, 2, S], F32).ap()
    v_d = nc.dram_tensor("v_d", [GROUPS, P, QT, 2, HD], F32).ap()
    y_d = nc.dram_tensor("y_d", [B, QT, P, D], F32).ap()
    x1_d = nc.dram_tensor("x1_d", [NBLK, 4, P, D], F32).ap()
    x1s_d = nc.dram_tensor("x1s_d", [NBLK, P, 2, DC, TB], F32).ap()

    stage_a(nc, x, xT, wkrT, wdkT, wupkT, wupvT, cosT, sinT, xs_d, k_d, v_d, y_d)
    stage_b(nc, wqT, woT, cosT, sinT, xs_d, k_d, v_d, y_d)
    stage_c(nc, y_d, x1_d, x1s_d)
    stage_d(nc, w1p, s1p, w3p, s3p, w2p, s2p, shifts, x1_d, x1s_d, out)


def words(ap):
    return ap.bitcast(F32)


def three_pass(nc, out, pairs, first=0, end=None):
    every = [(lhsT(a), rhs(b)) for lhsT, rhs in pairs for a, b in PASSES]
    for n in range(first, len(every) if end is None else end):
        ins = nc.tensor.matmul(out, *every[n], start=(n == 0), stop=(n == len(every) - 1))
    return ins


def stage_a(nc, x, xT, wkrT, wdkT, wupkT, wupvT, cosT, sinT, xs_d, k_d, v_d, y_d):
    with ExitStack() as ctx:
        def sb(name, shape, dt):
            return ctx.enter_context(nc.sbuf_tensor(name, shape, dt))

        def sem(name):
            return ctx.enter_context(nc.semaphore(name))

        raw = sb("a_raw", [P, 2, DC, 512], F32)
        wdk = sb("a_wdk", [P, 2, DC, 512], F32R)
        wkr = sb("a_wkr", [P, 2, DC, 512], F32R)
        wupk = sb("a_wupk", [P, 2, DC, 512], F32R)
        wupv = sb("a_wupv", [P, 2, 2, DC, 512], F32R)
        xraw = sb("a_xraw", [P, DC, TB], F32)
        xs = sb("a_xs", [P, 2, DC, TB], F32R)
        cs = sb("a_cs", [P, 2, DC, TB], F32R)
        cosk = sb("a_cos", [P, S], F32)
        sink = sb("a_sin", [P, S], F32)
        rt = sb("a_rt", [P, 4, TB], F32)
        kf = sb("a_kf", [P, 2, TB], F32)
        ks = sb("a_ks", [P, 4, 2, TB], F32R)
        vs = sb("a_vs", [P, 2, 4, 2, HD], F32R)
        RING = 5
        bank = [ctx.enter_context(nc.psum_tensor(f"a_ps{i}", [P, TB], F32)) for i in range(RING)]

        w_in = [sem("a_w_in0"), sem("a_w_in1")]
        tab_in, x_in = sem("a_tab_in"), sem("a_x_in")
        w_hi, w_lo = sem("a_w_hi"), sem("a_w_lo")
        x_hi, x_lo = sem("a_x_hi"), sem("a_x_lo")
        mm = sem("a_mm")
        bank_free = sem("a_bank_free")
        part_hi = sem("a_part_hi")
        rope_t, rope_done = sem("a_rope_t"), sem("a_rope_done")
        kr_lo = sem("a_kr_lo")
        k_out, xs_out, y_out = sem("a_k_out"), sem("a_xs_out"), sem("a_y_out")
        v_out = [sem("a_v_out0"), sem("a_v_out1")]

        MM0, FREE0, KRLO0, XLO0, OUT0 = 20, RING, 2, 1, 1
        WEIGHTS = [(wdkT, None, wdk), (wkrT, None, wkr), (wupkT, None, wupk), (wupvT, 0, wupv), (wupvT, 1, wupv)]
        NW = len(WEIGHTS)
        CG, RG, NG, VG, GROUPS_A = 0, 4, 8, 12, 20

        def weight_part(n):
            _s, half, w = WEIGHTS[n]
            return (lambda p: w[:, p]) if half is None else (lambda p: w[:, half, p])

        block = ctx.enter_context(nc.Block())

        @block.sync
        def _(sp):
            for n, (src, half, _w) in enumerate(WEIGHTS):
                if n >= 2:
                    sp.wait_ge(w_lo, n - 1)
                s = src if half is None else src[:, :, half * 512:half * 512 + 512]
                sp.dma_start(raw[:, n % 2], s).then_inc(w_in[n % 2], 16)
                if n == 1:
                    for g in range(4):
                        sp.dma_start(cosk[32 * g:32 * g + 32, :], cosT[0:32, :]).then_inc(tab_in, 16)
                        sp.dma_start(sink[32 * g:32 * g + 32, :], sinT[64:96, :]).then_inc(tab_in, 16)
            sp.dma_start(y_d.rearrange("b i p d -> (b i p) d"), x.rearrange("b s d -> (b s) d")).then_inc(y_out, 16)
            with sp.Fori(0, NBLK) as t:
                sp.wait_ge(x_lo, t + 1 + XLO0)
                sp.dma_start(xs_d[t], words(xs[:])).then_inc(xs_out, 16)
                for n in range(8):
                    quad, part = n // 2 % 2, 2 * (n % 2) + n // 4
                    if n < 4:
                        sp.wait_ge(kr_lo, 4 * t + n + 1 + KRLO0)
                    else:
                        sp.wait_ge(bank_free, GROUPS_A * t + NG + (n - 4) + 1 + FREE0)
                    sp.dma_start(k_d[(t // 2) * 2 + quad, part, :, :, bass.ds((t % 2) * TB, TB)],
                                 words(ks[:, n % 4])).then_inc(k_out, 16)
                for n in range(8):
                    sp.wait_ge(bank_free, GROUPS_A * t + VG + n + 1 + FREE0)
                    sp.dma_start(
                        v_d[bass.ds((t // 2) * KV + 4 * (n % 2), 4), :, (t % 2) * 4 + n // 2]
                        .rearrange("g p l d -> p g (l d)"),
                        words(vs[:, n % 2]).rearrange("p g l d -> p g (l d)")).then_inc(v_out[n % 2], 16)
            sp.wait_ge(xs_out, 16 * NBLK + OUT0)
            sp.wait_ge(k_out, 16 * 8 * NBLK + OUT0)
            for p in range(2):
                sp.wait_ge(v_out[p], 16 * 4 * NBLK + OUT0)
            sp.wait_ge(y_out, 16)

        @block.gpsimd
        def _(pool):
            pool.sem_inc(x_lo, XLO0)
            pool.sem_inc(kr_lo, KRLO0)
            pool.dma_start(xraw[:], xT[0]).then_inc(x_in, 16)
            for n in range(NW):
                pool.wait_ge(w_hi, n + 1)
                w = weight_part(n)
                nc.gpsimd.tensor_tensor(w(LO), raw[:, n % 2], w(HI), ALU.subtract).then_inc(w_lo, 1)

            def rope_lo(t):
                for n in range(4):
                    pool.wait_ge(part_hi, GROUPS_A * t + RG + n + 1)
                    nc.gpsimd.tensor_tensor(ks[:, n, LO], kf[:, n % 2], ks[:, n, HI], ALU.subtract).then_inc(kr_lo, 1)

            with pool.Fori(0, NBLK - 1) as t:
                rope_lo(t)
                pool.wait_ge(x_lo, t + 1 + XLO0)
                pool.dma_start(xraw[:], xT[t + 1]).then_inc(x_in, 16)
            rope_lo(NBLK - 1)

        @block.scalar
        def _(act):
            act.sem_inc(xs_out, OUT0)
            act.sem_inc(k_out, OUT0)
            act.sem_inc(v_out[0], OUT0)
            act.sem_inc(v_out[1], OUT0)
            for n in range(NW):
                act.wait_ge(w_in[n % 2], 16 * (n // 2 + 1))
                w = weight_part(n)
                nc.scalar.activation(w(HI), raw[:, n % 2], ACT.Copy).then_inc(w_hi, 1)
            with act.Fori(0, NBLK) as t:
                act.wait_ge(x_in, 16 * t + 16)
                act.wait_ge(mm, GROUPS_A * t + NG)
                act.wait_ge(xs_out, 16 * t + OUT0)
                nc.scalar.activation(xs[:, HI], xraw[:], ACT.Copy).then_inc(x_hi, 1)
                for m in range(DC):
                    act.wait_ge(mm, GROUPS_A * t + CG + m + 1 + MM0)
                    nc.scalar.activation(cs[:, HI, m], bank[(CG + m) % RING][:], ACT.Copy).then_inc(part_hi, 1)
                act.wait_ge(k_out, 16 * 8 * t + OUT0)
                for n in range(4):
                    act.wait_ge(rope_done, 4 * t + n + 1)
                    nc.scalar.activation(ks[:, n, HI], kf[:, n % 2], ACT.Copy).then_inc(part_hi, 1)
                act.wait_ge(k_out, 16 * (8 * t + 4) + OUT0)
                for n in range(4):
                    act.wait_ge(mm, GROUPS_A * t + NG + n + 1 + MM0)
                    nc.scalar.activation(ks[:, n, HI], bank[(NG + n) % RING][:], ACT.Copy).then_inc(part_hi, 1)
                for n in range(8):
                    act.wait_ge(mm, GROUPS_A * t + VG + n + 1 + MM0)
                    act.wait_ge(v_out[n % 2], 16 * (4 * t + n // 2) + OUT0)
                    nc.scalar.activation(vs[:, n % 2, :, HI, :], bank[(VG + n) % RING][:].rearrange("p (g d) -> p g d", g=4),
                                         ACT.Copy).then_inc(part_hi, 1)

        @block.vector
        def _(dve):
            dve.sem_inc(bank_free, FREE0)
            with dve.Fori(0, NBLK) as t:
                dve.wait_ge(x_hi, t + 1)
                nc.vector.tensor_tensor(xs[:, LO], xraw[:], xs[:, HI], ALU.subtract).then_inc(x_lo, 1)
                for m in range(DC):
                    dve.wait_ge(part_hi, GROUPS_A * t + CG + m + 1)
                    nc.vector.tensor_tensor(cs[:, LO, m], bank[(CG + m) % RING][:], cs[:, HI, m],
                                            ALU.subtract).then_inc(bank_free, 1)
                dve.wait_ge(tab_in, 16 * 8)
                cos_t, sin_t = (w[:, bass.ds((t % 2) * TB, TB)] for w in (cosk, sink))
                for quad in range(2):
                    if quad == 1:
                        dve.wait_ge(rope_done, 4 * t + 2)
                    for k in range(2):
                        g = RG + 2 * quad + k
                        dve.wait_ge(mm, GROUPS_A * t + g + 1 + MM0)
                        nc.vector.tensor_tensor(rt[:, 2 * k], bank[g % RING][:], cos_t, ALU.mult).then_inc(rope_t, 1)
                        nc.vector.tensor_tensor(rt[:, 2 * k + 1], bank[g % RING][:], sin_t, ALU.mult).then_inc(bank_free, 1)
                    dve.wait_ge(rope_t, 4 * t + 2 * quad + 2)
                    dve.wait_ge(bank_free, GROUPS_A * t + RG + 2 * quad + 2 + FREE0)
                    for k, (a, b, op) in enumerate(((0, 3, ALU.subtract), (2, 1, ALU.add))):
                        dve.wait_ge(kr_lo, 4 * t + 2 * quad + k + 1)
                        nc.vector.tensor_tensor(kf[:, k], rt[:, a], rt[:, b], op).then_inc(rope_done, 1)
                for n in range(4):
                    dve.wait_ge(part_hi, GROUPS_A * t + NG + n + 1)
                    nc.vector.tensor_tensor(ks[:, n, LO], bank[(NG + n) % RING][:], ks[:, n, HI],
                                            ALU.subtract).then_inc(bank_free, 1)
                for n in range(8):
                    dve.wait_ge(part_hi, GROUPS_A * t + VG + n + 1)
                    nc.vector.tensor_tensor(vs[:, n % 2, :, LO, :], bank[(VG + n) % RING][:].rearrange("p (g d) -> p g d", g=4),
                                            vs[:, n % 2, :, HI, :], ALU.subtract).then_inc(bank_free, 1)

        @block.tensor
        def _(pe):
            pe.sem_inc(mm, MM0)

            def group(t, g, pairs):
                pe.wait_ge(bank_free, GROUPS_A * t + g + 1)
                three_pass(nc, bank[g % RING][:], pairs).then_inc(mm, 1)

            def project(w, m, src):
                return [(lambda p, k=k: w(p)[:, k, m * P:(m + 1) * P], lambda p, k=k: src[:, p, k]) for k in range(DC)]

            with pe.Fori(0, NBLK) as t:
                pe.wait_ge(x_lo, t + 1 + XLO0)
                pe.wait_ge(w_lo, 1)
                for m in range(4):
                    group(t, CG + m, project(weight_part(0), m, xs))
                pe.wait_ge(w_lo, 2)
                for m in range(4):
                    group(t, RG + m, project(weight_part(1), m, xs))
                pe.wait_ge(w_lo, 3)
                pe.wait_ge(bank_free, GROUPS_A * t + CG + 4 + FREE0)
                for m in range(4):
                    group(t, NG + m, project(weight_part(2), m, cs))
                pe.wait_ge(w_lo, NW)
                for n in range(8):
                    w, tt = weight_part(3 + n % 2), n // 2
                    group(t, VG + n, [(lambda p, k=k: cs[:, p, k, tt * P:(tt + 1) * P], lambda p, k=k: w(p)[:, k])
                                      for k in range(DC)])


def stage_b(nc, wqT, woT, cosT, sinT, xs_d, k_d, v_d, y_d):
    with ExitStack() as ctx:
        def sb(name, shape, dt):
            return ctx.enter_context(nc.sbuf_tensor(name, shape, dt))

        def sem(name):
            return ctx.enter_context(nc.semaphore(name))

        xs = sb("b_xs", [P, 2, DC, TB], F32R)
        kt = sb("b_kt", [P, 2, S], F32R)
        vt = sb("b_vt", [P, QT, 2, HD], F32R)
        wraw = sb("b_wraw", [P, 2, 512], F32)
        wq = sb("b_wq", [P, GQ, 2, DC, HD], F32R)
        wo = sb("b_wo", [P, GQ, 2, D], F32R)
        qs = sb("b_qs", [P, 2, GQ, 2, TB], F32R)
        sw = sb("b_sw", [P, TB], F32)
        qf = sb("b_qf", [P, TB], F32)
        cosq = sb("b_cos", [P, S], F32)
        sinq = sb("b_sin", [P, S], F32)
        mask = sb("b_mask", [P, S], BF16)
        ident = sb("b_ident", [P, P], F32)
        sc = sb("b_sc", [P, S_RING, S], F32)
        spare = sb("b_spare", [P, 2], F32)
        nmax = sb("b_nmax", [P, S_RING], F32)
        rsum = sb("b_rsum", [P, S_RING], F32)
        rinv = sb("b_rinv", [P, S_RING], F32)
        pt = sb("b_pt", [P, PT_UNITS, 2, 4, GQ * P], F32R)
        ot = sb("b_ot", [P, 2, 2, GQ * P], F32R)
        ys = sb("b_ys", [P, 2, D], F32)
        sps = [ctx.enter_context(nc.psum_tensor(f"b_sps{i}", [P, S], F32)) for i in range(2)]
        tps = [ctx.enter_context(nc.psum_tensor(f"b_tps{i}", [P, 4, P], F32)) for i in range(2)]
        bank = [ctx.enter_context(nc.psum_tensor(f"b_ps{i}", [P, 512], F32)) for i in range(2)]

        tab_in, masked = sem("b_tab_in"), sem("b_masked")
        k_in, v_in, xs_in = sem("b_k_in"), sem("b_v_in"), sem("b_xs_in")
        w_in = [sem("b_w_in0"), sem("b_w_in1")]
        w_hi, w_lo = sem("b_w_hi"), sem("b_w_lo")
        y_in, y_out = [sem("b_y_in0"), sem("b_y_in1")], [sem("b_y_out0"), sem("b_y_out1")]
        s_done = sem("b_s_done")
        sc_done = sem("b_sc_done")
        exp_done, rinv_done, norm_done = sem("b_exp_done"), sem("b_rinv_done"), sem("b_norm_done")
        t_done = sem("b_t_done")
        pt_hi, pt_lo = sem("b_pt_hi"), sem("b_pt_lo")
        q_mm, q_cos = sem("b_q_mm"), sem("b_q_cos")
        sw_done, sin_done, add_done = sem("b_sw_done"), sem("b_sin_done"), sem("b_add_done")
        q_hi, q_lo = sem("b_q_hi"), sem("b_q_lo")
        pv_done, ot_hi, ot_lo = sem("b_pv_done"), sem("b_ot_hi"), sem("b_ot_lo")
        wo_done, y_added = sem("b_wo_done"), sem("b_y_added")

        SC0, TD0, PTLO0, PV0, WO0, ADD0, QLO0, YO0, WL0 = 2, 8, 2, 4, 8, 1, 1, 1, 2
        LAST = GROUPS - 1
        WPG = 8

        def thru(c):
            return pieces(c)[-1][0] + 1 if c >= 0 else pieces(c + CELLS)[-1][0] + 1 - PIECES

        def cell_at(step, it, turn):
            if step >= 0:
                return (it, step) if turn != "end" and step < CELLS else None
            return (it - 1, step + CELLS) if turn != "first" else None

        def scores_width(i):
            w = P * (i + 1)
            return [(0, max(w, 256))] if w <= 512 else [(0, w // 2), (w // 2, w)]

        def both_banks(ps, i):
            w = P * (i + 1)
            return ps[:, 0:w] if w <= 512 else ps[:, :].rearrange("p (b n) -> p b n", b=2)[:, :, 0:w // 2]

        def like_banks(ap, i):
            return ap if i < 4 else ap.rearrange("p (b n) -> p b n", b=2)

        def steps_of(turn):
            return range(CELLS) if turn != "end" else range(max(DONE_AT[n] for n in DONE_AT if FILL[n][2] < 0) + 3)

        def turns(engine, turn_of):
            turn_of(0, "first")
            with engine.Fori(1, LAST) as it:
                turn_of(it, "loop")
            turn_of(LAST, "last")
            turn_of(GROUPS, "end")

        WO_SPLIT = [DONE_AT[FILL.index(("wo", 7, -1, 6))] + 1 + h for h in range(GQ)]
        WQ_SPLIT = [max(DONE_AT[n] for n, f in enumerate(FILL) if f[:2] == ("q1", 3)) + 1 + h for h in range(GQ)]
        WO_LOADS = [s - 4 for s in WO_SPLIT]
        WQ_LOADS = [max(WO_SPLIT[2 + h % 2] + 1, s - 4) if h < 2 else WQ_SPLIT[h - 2] + 1 for h, s in enumerate(WQ_SPLIT)]

        block = ctx.enter_context(nc.Block())

        @block.sync
        def _(sp):
            def load_wq(it, h):
                sp.wait_ge(w_lo, WPG * it + h + 1)
                sp.dma_start(wraw[:, h % 2].rearrange("p (k m) -> p k m", k=DC), wqT[(it % KV) * GQ + h])\
                    .then_inc(w_in[h % 2], 16)

            def load_wo(it, h):
                sp.wait_ge(w_lo, WPG * it + 4 + h + 1)
                sp.dma_start(wraw[:, h % 2], woT[(it % KV) * GQ + h]).then_inc(w_in[h % 2], 16)

            def load_k(it):
                for part in range(4):
                    sp.dma_start(words(kt[32 * part:32 * part + 32]), k_d[it // 4, part, bass.ds((it % 4) * 32, 32)])\
                        .then_inc(k_in, 16)

            def load_v(it):
                sp.dma_start(words(vt[:]), v_d[it]).then_inc(v_in, 16)

            def load_xs(it, blk):
                sp.dma_start(words(xs[:]), xs_d[(it // KV) * 2 + blk]).then_inc(xs_in, 16)

            def load_y(it, i):
                sp.wait_ge(y_out[i % 2], 16 * (4 * it + i // 2) + YO0)
                sp.dma_start(ys[:, i % 2], y_d[it // KV, i]).then_inc(y_in[i % 2], 16)

            def store_y(it, i):
                sp.wait_ge(y_added, QT * it + i + 1)
                sp.dma_start(y_d[it // KV, i], ys[:, i % 2]).then_inc(y_out[i % 2], 16)

            def turn_of(it, turn):
                for step in steps_of(turn):
                    if step == 0 and turn in ("loop", "last"):
                        sp.wait_ge(s_done, CELLS * it)
                        load_k(it)
                    for _n, kind, a, g in finished(step, turn, 1):
                        if kind == "q0" and a == 3:
                            sp.wait_ge(q_mm, 8 * (it + g) + 4)
                            load_xs(it + g, 1)
                        if kind == "q1" and a == 3 and turn != "last":
                            sp.wait_ge(q_mm, 8 * (it + g) + 8)
                            load_xs(it + g + 1, 0)
                        if kind == "pv" and a == 7 and turn != "end":
                            sp.wait_ge(pv_done, QT * (it + g + 1) + PV0)
                            load_v(it + g + 1)
                    for _n, kind, a, g in finished(step, turn, 2):
                        if kind == "wo":
                            store_y(it + g, a)
                            if a + 2 < QT:
                                load_y(it + g, a + 2)
                            elif turn != "end":
                                load_y(it + g + 1, a + 2 - QT)
                    if turn != "end" and step in WO_LOADS:
                        load_wo(it, WO_LOADS.index(step))
                    if turn in ("first", "loop") and step in WQ_LOADS:
                        load_wq(it + 1, WQ_LOADS.index(step))

            load_wq(0, 0)
            load_wq(0, 1)
            load_xs(0, 0)
            sp.dma_start(sinq[:], sinT).then_inc(tab_in, 16)
            sp.dma_start(cosq[:], cosT).then_inc(tab_in, 16)
            load_wq(0, 2)
            load_wq(0, 3)
            load_k(0)
            load_v(0)
            sp.wait_ge(q_mm, 4)
            load_xs(0, 1)
            load_y(0, 0)
            load_y(0, 1)
            turns(sp, turn_of)
            for p in range(2):
                sp.wait_ge(y_out[p], 16 * 4 * GROUPS + YO0)

        @block.gpsimd
        def _(pool):
            pool.sem_inc(w_lo, WL0)
            pool.sem_inc(q_lo, QLO0)
            nc.gpsimd.memset(mask[:], 0.0).then_inc(masked, 1)
            nc.gpsimd.memset(ident[:], 0.0).then_inc(masked, 1)
            pool.wait_ge(masked, 2)
            nc.gpsimd.affine_select(out=mask[:, S - P:S], in_=mask[:, S - P:S], compare_op=ALU.is_ge, fill=MASKED,
                                    base=0, pattern=[[-1, P]], channel_multiplier=1).then_inc(masked, 1)
            nc.gpsimd.affine_select(out=ident[:], in_=ident[:], compare_op=ALU.not_equal, fill=1.0,
                                    base=0, pattern=[[-1, P]], channel_multiplier=1).then_inc(masked, 1)

            def times_sin(it, blk, h):
                pool.wait_ge(sw_done, 2 * (8 * it + 4 * blk + h + 1))
                nc.gpsimd.tensor_tensor(sw[:], sw[:], sinq[:, blk * TB:blk * TB + TB], ALU.mult).then_inc(sin_done, 1)

            def split_q(it, blk, h):
                pool.wait_ge(q_hi, 8 * it + 4 * blk + h + 1)
                nc.gpsimd.tensor_tensor(qs[:, blk, h, LO], qf[:], qs[:, blk, h, HI], ALU.subtract).then_inc(q_lo, 1)

            def split_wq(it, h):
                pool.wait_ge(w_hi, WPG * it + h + 1)
                nc.gpsimd.tensor_tensor(wq[:, h, LO].rearrange("p k m -> p (k m)"), wraw[:, h % 2],
                                        wq[:, h, HI].rearrange("p k m -> p (k m)"), ALU.subtract).then_inc(w_lo, 1)

            def split_wo(it, h):
                pool.wait_ge(w_hi, WPG * it + 4 + h + 1)
                nc.gpsimd.tensor_tensor(wo[:, h, LO], wraw[:, h % 2], wo[:, h, HI], ALU.subtract).then_inc(w_lo, 1)

            def turn_of(it, turn):
                for step in steps_of(turn):
                    for _n, kind, h, g in finished(step, turn, 2):
                        if kind in ("q0", "q1"):
                            split_q(it + g, int(kind == "q1"), h)
                    for _n, kind, h, g in finished(step, turn, 1):
                        if kind in ("q0", "q1"):
                            times_sin(it + g, int(kind == "q1"), h)
                    if turn != "end" and step in WO_SPLIT:
                        split_wo(it, WO_SPLIT.index(step))
                    if turn in ("first", "loop") and step in WQ_SPLIT:
                        split_wq(it + 1, WQ_SPLIT.index(step))

            for h in range(GQ):
                split_wq(0, h)
            pool.wait_ge(tab_in, 32)
            for h in range(GQ):
                times_sin(0, 0, h)
                split_q(0, 0, h)
            turns(pool, turn_of)

        @block.scalar
        def _(act):
            act.sem_inc(y_out[0], YO0)
            act.sem_inc(y_out[1], YO0)

            def swap_q(it, blk, h, bk):
                n = 8 * it + 4 * blk + h
                act.wait_ge(q_mm, n + 1)
                act.wait_ge(add_done, n + 1)
                nc.scalar.activation(sw[0:64], bank[bk][64:128], ACT.Copy).then_inc(sw_done, 1)
                nc.scalar.activation(sw[64:128], bank[bk][0:64], ACT.Copy).then_inc(sw_done, 1)

            def hi_q(it, blk, h):
                act.wait_ge(add_done, 8 * it + 4 * blk + h + 1 + ADD0)
                nc.scalar.activation(qs[:, blk, h, HI], qf[:], ACT.Copy).then_inc(q_hi, 1)

            def hi_wq(it, h):
                act.wait_ge(w_in[h % 2], 16 * (4 * it + h // 2 + 1))
                if not (isinstance(it, int) and it == 0):
                    act.wait_ge(q_mm, 8 * it - 4 + h + 1)
                nc.scalar.activation(wq[:, h, HI].rearrange("p k m -> p (k m)"), wraw[:, h % 2], ACT.Copy).then_inc(w_hi, 1)

            def hi_wo(it, h):
                act.wait_ge(w_in[h % 2], 16 * (4 * it + 2 + h // 2 + 1))
                act.wait_ge(wo_done, QT * it + WO0)
                nc.scalar.activation(wo[:, h, HI], wraw[:, h % 2], ACT.Copy).then_inc(w_hi, 1)

            def exp(it, c):
                slot, w = c % S_RING, P * (c // GQ + 1)
                act.wait_ge(sc_done, CELLS * it + c + 1 + SC0)
                nc.scalar.activation(sc[:, slot, 0:w], sc[:, slot, 0:w], ACT.Exp, bias=nmax[:, slot:slot + 1], scale=-1.0,
                                     accum_out=rsum[:, slot:slot + 1]).then_inc(exp_done, 1)

            def normalise(it, c):
                slot, w = c % S_RING, P * (c // GQ + 1)
                act.wait_ge(rinv_done, CELLS * it + c + 1)
                nc.scalar.activation(sc[:, slot, 0:w], sc[:, slot, 0:w], ACT.Copy, scale=rinv[:, slot:slot + 1])\
                    .then_inc(norm_done, 1)

            def hi_pt(it, c):
                i, h = c // GQ, c % GQ
                for n, j0, nj in pieces(c):
                    u = unit_of(i, j0)
                    act.wait_ge(t_done, PIECES * it + n + 1 + TD0)
                    if h == 0:
                        tile = UNIT_TILE[(u - PT_UNITS) % UNITS] - (QT if u < PT_UNITS else 0)
                        act.wait_ge(pv_done, QT * it + tile + 1 + PV0)
                    nc.scalar.activation(pt[:, u % PT_UNITS, HI, 0:nj, h * P:(h + 1) * P], tps[n % 2][:, 0:nj], ACT.Copy)\
                        .then_inc(pt_hi, 1)

            def hi_ot(it, i, bk):
                act.wait_ge(pv_done, QT * it + i + 1 + PV0)
                act.wait_ge(wo_done, QT * it + i - 1 + WO0)
                nc.scalar.activation(ot[:, i % 2, HI], bank[bk][:], ACT.Copy).then_inc(ot_hi, 1)

            def turn_of(it, turn):
                for step in steps_of(turn):
                    for n, kind, a, g in finished(step, turn, 1):
                        if kind in ("q0", "q1"):
                            swap_q(it + g, int(kind == "q1"), a, n % 2)
                        elif kind == "pv":
                            hi_ot(it + g, a, n % 2)
                    if cell := cell_at(step - 2, it, turn):
                        normalise(*cell)
                    if cell := cell_at(step, it, turn):
                        exp(*cell)
                    for _n, kind, a, g in finished(step, turn, 2):
                        if kind in ("q0", "q1"):
                            hi_q(it + g, int(kind == "q1"), a)
                    if turn != "end" and step in WO_SPLIT:
                        hi_wo(it, WO_SPLIT.index(step))
                    if turn in ("first", "loop") and step in WQ_SPLIT:
                        hi_wq(it + 1, WQ_SPLIT.index(step))
                    if cell := cell_at(step - LAG, it, turn):
                        hi_pt(*cell)

            for h in range(GQ):
                hi_wq(0, h)
            for h in range(GQ):
                swap_q(0, 0, h, h % 2)
                hi_q(0, 0, h)
            turns(act, turn_of)

        @block.vector
        def _(dve):
            dve.sem_inc(sc_done, SC0)
            dve.sem_inc(pt_lo, PTLO0)
            dve.sem_inc(add_done, ADD0)
            dve.wait_ge(tab_in, 32)
            dve.wait_ge(masked, 4)

            def cos_q(it, blk, h, bk):
                n = 8 * it + 4 * blk + h
                dve.wait_ge(sw_done, 2 * (n + 1))
                dve.wait_ge(q_lo, n + 1)
                nc.vector.tensor_tensor(qf[:], bank[bk][:], cosq[:, blk * TB:blk * TB + TB], ALU.mult).then_inc(q_cos, 1)

            def add_q(it, blk, h):
                n = 8 * it + 4 * blk + h
                dve.wait_ge(sin_done, n + 1)
                dve.wait_ge(q_cos, n + 1)
                nc.vector.tensor_tensor(qf[:], qf[:], sw[:], ALU.add).then_inc(add_done, 1)

            def scores_there(it, c):
                dve.wait_ge(s_done, CELLS * it + c + 1)
                dve.wait_ge(t_done, PIECES * it + thru(c - S_RING) + TD0)

            def mask_max(it, c):
                i, slot = c // GQ, c % S_RING
                w = P * (i + 1)
                nc.vector.tensor_tensor_reduce(out=like_banks(sc[:, slot, 0:w], i), in0=both_banks(sps[c % 2], i),
                                               in1=like_banks(mask[:, S - w:S], i),
                                               scale=-SCALE, scalar=3.0e38, op0=ALU.add, op1=ALU.min,
                                               accum_out=nmax[:, slot:slot + 1]).then_inc(sc_done, 1)

            def reciprocal(it, c):
                slot = c % S_RING
                dve.wait_ge(exp_done, CELLS * it + c + 1)
                nc.vector.reciprocal(rinv[:, slot:slot + 1], rsum[:, slot:slot + 1]).then_inc(rinv_done, 1)

            def lo_pt(it, c):
                i, h = c // GQ, c % GQ
                for n, j0, nj in pieces(c):
                    u = unit_of(i, j0) % PT_UNITS
                    dve.wait_ge(pt_hi, PIECES * it + n + 1)
                    nc.vector.tensor_tensor(pt[:, u, LO, 0:nj, h * P:(h + 1) * P], tps[n % 2][:, 0:nj],
                                            pt[:, u, HI, 0:nj, h * P:(h + 1) * P], ALU.subtract).then_inc(pt_lo, 1)

            def lo_ot(it, i, bk):
                dve.wait_ge(ot_hi, QT * it + i + 1)
                nc.vector.tensor_tensor(ot[:, i % 2, LO], bank[bk][:], ot[:, i % 2, HI], ALU.subtract).then_inc(ot_lo, 1)

            def add_y(it, i, bk):
                dve.wait_ge(wo_done, QT * it + i + 1 + WO0)
                dve.wait_ge(y_in[i % 2], 16 * (4 * it + i // 2 + 1))
                nc.vector.tensor_tensor(ys[:, i % 2], bank[bk][:], ys[:, i % 2], ALU.add).then_inc(y_added, 1)

            def turn_of(it, turn):
                for step in steps_of(turn):
                    for n, kind, a, g in finished(step, turn, 1):
                        if kind in ("q0", "q1"):
                            cos_q(it + g, int(kind == "q1"), a, n % 2)
                        elif kind == "pv":
                            lo_ot(it + g, a, n % 2)
                        else:
                            add_y(it + g, a, n % 2)
                    if here := cell_at(step, it, turn):
                        scores_there(*here)
                    if cell := cell_at(step - 2, it, turn):
                        reciprocal(*cell)
                    elif here:
                        nc.vector.memset(spare[:, step:step + 1], 0.0)
                    if here:
                        mask_max(*here)
                    for _n, kind, a, g in finished(step, turn, 2):
                        if kind in ("q0", "q1"):
                            add_q(it + g, int(kind == "q1"), a)
                    if cell := cell_at(step - LAG, it, turn):
                        lo_pt(*cell)

            for h in range(GQ):
                cos_q(0, 0, h, h % 2)
                add_q(0, 0, h)
            turns(dve, turn_of)

        @block.tensor
        def _(pe):
            pe.sem_inc(t_done, TD0)
            pe.sem_inc(pv_done, PV0)
            pe.sem_inc(wo_done, WO0)
            pe.wait_ge(masked, 4)

            def scores(it, c):
                i, h = c // GQ, c % GQ
                if c == 0:
                    pe.wait_ge(k_in, 64 * (it + 1))
                pe.wait_ge(q_lo, 8 * it + 4 * (i // 4) + h + 1 + QLO0)
                pe.wait_ge(sc_done, CELLS * it + c + 1)
                q = (i % 4) * P
                for k, (a, b) in enumerate(scores_width(i)):
                    last = three_pass(nc, sps[c % 2][:, 512 * k:512 * k + b - a], [(lambda p: qs[:, i // 4, h, p, q:q + P], lambda p: kt[:, p, a:b])])
                last.then_inc(s_done, 1)

            def transposes(it, c, piece):
                n, j0, nj = piece
                pe.wait_ge(norm_done, CELLS * it + c + 1)
                pe.wait_ge(pt_lo, PIECES * it + n + 1)
                for j in range(nj):
                    last = nc.tensor.transpose(tps[n % 2][:, j], sc[:, c % S_RING, (j0 + j) * P:(j0 + j + 1) * P], ident[:])
                last.then_inc(t_done, 1)

            def bank_taken(kind, a, it):
                if kind == "pv":
                    pe.wait_ge(ot_lo, QT * it + a + 1)
                elif kind == "wo":
                    pe.wait_ge(y_added, QT * it + a + 1)
                else:
                    pe.wait_ge(q_cos, 8 * it + 4 * int(kind == "q1") + a + 1)

            def queries(it, blk, h, bk, a, b):
                if a == 0:
                    pe.wait_ge(xs_in, 16 * (2 * it + blk + 1))
                    pe.wait_ge(w_lo, WPG * it + h + 1 + WL0)
                ins = three_pass(nc, bank[bk][:], [(lambda p, k=k: wq[:, h, p, k], lambda p, k=k: xs[:, p, k])
                                                   for k in range(DC)], a, b)
                if b == products("q0", h):
                    ins.then_inc(q_mm, 1)

            def values(it, i, bk, a, b):
                if a == 0:
                    if i == 0:
                        pe.wait_ge(v_in, 16 * (it + 1))
                    pe.wait_ge(pt_lo, PIECES * it + thru(GQ * i + GQ - 1) + PTLO0)
                ins = three_pass(nc, bank[bk][:],
                                 [(lambda p, j=j: vt[:, j, p], lambda p, j=j: pt[:, unit_of(i, j) % PT_UNITS, p, j % 4])
                                  for j in range(i + 1)], a, b)
                if b == products("pv", i):
                    ins.then_inc(pv_done, 1)

            def project(it, i, bk, a, b):
                if a == 0:
                    pe.wait_ge(w_lo, WPG * (it + 1) + WL0)
                    pe.wait_ge(ot_lo, QT * it + i + 1)
                ins = three_pass(nc, bank[bk][:], [(lambda p, h=h: ot[:, i % 2, p, h * P:(h + 1) * P], lambda p, h=h: wo[:, h, p])
                                                   for h in range(GQ)], a, b)
                if b == products("wo", i):
                    ins.then_inc(wo_done, 1)

            def fill(it, turn, parts):
                for n, a, b in parts:
                    if not valid(n, turn):
                        continue
                    kind, t, g, _s = FILL[n]
                    if a == 0 and (before := bank_before(n, turn)):
                        bank_taken(before[0], before[1], it + before[2])
                    if kind == "pv":
                        values(it + g, t, n % 2, a, b)
                    elif kind == "wo":
                        project(it + g, t, n % 2, a, b)
                    else:
                        queries(it + g, int(kind == "q1"), t, n % 2, a, b)

            def turn_of(it, turn):
                if turn == "first":
                    pe.wait_ge(q_cos, GQ)
                for step in range(CELLS):
                    parts = SPREAD[step]
                    here, cell = cell_at(step, it, turn), cell_at(step - LAG, it, turn)
                    if step == 0:
                        fill(it, turn, parts)
                        parts = []
                    if here:
                        scores(*here)
                    ts = pieces(cell[1]) if cell else []
                    thirds = [cut(parts, k, len(ts) + 1) for k in range(len(ts) + 1)]
                    fill(it, turn, thirds[0])
                    for k, piece in enumerate(ts):
                        transposes(*cell, piece)
                        fill(it, turn, thirds[k + 1])

            for h in range(GQ):
                if h >= 2:
                    pe.wait_ge(q_cos, h - 1)
                queries(0, 0, h, h % 2, 0, products("q0", h))
            turns(pe, turn_of)


def rstd_steps(nc, dve, chain, var, sd, rs, tmp, sqrt_asked, sqrt_done, asked, done):
    def link(ins):
        chain[0] = chain[0] + 1
        ins.then_inc(chain[1], 1)
        dve.wait_ge(chain[1], chain[0])

    nc.vector.tensor_scalar(var, var, EPS, None, ALU.add).then_inc(sqrt_asked, 1)
    dve.wait_ge(sqrt_asked, asked)
    dve.wait_ge(sqrt_done, done)
    link(nc.vector.reciprocal(rs, sd))
    link(nc.vector.tensor_tensor(tmp, rs, rs, ALU.mult))
    link(nc.vector.tensor_tensor(tmp, tmp, var, ALU.mult))
    link(nc.vector.tensor_scalar(tmp, tmp, -0.5, 1.5, ALU.mult, ALU.add))
    link(nc.vector.tensor_tensor(rs, rs, tmp, ALU.mult))


def stage_c(nc, y_d, x1_d, x1s_d):
    NT = B * QT
    with ExitStack() as ctx:
        def sb(name, shape, dt):
            return ctx.enter_context(nc.sbuf_tensor(name, shape, dt))

        def sem(name):
            return ctx.enter_context(nc.semaphore(name))

        y = sb("c_y", [P, NT, D], F32)
        stats = sb("c_stats", [P, NT, 6], F32)
        mv = sb("c_mv", [P, NT, 2], F32)
        var, sd, rs, tmp = (sb(f"c_{n}", [P, NT], F32) for n in ("var", "sd", "rs", "tmp"))
        ident = sb("c_ident", [P, P], F32)
        xs = sb("c_xs", [P, 2, 2, DC, TB], F32R)
        tps = [ctx.enter_context(nc.psum_tensor(f"c_tps{i}", [P, DC, P], F32)) for i in range(4)]

        y_in = [sem(f"c_y_in{b}") for b in range(NBLK)]
        ids, st, ag = sem("c_ids"), sem("c_st"), sem("c_ag")
        link = sem("c_link")
        sqrt_asked, sqrt_done = sem("c_sqrt_asked"), sem("c_sqrt_done")
        norm, t_done, t_hi, t_lo = sem("c_norm"), sem("c_t_done"), sem("c_t_hi"), sem("c_t_lo")
        x1_out = sem("c_x1_out")
        xs_out = [sem("c_xs_out0"), sem("c_xs_out1")]

        block = ctx.enter_context(nc.Block())

        @block.sync
        def _(sp):
            for b in range(NBLK):
                sp.dma_start(y[:, 4 * b:4 * b + 4], y_d[b // 2, (b % 2) * 4:(b % 2) * 4 + 4].rearrange("i p d -> p i d"))\
                    .then_inc(y_in[b], 16)
            for b in range(NBLK):
                sp.wait_ge(norm, 4 * b + 4)
                sp.dma_start(x1_d[b].rearrange("i p d -> p i d"), y[:, 4 * b:4 * b + 4]).then_inc(x1_out, 16)
                sp.wait_ge(t_lo, 4 * b + 4)
                sp.dma_start(x1s_d[b], words(xs[:, b % 2])).then_inc(xs_out[b % 2], 16)
            sp.wait_ge(x1_out, 16 * NBLK)
            for p in range(2):
                sp.wait_ge(xs_out[p], 16 * NBLK // 2)

        @block.gpsimd
        def _(pool):
            nc.gpsimd.memset(ident[:], 0.0).then_inc(ids, 1)
            pool.wait_ge(ids, 1)
            nc.gpsimd.affine_select(out=ident[:], in_=ident[:], compare_op=ALU.not_equal, fill=1.0,
                                    base=0, pattern=[[-1, P]], channel_multiplier=1).then_inc(ids, 1)

        @block.vector
        def _(dve):
            for n in range(NT):
                dve.wait_ge(y_in[n // 4], 16)
                nc.vector.bn_stats(stats[:, n], y[:, n]).then_inc(st, 1)
            for n in range(NT):
                dve.wait_ge(st, n + 1)
                nc.vector.bn_aggr(mv[:, n], stats[:, n]).then_inc(ag, 1)
            dve.wait_ge(ag, NT)
            nc.vector.tensor_copy(var[:], mv[:, :, 1]).then_inc(ag, 1)
            dve.wait_ge(ag, NT + 1)
            rstd_steps(nc, dve, [0, link], var[:], sd[:], rs[:], tmp[:], sqrt_asked, sqrt_done, 1, 1)
            for n in range(NT + 1):
                if n < NT:
                    nc.vector.tensor_scalar(y[:, n], y[:, n], mv[:, n, 0:1], rs[:, n:n + 1], ALU.subtract, ALU.mult)\
                        .then_inc(norm, 1)
                if n >= 1:
                    m, t = n - 1, (n - 1) % 4 * P
                    dve.wait_ge(t_hi, m + 1)
                    b = m // 4 % 2
                    nc.vector.tensor_tensor(xs[:, b, LO, :, t:t + P], tps[m % 4][:], xs[:, b, HI, :, t:t + P], ALU.subtract)\
                        .then_inc(t_lo, 1)

        @block.scalar
        def _(act):
            act.wait_ge(sqrt_asked, 1)
            nc.scalar.activation(sd[:], var[:], ACT.Sqrt).then_inc(sqrt_done, 1)
            for n in range(NT):
                act.wait_ge(t_done, n + 1)
                if n % 4 == 0 and n >= 8:
                    act.wait_ge(xs_out[n // 4 % 2], 16)
                t = n % 4 * P
                nc.scalar.activation(xs[:, n // 4 % 2, HI, :, t:t + P], tps[n % 4][:], ACT.Copy).then_inc(t_hi, 1)

        @block.tensor
        def _(pe):
            pe.wait_ge(ids, 2)
            for n in range(NT):
                pe.wait_ge(norm, n + 1)
                if n >= 4:
                    pe.wait_ge(t_lo, n - 3)
                for k in range(DC):
                    last = nc.tensor.transpose(tps[n % 4][:, k], y[:, n, k * P:(k + 1) * P], ident[:])
                last.then_inc(t_done, 1)


def stage_d(nc, w1p, s1p, w3p, s3p, w2p, s2p, shifts, x1_d, x1s_d, out):
    with ExitStack() as ctx:
        def sb(name, shape, dt):
            return ctx.enter_context(nc.sbuf_tensor(name, shape, dt))

        def sem(name):
            return ctx.enter_context(nc.semaphore(name))

        w1 = sb("d_w1", [P, 2, DC, F], F32R)
        w3 = sb("d_w3", [P, 2, DC, F], F32R)
        w2 = sb("d_w2", [P, 2, FT, D], F32R)
        pk = sb("d_pk", [P, 2, 3, 512], I32)
        sl = sb("d_sl", [P, 2, 3, 512], F32)
        sh = sb("d_sh", [P, 5, 2], I32)
        xs = sb("d_xs", [P, 2, 2, DC, TB], F32R)
        x1 = sb("d_x1", [P, 4, D], F32)
        hb = sb("d_hb", [P, 2, TB], F32)
        hs = sb("d_hs", [P, 2, 2, TB], F32R)
        stats = sb("d_stats", [P, 4, 6], F32)
        mv = sb("d_mv", [P, 4, 2], F32)
        var, sd, rs, tmp = (sb(f"d_{n}", [P, 4], F32) for n in ("var", "sd", "rs", "tmp"))
        aps = [ctx.enter_context(nc.psum_tensor(f"d_a{i}", [P, TB], F32)) for i in range(2)]
        bps = [ctx.enter_context(nc.psum_tensor(f"d_b{i}", [P, TB], F32)) for i in range(2)]
        yps = [ctx.enter_context(nc.psum_tensor(f"d_y{i}", [P, D], F32)) for i in range(4)]

        sh_in = sem("d_sh_in")
        pk_in = [sem("d_pk_in0"), sem("d_pk_in1")]
        shifted, unpacked, w_hi, w_lo = sem("d_shifted"), sem("d_unpacked"), sem("d_w_hi"), sem("d_w_lo")
        xs_in, x1_in, o_out = sem("d_xs_in"), sem("d_x1_in"), sem("d_o_out")
        a_done, b_done, ab_free = sem("d_a_done"), sem("d_b_done"), sem("d_ab_free")
        exp_done, link = sem("d_exp_done"), sem("d_link")
        h_hi, h_lo, h_used = sem("d_h_hi"), sem("d_h_lo"), sem("d_h_used")
        z_done, st, rlink = sem("d_z_done"), sem("d_st"), sem("d_rlink")
        sqrt_asked, sqrt_done, o_ready = sem("d_sqrt_asked"), sem("d_sqrt_done"), sem("d_o_ready")

        AB0, HLO0, HU0, Z0, O0 = 2, 2, 2, 1, 1
        LOADS = 2 * 2 + 2 * 2 + 1 + 4

        def width(f):
            return min(P, F - f * P)

        block = ctx.enter_context(nc.Block())

        @block.sync
        def _(sp):
            sp.dma_start(sh[:], shifts).then_inc(sh_in, 16)
            for f in range(FT):
                if f == 1:
                    sp.dma_start(words(xs[:, 0]), x1s_d[0]).then_inc(xs_in, 16)
                if f >= 2:
                    sp.wait_ge(w_lo, 3 * (f - 1))
                n, b = width(f), f % 2
                cols = slice(f * P, f * P + n)
                for m, (w, s) in enumerate(((w1p, s1p), (w3p, s3p))):
                    pv = pk[:, b, m, 0:DC * n].rearrange("p (k c) -> p k c", k=DC)
                    sv = sl[:, b, m, 0:DC * n].rearrange("p (k c) -> p k c", k=DC)
                    for half in range(2):
                        rows = slice(64 * half, 64 * half + 64)
                        sp.dma_start(pv[rows], w[:, :, cols]).then_inc(pk_in[b], 16)
                        sp.dma_start(sv[rows], s[half:half + 1, :, cols].broadcast_to((64, DC, n))).then_inc(pk_in[b], 16)
                sp.dma_start(pk[0:n, b, 2], w2p[f * P:f * P + n]).then_inc(pk_in[b], 16)
                for q in range(n // 32):
                    sp.dma_start(sl[32 * q:32 * q + 32, b, 2], s2p[4 * f + q:4 * f + q + 1].broadcast_to((32, D)))\
                        .then_inc(pk_in[b], 16)

            def block_io(n, last):
                if not last:
                    sp.wait_ge(a_done, FT * n + 1)
                    sp.dma_start(words(xs[:, (n + 1) % 2]), x1s_d[n + 1]).then_inc(xs_in, 16)
                sp.wait_ge(o_out, 16 * n + O0)
                sp.dma_start(x1[:], x1_d[n].rearrange("i p d -> p i d")).then_inc(x1_in, 16)
                sp.wait_ge(o_ready, 4 * n + 4)
                sp.dma_start(out[n].rearrange("i p d -> p i d"), x1[:]).then_inc(o_out, 16)

            with sp.Fori(0, NBLK - 1) as n:
                block_io(n, False)
            block_io(NBLK - 1, True)
            sp.wait_ge(o_out, 16 * NBLK + O0)

        def split_views(m, f, p):
            n, b = width(f), f % 2
            if m < 2:
                w = (w1, w3)[m]
                return w[:, p, :, f * P:f * P + n], sl[:, b, m, 0:DC * n].rearrange("p (k c) -> p k c", k=DC)
            return w2[0:n, p, f].rearrange("p (m c) -> p c m", c=4), sl[0:n, b, 2].rearrange("p (c m) -> p c m", c=4)

        @block.gpsimd
        def _(pool):
            for f in range(FT):
                for m in range(3):
                    pool.wait_ge(w_hi, 3 * f + m + 1)
                    lo, src = split_views(m, f, LO)
                    nc.gpsimd.tensor_tensor(lo, src, split_views(m, f, HI)[0], ALU.subtract).then_inc(w_lo, 1)

        @block.scalar
        def _(act):
            act.sem_inc(o_out, O0)

            def weights_hi(f):
                for m in range(3):
                    act.wait_ge(unpacked, 3 * f + m + 1)
                    hi, src = split_views(m, f, HI)
                    nc.scalar.activation(hi, src, ACT.Copy).then_inc(w_hi, 1)

            def hidden(n, f, first):
                k, w = FT * n + f, width(f)
                act.wait_ge(a_done, k + 1)
                act.wait_ge(h_lo, k + 1)
                nc.scalar.activation(hb[0:w, f % 2], aps[f % 2][0:w], ACT.Exp, scale=-1.0).then_inc(exp_done, 1)
                if first and f + 2 < FT:
                    weights_hi(f + 2)
                act.wait_ge(ab_free, k + 1 + AB0)
                act.wait_ge(h_used, k + 1)
                nc.scalar.activation(hs[0:w, f % 2, HI], hb[0:w, f % 2], ACT.Copy).then_inc(h_hi, 1)

            def block_of(n, first):
                for f in range(FT):
                    hidden(n, f, first)
                act.wait_ge(sqrt_asked, n + 1)
                nc.scalar.activation(sd[:], var[:], ACT.Sqrt).then_inc(sqrt_done, 1)

            weights_hi(0)
            weights_hi(1)
            block_of(0, True)
            with act.Fori(1, NBLK) as n:
                block_of(n, False)

        @block.vector
        def _(dve):
            dve.sem_inc(ab_free, AB0)
            dve.sem_inc(h_lo, HLO0)
            dve.sem_inc(z_done, Z0)
            dve.wait_ge(sh_in, 16)

            def unpack(f):
                n, b = width(f), f % 2
                dve.wait_ge(pk_in[b], 16 * ((LOADS * (f // 2)) + LOADS - (4 - n // 32)))
                for m in range(2):
                    v = pk[:, b, m, 0:DC * n]
                    nc.vector.tensor_scalar(v, v, sh[:, 0, 0:1], sh[:, 0, 1:2], ALU.logical_shift_left,
                                            ALU.arith_shift_right).then_inc(shifted, 1)
                for c in range(4):
                    v = pk[0:n, b, 2, c * P:(c + 1) * P]
                    nc.vector.tensor_scalar(v, v, sh[0:n, 1 + c, 0:1], sh[0:n, 1 + c, 1:2], ALU.logical_shift_left,
                                            ALU.arith_shift_right).then_inc(shifted, 1)
                for m, (rows, cols) in enumerate(((P, DC * n), (P, DC * n), (n, D))):
                    dve.wait_ge(shifted, 6 * f + (1, 2, 6)[m])
                    v = sl[0:rows, b, m, 0:cols]
                    nc.vector.tensor_tensor(v, pk[0:rows, b, m, 0:cols], v, ALU.mult).then_inc(unpacked, 1)

            def hidden(n, f, first):
                k, w = FT * n + f, width(f)
                v = hb[0:w, f % 2]
                dve.wait_ge(exp_done, k + 1)
                nc.vector.tensor_scalar(v, v, 1.0, None, ALU.add).then_inc(link, 1)
                dve.wait_ge(link, 3 * k + 1)
                nc.vector.reciprocal(v, v).then_inc(link, 1)
                dve.wait_ge(link, 3 * k + 2)
                nc.vector.tensor_tensor(v, aps[f % 2][0:w], v, ALU.mult).then_inc(link, 1)
                dve.wait_ge(link, 3 * k + 3)
                dve.wait_ge(b_done, k + 1)
                nc.vector.tensor_tensor(v, bps[f % 2][0:w], v, ALU.mult).then_inc(ab_free, 1)
                if first and f + 2 < FT:
                    unpack(f + 2)
                dve.wait_ge(h_hi, k + 1)
                nc.vector.tensor_tensor(hs[0:w, f % 2, LO], v, hs[0:w, f % 2, HI], ALU.subtract).then_inc(h_lo, 1)

            def finish(n):
                dve.wait_ge(x1_in, 16 * n + 16)
                dve.wait_ge(h_used, FT * (n + 1) + HU0)
                for t in range(4):
                    nc.vector.tensor_tensor(x1[:, t], yps[t][:], x1[:, t], ALU.add).then_inc(z_done, 1)
                for t in range(4):
                    dve.wait_ge(z_done, 4 * n + t + 1 + Z0)
                    nc.vector.bn_stats(stats[:, t], x1[:, t]).then_inc(st, 1)
                dve.wait_ge(st, 9 * n + 4)
                nc.vector.memset(tmp[:], 0.0)
                for t in range(4):
                    nc.vector.bn_aggr(mv[:, t], stats[:, t]).then_inc(st, 1)
                dve.wait_ge(st, 9 * n + 8)
                nc.vector.tensor_copy(var[:], mv[:, :, 1]).then_inc(st, 1)
                dve.wait_ge(st, 9 * n + 9)
                rstd_steps(nc, dve, [5 * n, rlink], var[:], sd[:], rs[:], tmp[:], sqrt_asked, sqrt_done, n + 1, n + 1)
                for t in range(4):
                    nc.vector.tensor_scalar(x1[:, t], x1[:, t], mv[:, t, 0:1], rs[:, t:t + 1], ALU.subtract, ALU.mult)\
                        .then_inc(o_ready, 1)

            unpack(0)
            unpack(1)
            for f in range(FT):
                hidden(0, f, True)
            finish(0)
            with dve.Fori(1, NBLK) as n:
                for f in range(FT):
                    hidden(n, f, False)
                finish(n)

        @block.tensor
        def _(pe):
            pe.sem_inc(h_used, HU0)

            def up(n, f):
                w = width(f)
                cols = slice(f * P, f * P + w)
                pe.wait_ge(ab_free, FT * n + f + 1)
                for m, (ps, wt, done) in enumerate(((aps, w1, a_done), (bps, w3, b_done))):
                    pe.wait_ge(w_lo, 3 * f + m + 1)
                    three_pass(nc, ps[f % 2][0:w], [(lambda p, k=k: wt[:, p, k, cols], lambda p, k=k: xs[:, n % 2, p, k])
                                                    for k in range(DC)]).then_inc(done, 1)

            def down(n, f):
                w = width(f)
                pe.wait_ge(w_lo, 3 * f + 3)
                pe.wait_ge(h_lo, FT * n + f + 1 + HLO0)
                if f == 0:
                    pe.wait_ge(z_done, 4 * n + Z0)
                for t in range(4):
                    for k, (a, b) in enumerate(PASSES):
                        last = nc.tensor.matmul(yps[t][:], hs[0:w, f % 2, a, t * P:(t + 1) * P], w2[0:w, b, f],
                                                start=(f == 0 and k == 0), stop=(f == FT - 1 and k == 2))
                last.then_inc(h_used, 1)

            with pe.Fori(0, NBLK) as n:
                pe.wait_ge(xs_in, 16 * n + 16)
                for f in range(FT + 1):
                    if f < FT:
                        up(n, f)
                    if f >= 1:
                        down(n, f - 1)


def kernel(L0_attn_hidden_states, L0_attn_Wq, L0_attn_Wkr, L0_attn_Wdk, L0_attn_Wupk, L0_attn_Wupv, L0_attn_Wo,
           L0_ffn_w1, L0_ffn_s1, L0_ffn_w2, L0_ffn_s2, L0_ffn_w3, L0_ffn_s3):
    import concourse.bacc as bacc
    from concourse.bass_utils import run_bass_kernel_spmd

    x = np.asarray(L0_attn_hidden_states)

    def chunked(wT, n):
        return wT.reshape(DC, P, n).transpose(1, 0, 2)

    def quads(w):
        w = np.asarray(w).reshape(2, 4, 2, 32, D).transpose(0, 2, 1, 3, 4).reshape(512, D)
        return chunked(w.T, 512)

    def packed_up(w):
        return np.asarray(w).reshape(F, 4, 64).transpose(2, 1, 0)

    def scales_up(s):
        return np.asarray(s).reshape(F, 4, 2).transpose(2, 1, 0)

    d = np.arange(D).reshape(P, 4).T.reshape(-1)
    flat = F * d[None, :] + np.arange(F)[:, None]
    w2p = np.asarray(L0_ffn_w2)[flat // P, flat % 64]
    s2p = np.asarray(L0_ffn_s2)[(F * d[None, :] + 32 * np.arange(F // 32)[:, None]) // 64]

    inv_freq = 1.0 / 10000.0 ** (np.arange(0, HD, 2, dtype=np.float32) / HD)
    emb = np.outer(np.arange(S, dtype=np.float32), inv_freq)
    emb = np.concatenate([emb, emb], axis=-1)
    cosT = np.cos(emb).astype(np.float32).T
    sinT = np.sin(emb).astype(np.float32).T.copy()
    sinT[:HD // 2] *= -1
    shifts = np.zeros((P, 5, 2), np.int32)
    p = np.arange(P)
    for k in range(5):
        low = (p if k == 0 else (F % P * (k - 1) + p) % P) >= 64
        shifts[:, k, 0] = np.where(low, 28, 0)
        shifts[:, k, 1] = np.where(low, 28, 4)

    arrays = {
        "x": x,
        "xT": x.reshape(NBLK, TB, DC, P).transpose(0, 3, 2, 1),
        "wqT": np.asarray(L0_attn_Wq).reshape(HEADS, HD, DC, P).transpose(0, 3, 2, 1),
        "wkrT": quads(L0_attn_Wkr),
        "wdkT": chunked(np.asarray(L0_attn_Wdk).T, C),
        "wupkT": quads(L0_attn_Wupk),
        "wupvT": chunked(np.asarray(L0_attn_Wupv).T, KV * HD),
        "woT": np.asarray(L0_attn_Wo).T.reshape(HEADS, HD, D),
        "w1p": packed_up(L0_ffn_w1), "s1p": scales_up(L0_ffn_s1),
        "w3p": packed_up(L0_ffn_w3), "s3p": scales_up(L0_ffn_s3),
        "w2p": w2p, "s2p": s2p,
        "cosT": cosT, "sinT": sinT, "shifts": shifts,
    }
    nc = bacc.Bacc("TRN2", target_bir_lowering=False, num_devices=1)
    feeds, args = {}, []
    for name, a in arrays.items():
        a = np.ascontiguousarray(a)
        feeds[f"in_{name}"] = a
        args.append(nc.dram_tensor(f"in_{name}", a.shape, mybir.dt.from_np(a.dtype), kind="ExternalInput").ap())
    args.append(nc.dram_tensor("out", (NBLK, 4, P, D), F32, kind="ExternalOutput").ap())
    program(nc, *args)
    result = run_bass_kernel_spmd(nc, [feeds], core_ids=[0])
    return result.results[0]["out"].reshape(B, S, D)
```

```python
from contextlib import ExitStack

import numpy as np
import concourse.bass as bass
from concourse import mybir

F32 = mybir.dt.float32
F32R = mybir.dt.float32r
BF16 = mybir.dt.bfloat16
I32 = mybir.dt.int32
ALU = mybir.AluOpType
ACT = mybir.ActivationFunctionType

B, S, D = 2, 1024, 512
HEADS, KV, HD = 32, 8, 128
GQ = HEADS // KV
GROUPS = B * KV
C = 512
F = 1376
P = 128
DC = D // P
TB = 512
NBLK = B * S // TB
QT = S // P
FT = (F + P - 1) // P
HI, LO = 0, 1
PASSES = ((HI, HI), (HI, LO), (LO, HI))
SCALE = float(1.0 / np.sqrt(np.float32(HD)))
MASKED = -1.0e30
EPS = 1e-5

CELLS = QT * GQ
LAG = 3
S_RING = 4
PT_UNITS = 4
UNITS = 12


def pieces(c):
    i = c // GQ
    first = c if i < 4 else 16 + 2 * (c - 16)
    out = [(first, 0, min(4, i + 1))]
    if i >= 4:
        out.append((first + 1, 4, i - 3))
    return out


PIECES = 48


def unit_of(i, j0):
    return i if i < 4 else 4 + 2 * (i - 4) + j0 // 4


UNIT_TILE = [0, 1, 2, 3, 4, 4, 5, 5, 6, 6, 7, 7]

FILL = [('pv', 6, -1, 0), ('wo', 5, -1, 1), ('q1', 0, 0, 2), ('pv', 7, -1, 3), ('wo', 6, -1, 5),
        ('wo', 7, -1, 9), ('q1', 1, 0, 0), ('pv', 0, 0, 9), ('q1', 2, 0, 0), ('pv', 1, 0, 8), ('q1', 3, 0, 3),
        ('wo', 0, 0, 14), ('wo', 1, 0, 14), ('pv', 2, 0, 16), ('pv', 3, 0, 20), ('wo', 2, 0, 20),
        ('q0', 0, 1, 20), ('wo', 3, 0, 20), ('q0', 1, 1, 20), ('pv', 4, 0, 22), ('q0', 2, 1, 22),
        ('wo', 4, 0, 21), ('pv', 5, 0, 25), ('q0', 3, 1, 27)]
ROOM = [29, 8, 9, 6, 5, 8, 12, 11, 10, 9, 7, 8, 8, 8, 9, 8, 9, 9, 11, 12, 8, 12, 12, 9, 13, 10, 12, 11, 13, 13,
        11, 7]


def part_of(step):
    return (step >= LAG) + (step >= 16) + (step >= 24)


ACT_ORDER = (("take", 0, "q", "normalise", 1, "exp", "weights"),
             ("take", "q", "normalise", 0, "exp", 1, "weights"),
             ("take", "normalise", 0, "exp", "weights", 1, "q"),
             ("take", "normalise", 0, "exp", "weights", 1, "q"))
DVE_ORDER = (("q", "max", "take", 0, 1),
             ("q", "max", "take", 0, 1),
             ("take", "q", "max", 0, 1),
             ("take", "max", "q", 0, 1))
PE_ORDER = (("scores", "fill", "fill", 0, "fill", 1),
            ("fill", "scores", 0, "fill", "fill", 1),
            ("scores", "fill", 0, "fill", 1, "fill"),
            ("scores", "fill", 0, "fill", 1, "fill"))
SHARES = ((1,), (0, 1), (1, 1.25, 1))


def products(kind, a):
    return 3 * (a + 1) if kind == "pv" else 12


def done_of(done, kind, a):
    return next((s for n, s in done.items() if FILL[n][:2] == (kind, a)), None)


def spread():
    steps, n, at, done = [[] for _ in range(CELLS)], 0, 0, {}
    for s in range(CELLS):
        room = ROOM[s] if s < CELLS - 1 else 10 ** 6
        while n < len(FILL) and FILL[n][3] <= s and room:
            kind, a, _g, _s = FILL[n]
            if at == 0 and (done.get(n - 2, -1) == s or kind == "wo" and done_of(done, "pv", a) == s):
                break
            take = min(room, products(kind, a) - at)
            steps[s].append((n, at, at + take))
            room, at = room - take, at + take
            if at == products(kind, a):
                done[n] = s
                n, at = n + 1, 0
    assert n == len(FILL)
    return steps


SPREAD = spread()
DONE_AT = {n: s for s in range(CELLS) for n, _a, b in SPREAD[s] if b == products(*FILL[n][:2])}


def cut(parts, weights):
    total, shares = sum(b - a for _n, a, b in parts), []
    ends = [round(total * sum(weights[:k]) / sum(weights)) for k in range(len(weights) + 1)]
    for lo, hi in zip(ends, ends[1:]):
        at, share = 0, []
        for place, a, b in parts:
            x, y = max(lo, at), min(hi, at + b - a)
            if x < y:
                share.append((place, a + x - at, a + y - at))
            at += b - a
        shares.append(share)
    return shares


def valid(n, turn):
    g = FILL[n][2]
    return {"first": g >= 0, "loop": True, "last": g <= 0, "end": g < 0}[turn]


def finished(step, turn, ago):
    s, before = step - ago, {"first": None, "loop": "loop", "last": "loop", "end": "last"}[turn]
    shift = 0
    if s < 0:
        if before is None:
            return []
        s, turn, shift = s + CELLS, before, -1
    if s >= CELLS:
        return []
    return [(n, FILL[n][0], FILL[n][1], FILL[n][2] + shift)
            for n in sorted(DONE_AT) if DONE_AT[n] == s and valid(n, turn)]


def bank_before(n, turn):
    shift, bank = 0, n % 2
    while True:
        n -= 1
        if n < 0:
            turn = {"first": None, "loop": "loop", "last": "loop", "end": "last"}[turn]
            if turn is None:
                return None
            n, shift = len(FILL) - 1, shift - 1
        if n % 2 == bank and valid(n, turn):
            return FILL[n][0], FILL[n][1], FILL[n][2] + shift


def program(nc, x, xT, wqT, wkrT, wdkT, wupkT, wupvT, woT, w13p, s13p, w2p, s2p, cosT, sinT, shifts, out):
    xs_d = nc.dram_tensor("xs_d", [NBLK, P, 2, DC, TB], F32).ap()
    k_d = nc.dram_tensor("k_d", [GROUPS // 4, 4, P, 2, S], F32).ap()
    v_d = nc.dram_tensor("v_d", [GROUPS, P, QT, 2, HD], F32).ap()
    y_d = nc.dram_tensor("y_d", [B, QT, P, D], F32).ap()
    x1_d = nc.dram_tensor("x1_d", [NBLK, 4, P, D], F32).ap()

    stage_a(nc, x, xT, wkrT, wdkT, wupkT, wupvT, cosT, sinT, xs_d, k_d, v_d, y_d)
    stage_b(nc, wqT, woT, cosT, sinT, xs_d, k_d, v_d, y_d)
    stage_c(nc, w13p, s13p, w2p, s2p, shifts, y_d, x1_d, out)


def words(ap):
    return ap.bitcast(F32)


def three_pass(nc, out, pairs, first=0, end=None):
    every = [(lhsT(a), rhs(b)) for lhsT, rhs in pairs for a, b in PASSES]
    for n in range(first, len(every) if end is None else end):
        ins = nc.tensor.matmul(out, *every[n], start=(n == 0), stop=(n == len(every) - 1))
    return ins


def stage_a(nc, x, xT, wkrT, wdkT, wupkT, wupvT, cosT, sinT, xs_d, k_d, v_d, y_d):
    with ExitStack() as ctx:
        def sb(name, shape, dt):
            return ctx.enter_context(nc.sbuf_tensor(name, shape, dt))

        def sem(name):
            return ctx.enter_context(nc.semaphore(name))

        raw = sb("a_raw", [P, 2, DC, 512], F32)
        wdk = sb("a_wdk", [P, 2, DC, 512], F32R)
        wkr = sb("a_wkr", [P, 2, DC, 512], F32R)
        wupk = sb("a_wupk", [P, 2, DC, 512], F32R)
        wupv = sb("a_wupv", [P, 2, 2, DC, 512], F32R)
        xraw = sb("a_xraw", [P, DC, TB], F32)
        xs = sb("a_xs", [P, 2, 2, DC, TB], F32R)
        cs = sb("a_cs", [P, 2, DC, TB], F32R)
        cosk = sb("a_cos", [P, S], F32)
        sink = sb("a_sin", [P, S], F32)
        rt = sb("a_rt", [P, 4, TB], F32)
        kf = sb("a_kf", [P, 2, TB], F32)
        ks = sb("a_ks", [P, 4, 2, TB], F32R)
        vs = sb("a_vs", [P, 2, 4, 2, HD], F32R)
        nop = sb("a_nop", [P, 2], F32)
        RING = 5
        bank = [ctx.enter_context(nc.psum_tensor(f"a_ps{i}", [P, TB], F32)) for i in range(RING)]

        w_in = [sem("a_w_in0"), sem("a_w_in1")]
        tab_in, x_in = sem("a_tab_in"), sem("a_x_in")
        w_hi, w_lo = sem("a_w_hi"), sem("a_w_lo")
        wdk_lo = sem("a_wdk_lo")
        x_hi, x_lo = sem("a_x_hi"), sem("a_x_lo")
        mm = sem("a_mm")
        bank_free = sem("a_bank_free")
        part_hi = sem("a_part_hi")
        rope_t, rope_done = sem("a_rope_t"), sem("a_rope_done")
        kr_lo = sem("a_kr_lo")
        k_out, xs_out, y_out = sem("a_k_out"), sem("a_xs_out"), sem("a_y_out")
        v_out = [sem("a_v_out0"), sem("a_v_out1")]

        MM0, FREE0, KRLO0, XLO0, OUT0 = 20, RING, 2, 1, 1
        WEIGHTS = [(wdkT, None, wdk), (wkrT, None, wkr), (wupkT, None, wupk), (wupvT, 0, wupv), (wupvT, 1, wupv)]
        NW = len(WEIGHTS)
        CG, RG, NG, VG, GROUPS_A = 0, 4, 8, 12, 20

        def weight_part(n):
            _s, half, w = WEIGHTS[n]
            return (lambda p: w[:, p]) if half is None else (lambda p: w[:, half, p])

        block = ctx.enter_context(nc.Block())

        @block.sync
        def _(sp):
            sp.dma_start(xraw[:], xT[0]).then_inc(x_in, 16)
            for n, (src, half, _w) in enumerate(WEIGHTS):
                if n == 2:
                    sp.wait_ge(wdk_lo, 1)
                if n >= 3:
                    sp.wait_ge(w_lo, n - 2)
                s = src if half is None else src[:, :, half * 512:half * 512 + 512]
                sp.dma_start(raw[:, n % 2], s).then_inc(w_in[n % 2], 16)
                if n == 1:
                    for g in range(4):
                        sp.dma_start(cosk[32 * g:32 * g + 32, :], cosT[0:32, :]).then_inc(tab_in, 16)
                        sp.dma_start(sink[32 * g:32 * g + 32, :], sinT[64:96, :]).then_inc(tab_in, 16)

            def block_of(t, last):
                sp.wait_ge(x_lo, t + 1 + XLO0)
                if not last:
                    sp.dma_start(xraw[:], xT[t + 1]).then_inc(x_in, 16)
                sp.dma_start(xs_d[t], words(xs[:, t % 2])).then_inc(xs_out, 16)
                for n in range(8):
                    quad, part = n // 2 % 2, 2 * (n % 2) + n // 4
                    if n < 4:
                        sp.wait_ge(kr_lo, 4 * t + n + 1 + KRLO0)
                    else:
                        sp.wait_ge(bank_free, GROUPS_A * t + NG + (n - 4) + 1 + FREE0)
                    sp.dma_start(k_d[(t // 2) * 2 + quad, part, :, :, bass.ds((t % 2) * TB, TB)],
                                 words(ks[:, n % 4])).then_inc(k_out, 16)
                for n in range(8):
                    sp.wait_ge(bank_free, GROUPS_A * t + VG + n + 1 + FREE0)
                    sp.dma_start(
                        v_d[bass.ds((t // 2) * KV + 4 * (n % 2), 4), :, (t % 2) * 4 + n // 2]
                        .rearrange("g p l d -> p g (l d)"),
                        words(vs[:, n % 2]).rearrange("p g l d -> p g (l d)")).then_inc(v_out[n % 2], 16)

            with sp.Fori(0, NBLK - 1) as t:
                block_of(t, False)
            sp.dma_start(y_d.rearrange("b i p d -> (b i p) d"), x.rearrange("b s d -> (b s) d")).then_inc(y_out, 16)
            block_of(NBLK - 1, True)
            sp.wait_ge(xs_out, 16 * NBLK + OUT0)
            sp.wait_ge(k_out, 16 * 8 * NBLK + OUT0)
            for p in range(2):
                sp.wait_ge(v_out[p], 16 * 4 * NBLK + OUT0)
            sp.wait_ge(y_out, 16)

        @block.gpsimd
        def _(pool):
            pool.sem_inc(x_lo, XLO0)
            pool.sem_inc(kr_lo, KRLO0)
            for n in range(1, NW):
                pool.wait_ge(w_hi, n + 1)
                w = weight_part(n)
                nc.gpsimd.tensor_tensor(w(LO), raw[:, n % 2], w(HI), ALU.subtract).then_inc(w_lo, 1)

            def rope_lo(t):
                for n in range(4):
                    pool.wait_ge(part_hi, GROUPS_A * t + RG + n + 1)
                    nc.gpsimd.tensor_tensor(ks[:, n, LO], kf[:, n % 2], ks[:, n, HI], ALU.subtract).then_inc(kr_lo, 1)

            with pool.Fori(0, NBLK) as t:
                rope_lo(t)

        @block.scalar
        def _(act):
            act.sem_inc(xs_out, OUT0)
            act.sem_inc(k_out, OUT0)
            act.sem_inc(v_out[0], OUT0)
            act.sem_inc(v_out[1], OUT0)
            def weight_hi(n):
                act.wait_ge(w_in[n % 2], 16 * (n // 2 + 1))
                w = weight_part(n)
                nc.scalar.activation(w(HI), raw[:, n % 2], ACT.Copy).then_inc(w_hi, 1)

            def x_split(t):
                if type(t) is not int:
                    act.wait_ge(xs_out, 16 * (t - 1) + OUT0)
                    nc.scalar.copy(nop[:, 0:1], cosk[:, 0:1])
                    act.wait_ge(x_in, 16 * t + 16)
                    nc.scalar.copy(nop[:, 1:2], cosk[:, 0:1])
                else:
                    act.wait_ge(x_in, 16 * t + 16)
                nc.scalar.activation(xs[:, t % 2, HI], xraw[:], ACT.Copy).then_inc(x_hi, 1)

            def block_of(t, first, last):
                for m in range(DC):
                    act.wait_ge(mm, GROUPS_A * t + CG + m + 1 + MM0)
                    nc.scalar.activation(cs[:, HI, m], bank[(CG + m) % RING][:], ACT.Copy).then_inc(part_hi, 1)
                if first:
                    weight_hi(3)
                    weight_hi(4)
                act.wait_ge(k_out, 16 * 8 * t + OUT0)
                for n in range(4):
                    act.wait_ge(rope_done, 4 * t + n + 1)
                    nc.scalar.activation(ks[:, n, HI], kf[:, n % 2], ACT.Copy).then_inc(part_hi, 1)
                if not last:
                    x_split(t + 1)
                act.wait_ge(k_out, 16 * (8 * t + 4) + OUT0)
                for n in range(4):
                    act.wait_ge(mm, GROUPS_A * t + NG + n + 1 + MM0)
                    nc.scalar.activation(ks[:, n, HI], bank[(NG + n) % RING][:], ACT.Copy).then_inc(part_hi, 1)
                for n in range(8):
                    act.wait_ge(mm, GROUPS_A * t + VG + n + 1 + MM0)
                    act.wait_ge(v_out[n % 2], 16 * (4 * t + n // 2) + OUT0)
                    nc.scalar.activation(vs[:, n % 2, :, HI, :],
                                         bank[(VG + n) % RING][:].rearrange("p (g d) -> p g d", g=4), ACT.Copy).then_inc(part_hi, 1)

            x_split(0)
            for n in range(3):
                weight_hi(n)
            block_of(0, True, False)
            with act.Fori(1, NBLK - 1) as t:
                block_of(t, False, False)
            block_of(NBLK - 1, False, True)

        @block.vector
        def _(dve):
            dve.sem_inc(bank_free, FREE0)
            def x_split(t):
                dve.wait_ge(x_hi, t + 1)
                nc.vector.tensor_tensor(xs[:, t % 2, LO], xraw[:], xs[:, t % 2, HI], ALU.subtract).then_inc(x_lo, 1)

            def block_of(t, last):
                for m in range(DC):
                    dve.wait_ge(part_hi, GROUPS_A * t + CG + m + 1)
                    nc.vector.tensor_tensor(cs[:, LO, m], bank[(CG + m) % RING][:], cs[:, HI, m],
                                            ALU.subtract).then_inc(bank_free, 1)
                dve.wait_ge(tab_in, 16 * 8)
                cos_t, sin_t = (w[:, bass.ds((t % 2) * TB, TB)] for w in (cosk, sink))
                for quad in range(2):
                    if quad == 1:
                        dve.wait_ge(rope_done, 4 * t + 2)
                    for k in range(2):
                        g = RG + 2 * quad + k
                        dve.wait_ge(mm, GROUPS_A * t + g + 1 + MM0)
                        nc.vector.tensor_tensor(rt[:, 2 * k], bank[g % RING][:], cos_t, ALU.mult).then_inc(rope_t, 1)
                        nc.vector.tensor_tensor(rt[:, 2 * k + 1], bank[g % RING][:], sin_t, ALU.mult)\
                            .then_inc(bank_free, 1)
                    dve.wait_ge(rope_t, 4 * t + 2 * quad + 2)
                    dve.wait_ge(bank_free, GROUPS_A * t + RG + 2 * quad + 2 + FREE0)
                    for k, (a, b, op) in enumerate(((0, 3, ALU.subtract), (2, 1, ALU.add))):
                        dve.wait_ge(kr_lo, 4 * t + 2 * quad + k + 1)
                        nc.vector.tensor_tensor(kf[:, k], rt[:, a], rt[:, b], op).then_inc(rope_done, 1)
                if not last:
                    x_split(t + 1)
                for n in range(4):
                    dve.wait_ge(part_hi, GROUPS_A * t + NG + n + 1)
                    nc.vector.tensor_tensor(ks[:, n, LO], bank[(NG + n) % RING][:], ks[:, n, HI],
                                            ALU.subtract).then_inc(bank_free, 1)
                for n in range(8):
                    dve.wait_ge(part_hi, GROUPS_A * t + VG + n + 1)
                    nc.vector.tensor_tensor(vs[:, n % 2, :, LO, :],
                                            bank[(VG + n) % RING][:].rearrange("p (g d) -> p g d", g=4),
                                            vs[:, n % 2, :, HI, :], ALU.subtract).then_inc(bank_free, 1)

            x_split(0)
            dve.wait_ge(w_hi, 1)
            nc.vector.tensor_tensor(wdk[:, LO], raw[:, 0], wdk[:, HI], ALU.subtract).then_inc(wdk_lo, 1)
            with dve.Fori(0, NBLK - 1) as t:
                block_of(t, False)
            block_of(NBLK - 1, True)

        @block.tensor
        def _(pe):
            pe.sem_inc(mm, MM0)

            def group(t, g, pairs):
                pe.wait_ge(bank_free, GROUPS_A * t + g + 1)
                three_pass(nc, bank[g % RING][:], pairs).then_inc(mm, 1)

            def project(w, m, src):
                return [(lambda p, k=k: w(p)[:, k, m * P:(m + 1) * P], lambda p, k=k: src[:, p, k]) for k in range(DC)]

            with pe.Fori(0, NBLK) as t:
                pe.wait_ge(x_lo, t + 1 + XLO0)
                pe.wait_ge(wdk_lo, 1)
                for m in range(4):
                    group(t, CG + m, project(weight_part(0), m, xs[:, t % 2]))
                pe.wait_ge(w_lo, 1)
                for m in range(4):
                    group(t, RG + m, project(weight_part(1), m, xs[:, t % 2]))
                pe.wait_ge(w_lo, 2)
                pe.wait_ge(bank_free, GROUPS_A * t + CG + 4 + FREE0)
                for m in range(4):
                    group(t, NG + m, project(weight_part(2), m, cs))
                pe.wait_ge(w_lo, NW - 1)
                for n in range(8):
                    w, tt = weight_part(3 + n % 2), n // 2
                    group(t, VG + n, [(lambda p, k=k: cs[:, p, k, tt * P:(tt + 1) * P], lambda p, k=k: w(p)[:, k])
                                      for k in range(DC)])


def stage_b(nc, wqT, woT, cosT, sinT, xs_d, k_d, v_d, y_d):
    with ExitStack() as ctx:
        def sb(name, shape, dt):
            return ctx.enter_context(nc.sbuf_tensor(name, shape, dt))

        def sem(name):
            return ctx.enter_context(nc.semaphore(name))

        xs = sb("b_xs", [P, 2, DC, TB], F32R)
        kt = sb("b_kt", [P, 2, S], F32R)
        vt = sb("b_vt", [P, QT, 2, HD], F32R)
        wraw = sb("b_wraw", [P, 2, 512], F32)
        wq = sb("b_wq", [P, GQ, 2, DC, HD], F32R)
        wo = sb("b_wo", [P, GQ, 2, D], F32R)
        qs = sb("b_qs", [P, 2, GQ, 2, TB], F32R)
        sw = sb("b_sw", [P, TB], F32)
        qf = sb("b_qf", [P, TB], F32)
        cosq = sb("b_cos", [P, S], F32)
        sinq = sb("b_sin", [P, S], F32)
        mask = sb("b_mask", [P, S], BF16)
        ident = sb("b_ident", [P, P], F32)
        sc = sb("b_sc", [P, S_RING, S], F32)
        spare = sb("b_spare", [P, 2], F32)
        nmax = sb("b_nmax", [P, S_RING], F32)
        rsum = sb("b_rsum", [P, S_RING], F32)
        rinv = sb("b_rinv", [P, S_RING], F32)
        pt = sb("b_pt", [P, PT_UNITS, 2, 4, GQ * P], F32R)
        ot = sb("b_ot", [P, 2, 2, GQ * P], F32R)
        ys = sb("b_ys", [P, 2, D], F32)
        sps = [ctx.enter_context(nc.psum_tensor(f"b_sps{i}", [P, S], F32)) for i in range(2)]
        tps = [ctx.enter_context(nc.psum_tensor(f"b_tps{i}", [P, 4, P], F32)) for i in range(2)]
        bank = [ctx.enter_context(nc.psum_tensor(f"b_ps{i}", [P, 512], F32)) for i in range(2)]

        tab_in, masked = sem("b_tab_in"), sem("b_masked")
        k_in, v_in, xs_in = sem("b_k_in"), sem("b_v_in"), sem("b_xs_in")
        w_in = [sem("b_w_in0"), sem("b_w_in1")]
        w_hi, w_lo = sem("b_w_hi"), sem("b_w_lo")
        y_in, y_out = [sem("b_y_in0"), sem("b_y_in1")], [sem("b_y_out0"), sem("b_y_out1")]
        s_done = sem("b_s_done")
        sc_done = sem("b_sc_done")
        exp_done, rinv_done, norm_done = sem("b_exp_done"), sem("b_rinv_done"), sem("b_norm_done")
        t_done = sem("b_t_done")
        pt_hi, pt_lo = sem("b_pt_hi"), sem("b_pt_lo")
        x0_in = [sem(f"b_x0_in{k}") for k in range(DC - 1)]
        q_mm, q_cos = sem("b_q_mm"), sem("b_q_cos")
        sw_done, sin_done, add_done = sem("b_sw_done"), sem("b_sin_done"), sem("b_add_done")
        q_hi, q_lo = sem("b_q_hi"), sem("b_q_lo")
        pv_done, ot_hi, ot_lo = sem("b_pv_done"), sem("b_ot_hi"), sem("b_ot_lo")
        wo_done, y_added = sem("b_wo_done"), sem("b_y_added")

        SC0, TD0, PTLO0, PV0, WO0, ADD0, QLO0, YO0, WL0 = 2, 8, 2, 4, 8, 1, 1, 1, 2
        LAST = GROUPS - 1
        WPG = 8

        def thru(c):
            return pieces(c)[-1][0] + 1 if c >= 0 else pieces(c + CELLS)[-1][0] + 1 - PIECES

        def cell_at(step, it, turn):
            if step >= 0:
                return (it, step) if turn != "end" and step < CELLS else None
            return (it - 1, step + CELLS) if turn != "first" else None

        def scores_width(i):
            w = P * (i + 1)
            return [(0, max(w, 256))] if w <= 512 else [(0, w // 2), (w // 2, w)]

        def both_banks(ps, i):
            w = P * (i + 1)
            return ps[:, 0:w] if w <= 512 else ps[:, :].rearrange("p (b n) -> p b n", b=2)[:, :, 0:w // 2]

        def like_banks(ap, i):
            return ap if i < 4 else ap.rearrange("p (b n) -> p b n", b=2)

        def steps_of(turn):
            return range(CELLS) if turn != "end" else range(max(DONE_AT[n] for n in DONE_AT if FILL[n][2] < 0) + 3)

        def turns(engine, turn_of):
            turn_of(0, "first")
            with engine.Fori(1, LAST) as it:
                turn_of(it, "loop")
            turn_of(LAST, "last")
            turn_of(GROUPS, "end")

        WO_SPLIT = [DONE_AT[next(n for n, f in enumerate(FILL) if f[:2] == ("wo", 7))] + 1 + h for h in range(GQ)]
        WQ_SPLIT = [max(DONE_AT[n] for n, f in enumerate(FILL) if f[:2] == ("q1", 3)) + 1 + h for h in range(GQ)]
        WO_LOADS = [s - 4 for s in WO_SPLIT]
        WQ_LOADS = [max(WO_SPLIT[2 + h % 2] + 1, s - 4) if h < 2 else WQ_SPLIT[h - 2] + 1
                    for h, s in enumerate(WQ_SPLIT)]

        block = ctx.enter_context(nc.Block())

        @block.sync
        def _(sp):
            def load_wq(it, h):
                sp.wait_ge(w_lo, WPG * it + h + 1)
                sp.dma_start(wraw[:, h % 2].rearrange("p (k m) -> p k m", k=DC), wqT[(it % KV) * GQ + h])\
                    .then_inc(w_in[h % 2], 16)

            def load_wo(it, h):
                sp.wait_ge(w_lo, WPG * it + 4 + h + 1)
                sp.dma_start(wraw[:, h % 2], woT[(it % KV) * GQ + h]).then_inc(w_in[h % 2], 16)

            def load_k(it):
                for part in range(4):
                    sp.dma_start(words(kt[32 * part:32 * part + 32]), k_d[it // 4, part, bass.ds((it % 4) * 32, 32)])\
                        .then_inc(k_in, 16)

            def load_v(it):
                sp.dma_start(words(vt[:]), v_d[it]).then_inc(v_in, 16)

            def load_xs(it, blk):
                sp.dma_start(words(xs[:]), xs_d[(it // KV) * 2 + blk]).then_inc(xs_in, 16)

            def load_y(it, i):
                sp.wait_ge(y_out[i % 2], 16 * (4 * it + i // 2) + YO0)
                sp.dma_start(ys[:, i % 2], y_d[it // KV, i]).then_inc(y_in[i % 2], 16)

            def store_y(it, i):
                sp.wait_ge(y_added, QT * it + i + 1)
                sp.dma_start(y_d[it // KV, i], ys[:, i % 2]).then_inc(y_out[i % 2], 16)

            def turn_of(it, turn):
                for step in steps_of(turn):
                    if step == 0 and turn in ("loop", "last"):
                        sp.wait_ge(s_done, CELLS * it)
                        load_k(it)
                    for _n, kind, a, g in finished(step, turn, 1):
                        if kind == "q0" and a == 3:
                            sp.wait_ge(q_mm, 8 * (it + g) + 4)
                            load_xs(it + g, 1)
                        if kind == "q1" and a == 3 and turn != "last":
                            sp.wait_ge(q_mm, 8 * (it + g) + 8)
                            load_xs(it + g + 1, 0)
                        if kind == "pv" and a == 7 and turn != "end":
                            sp.wait_ge(pv_done, QT * (it + g + 1) + PV0)
                            load_v(it + g + 1)
                    for _n, kind, a, g in finished(step, turn, 2):
                        if kind == "wo":
                            store_y(it + g, a)
                            if a + 2 < QT:
                                load_y(it + g, a + 2)
                            elif turn != "end":
                                load_y(it + g + 1, a + 2 - QT)
                    if turn != "end" and step in WO_LOADS:
                        load_wo(it, WO_LOADS.index(step))
                    if turn in ("first", "loop") and step in WQ_LOADS:
                        load_wq(it + 1, WQ_LOADS.index(step))

            load_wq(0, 0)
            for k in range(DC):
                sp.dma_start(words(xs[:, :, k]), xs_d[0, :, :, k]).then_inc(x0_in[k] if k < DC - 1 else xs_in, 16)
            load_wq(0, 1)
            sp.dma_start(sinq[:], sinT).then_inc(tab_in, 16)
            sp.dma_start(cosq[:], cosT).then_inc(tab_in, 16)
            load_wq(0, 2)
            load_wq(0, 3)
            load_k(0)
            load_v(0)
            sp.wait_ge(q_mm, 4)
            load_xs(0, 1)
            load_y(0, 0)
            load_y(0, 1)
            turns(sp, turn_of)
            for p in range(2):
                sp.wait_ge(y_out[p], 16 * 4 * GROUPS + YO0)

        @block.gpsimd
        def _(pool):
            pool.sem_inc(w_lo, WL0)
            pool.sem_inc(q_lo, QLO0)
            nc.gpsimd.memset(mask[:], 0.0).then_inc(masked, 1)
            nc.gpsimd.memset(ident[:], 0.0).then_inc(masked, 1)
            pool.wait_ge(masked, 2)
            nc.gpsimd.affine_select(out=mask[:, S - P:S], in_=mask[:, S - P:S], compare_op=ALU.is_ge, fill=MASKED,
                                    base=0, pattern=[[-1, P]], channel_multiplier=1).then_inc(masked, 1)
            nc.gpsimd.affine_select(out=ident[:], in_=ident[:], compare_op=ALU.not_equal, fill=1.0,
                                    base=0, pattern=[[-1, P]], channel_multiplier=1).then_inc(masked, 1)

            def times_sin(it, blk, h):
                pool.wait_ge(sw_done, 2 * (8 * it + 4 * blk + h + 1))
                nc.gpsimd.tensor_tensor(sw[:], sw[:], sinq[:, blk * TB:blk * TB + TB], ALU.mult).then_inc(sin_done, 1)

            def split_q(it, blk, h):
                pool.wait_ge(q_hi, 8 * it + 4 * blk + h + 1)
                nc.gpsimd.tensor_tensor(qs[:, blk, h, LO], qf[:], qs[:, blk, h, HI], ALU.subtract).then_inc(q_lo, 1)

            def split_wq(it, h):
                pool.wait_ge(w_hi, WPG * it + h + 1)
                nc.gpsimd.tensor_tensor(wq[:, h, LO].rearrange("p k m -> p (k m)"), wraw[:, h % 2],
                                        wq[:, h, HI].rearrange("p k m -> p (k m)"), ALU.subtract).then_inc(w_lo, 1)

            def split_wo(it, h):
                pool.wait_ge(w_hi, WPG * it + 4 + h + 1)
                nc.gpsimd.tensor_tensor(wo[:, h, LO], wraw[:, h % 2], wo[:, h, HI], ALU.subtract).then_inc(w_lo, 1)

            def turn_of(it, turn):
                for step in steps_of(turn):
                    for _n, kind, h, g in finished(step, turn, 2):
                        if kind in ("q0", "q1"):
                            split_q(it + g, int(kind == "q1"), h)
                    for _n, kind, h, g in finished(step, turn, 1):
                        if kind in ("q0", "q1"):
                            times_sin(it + g, int(kind == "q1"), h)
                    if turn != "end" and step in WO_SPLIT:
                        split_wo(it, WO_SPLIT.index(step))
                    if turn in ("first", "loop") and step in WQ_SPLIT:
                        split_wq(it + 1, WQ_SPLIT.index(step))

            for h in range(GQ):
                split_wq(0, h)
            pool.wait_ge(tab_in, 32)
            for h in range(GQ):
                times_sin(0, 0, h)
            turns(pool, turn_of)

        @block.scalar
        def _(act):
            act.sem_inc(y_out[0], YO0)
            act.sem_inc(y_out[1], YO0)

            def swap_q(it, blk, h, bk):
                n = 8 * it + 4 * blk + h
                act.wait_ge(q_mm, n + 1)
                act.wait_ge(add_done, n + 1)
                nc.scalar.activation(sw[0:64], bank[bk][64:128], ACT.Copy).then_inc(sw_done, 1)
                nc.scalar.activation(sw[64:128], bank[bk][0:64], ACT.Copy).then_inc(sw_done, 1)

            def hi_q(it, blk, h):
                act.wait_ge(add_done, 8 * it + 4 * blk + h + 1 + ADD0)
                nc.scalar.activation(qs[:, blk, h, HI], qf[:], ACT.Copy).then_inc(q_hi, 1)

            def hi_wq(it, h):
                act.wait_ge(w_in[h % 2], 16 * (4 * it + h // 2 + 1))
                if not (isinstance(it, int) and it == 0):
                    act.wait_ge(q_mm, 8 * it - 4 + h + 1)
                nc.scalar.activation(wq[:, h, HI].rearrange("p k m -> p (k m)"), wraw[:, h % 2], ACT.Copy)\
                    .then_inc(w_hi, 1)

            def hi_wo(it, h):
                act.wait_ge(w_in[h % 2], 16 * (4 * it + 2 + h // 2 + 1))
                act.wait_ge(wo_done, QT * it + WO0)
                nc.scalar.activation(wo[:, h, HI], wraw[:, h % 2], ACT.Copy).then_inc(w_hi, 1)

            def exp(it, c):
                slot, w = c % S_RING, P * (c // GQ + 1)
                act.wait_ge(sc_done, CELLS * it + c + 1 + SC0)
                nc.scalar.activation(sc[:, slot, 0:w], sc[:, slot, 0:w], ACT.Exp, bias=nmax[:, slot:slot + 1],
                                     scale=-1.0, accum_out=rsum[:, slot:slot + 1]).then_inc(exp_done, 1)

            def normalise(it, c):
                slot, w = c % S_RING, P * (c // GQ + 1)
                act.wait_ge(rinv_done, CELLS * it + c + 1)
                nc.scalar.activation(sc[:, slot, 0:w], sc[:, slot, 0:w], ACT.Copy, scale=rinv[:, slot:slot + 1])\
                    .then_inc(norm_done, 1)

            def hi_pt(it, c, which):
                i, h = c // GQ, c % GQ
                for n, j0, nj in pieces(c)[which:which + 1]:
                    u = unit_of(i, j0)
                    act.wait_ge(t_done, PIECES * it + n + 1 + TD0)
                    if h == 0:
                        tile = UNIT_TILE[(u - PT_UNITS) % UNITS] - (QT if u < PT_UNITS else 0)
                        act.wait_ge(pv_done, QT * it + tile + 1 + PV0)
                    nc.scalar.activation(pt[:, u % PT_UNITS, HI, 0:nj, h * P:(h + 1) * P], tps[n % 2][:, 0:nj],
                                         ACT.Copy)\
                        .then_inc(pt_hi, 1)

            def hi_ot(it, i, bk):
                act.wait_ge(pv_done, QT * it + i + 1 + PV0)
                act.wait_ge(wo_done, QT * it + i - 1 + WO0)
                nc.scalar.activation(ot[:, i % 2, HI], bank[bk][:], ACT.Copy).then_inc(ot_hi, 1)

            def take(n, kind, it, a):
                if kind in ("q0", "q1"):
                    swap_q(it, int(kind == "q1"), a, n % 2)
                elif kind == "pv":
                    hi_ot(it, a, n % 2)

            def turn_of(it, turn):
                for step in steps_of(turn):
                    for job in ACT_ORDER[part_of(step)]:
                        if job == "take":
                            for n, kind, a, g in finished(step, turn, 1):
                                take(n, kind, it + g, a)
                        elif job == "normalise":
                            if cell := cell_at(step - 2, it, turn):
                                normalise(*cell)
                        elif job == "exp":
                            if cell := cell_at(step, it, turn):
                                exp(*cell)
                        elif job == "q":
                            for _n, kind, a, g in finished(step, turn, 2):
                                if kind in ("q0", "q1"):
                                    hi_q(it + g, int(kind == "q1"), a)
                        elif job == "weights":
                            if turn != "end" and step in WO_SPLIT:
                                hi_wo(it, WO_SPLIT.index(step))
                            if turn in ("first", "loop") and step in WQ_SPLIT:
                                hi_wq(it + 1, WQ_SPLIT.index(step))
                        elif cell := cell_at(step - LAG, it, turn):
                            hi_pt(*cell, job)

            for h in range(GQ):
                hi_wq(0, h)
            for h in range(GQ):
                swap_q(0, 0, h, h % 2)
                hi_q(0, 0, h)
            turns(act, turn_of)

        @block.vector
        def _(dve):
            dve.sem_inc(sc_done, SC0)
            dve.sem_inc(pt_lo, PTLO0)
            dve.sem_inc(add_done, ADD0)
            dve.wait_ge(tab_in, 32)
            dve.wait_ge(masked, 4)

            def cos_q(it, blk, h, bk):
                n = 8 * it + 4 * blk + h
                dve.wait_ge(sw_done, 2 * (n + 1))
                dve.wait_ge(q_lo, n + 1)
                nc.vector.tensor_tensor(qf[:], bank[bk][:], cosq[:, blk * TB:blk * TB + TB], ALU.mult)\
                    .then_inc(q_cos, 1)

            def add_q(it, blk, h):
                n = 8 * it + 4 * blk + h
                dve.wait_ge(sin_done, n + 1)
                dve.wait_ge(q_cos, n + 1)
                nc.vector.tensor_tensor(qf[:], qf[:], sw[:], ALU.add).then_inc(add_done, 1)

            def scores_there(it, c):
                dve.wait_ge(s_done, CELLS * it + c + 1)
                dve.wait_ge(t_done, PIECES * it + thru(c - S_RING) + TD0)

            def mask_max(it, c):
                i, slot = c // GQ, c % S_RING
                w = P * (i + 1)
                nc.vector.tensor_tensor_reduce(out=like_banks(sc[:, slot, 0:w], i), in0=both_banks(sps[c % 2], i),
                                               in1=like_banks(mask[:, S - w:S], i),
                                               scale=-SCALE, scalar=3.0e38, op0=ALU.add, op1=ALU.min,
                                               accum_out=nmax[:, slot:slot + 1]).then_inc(sc_done, 1)

            def reciprocal(it, c):
                slot = c % S_RING
                dve.wait_ge(exp_done, CELLS * it + c + 1)
                nc.vector.reciprocal(rinv[:, slot:slot + 1], rsum[:, slot:slot + 1]).then_inc(rinv_done, 1)

            def lo_pt(it, c, which):
                i, h = c // GQ, c % GQ
                for n, j0, nj in pieces(c)[which:which + 1]:
                    u = unit_of(i, j0) % PT_UNITS
                    dve.wait_ge(pt_hi, PIECES * it + n + 1)
                    nc.vector.tensor_tensor(pt[:, u, LO, 0:nj, h * P:(h + 1) * P], tps[n % 2][:, 0:nj],
                                            pt[:, u, HI, 0:nj, h * P:(h + 1) * P], ALU.subtract).then_inc(pt_lo, 1)

            def lo_ot(it, i, bk):
                dve.wait_ge(ot_hi, QT * it + i + 1)
                nc.vector.tensor_tensor(ot[:, i % 2, LO], bank[bk][:], ot[:, i % 2, HI], ALU.subtract)\
                    .then_inc(ot_lo, 1)

            def add_y(it, i, bk):
                dve.wait_ge(wo_done, QT * it + i + 1 + WO0)
                dve.wait_ge(y_in[i % 2], 16 * (4 * it + i // 2 + 1))
                nc.vector.tensor_tensor(ys[:, i % 2], bank[bk][:], ys[:, i % 2], ALU.add).then_inc(y_added, 1)

            def take(n, kind, it, a):
                if kind in ("q0", "q1"):
                    cos_q(it, int(kind == "q1"), a, n % 2)
                elif kind == "pv":
                    lo_ot(it, a, n % 2)
                else:
                    add_y(it, a, n % 2)

            def turn_of(it, turn):
                for step in steps_of(turn):
                    here = cell_at(step, it, turn)
                    for job in DVE_ORDER[part_of(step)]:
                        if job == "take":
                            for n, kind, a, g in finished(step, turn, 1):
                                take(n, kind, it + g, a)
                        elif job == "max":
                            if here:
                                scores_there(*here)
                            if cell := cell_at(step - 2, it, turn):
                                reciprocal(*cell)
                            elif here:
                                nc.vector.memset(spare[:, step:step + 1], 0.0)
                            if here:
                                mask_max(*here)
                        elif job == "q":
                            for _n, kind, a, g in finished(step, turn, 2):
                                if kind in ("q0", "q1"):
                                    add_q(it + g, int(kind == "q1"), a)
                        elif cell := cell_at(step - LAG, it, turn):
                            lo_pt(*cell, job)

            for h in range(GQ):
                cos_q(0, 0, h, h % 2)
                add_q(0, 0, h)
                dve.wait_ge(q_hi, h + 1)
                nc.vector.tensor_tensor(qs[:, 0, h, LO], qf[:], qs[:, 0, h, HI], ALU.subtract).then_inc(q_lo, 1)
            turns(dve, turn_of)

        @block.tensor
        def _(pe):
            pe.sem_inc(t_done, TD0)
            pe.sem_inc(pv_done, PV0)
            pe.sem_inc(wo_done, WO0)
            pe.wait_ge(masked, 4)

            def scores(it, c):
                i, h = c // GQ, c % GQ
                if c == 0:
                    pe.wait_ge(k_in, 64 * (it + 1))
                pe.wait_ge(q_lo, 8 * it + 4 * (i // 4) + h + 1 + QLO0)
                pe.wait_ge(sc_done, CELLS * it + c + 1)
                q = (i % 4) * P
                for k, (a, b) in enumerate(scores_width(i)):
                    last = three_pass(nc, sps[c % 2][:, 512 * k:512 * k + b - a],
                                      [(lambda p: qs[:, i // 4, h, p, q:q + P], lambda p: kt[:, p, a:b])])
                last.then_inc(s_done, 1)

            def transposes(it, c, piece):
                n, j0, nj = piece
                pe.wait_ge(norm_done, CELLS * it + c + 1)
                pe.wait_ge(pt_lo, PIECES * it + n + 1)
                for j in range(nj):
                    last = nc.tensor.transpose(tps[n % 2][:, j], sc[:, c % S_RING, (j0 + j) * P:(j0 + j + 1) * P],
                                               ident[:])
                last.then_inc(t_done, 1)

            def bank_taken(kind, a, it):
                if kind == "pv":
                    pe.wait_ge(ot_lo, QT * it + a + 1)
                elif kind == "wo":
                    pe.wait_ge(y_added, QT * it + a + 1)
                else:
                    pe.wait_ge(q_cos, 8 * it + 4 * int(kind == "q1") + a + 1)

            def head_products(h, bk, a, b):
                return three_pass(nc, bank[bk][:], [(lambda p, k=k: wq[:, h, p, k], lambda p, k=k: xs[:, p, k])
                                                    for k in range(DC)], a, b)

            def queries(it, blk, h, bk, a, b):
                if a == 0:
                    pe.wait_ge(xs_in, 16 * (2 * it + blk + 1))
                    pe.wait_ge(w_lo, WPG * it + h + 1 + WL0)
                ins = head_products(h, bk, a, b)
                if b == products("q0", h):
                    ins.then_inc(q_mm, 1)

            def values(it, i, bk, a, b):
                if a == 0:
                    if i == 0:
                        pe.wait_ge(v_in, 16 * (it + 1))
                    pe.wait_ge(pt_lo, PIECES * it + thru(GQ * i + GQ - 1) + PTLO0)
                ins = three_pass(nc, bank[bk][:],
                                 [(lambda p, j=j: vt[:, j, p], lambda p, j=j: pt[:, unit_of(i, j) % PT_UNITS, p, j % 4])
                                  for j in range(i + 1)], a, b)
                if b == products("pv", i):
                    ins.then_inc(pv_done, 1)

            def project(it, i, bk, a, b):
                if a == 0:
                    pe.wait_ge(w_lo, WPG * (it + 1) + WL0)
                    pe.wait_ge(ot_lo, QT * it + i + 1)
                ins = three_pass(nc, bank[bk][:],
                                 [(lambda p, h=h: ot[:, i % 2, p, h * P:(h + 1) * P], lambda p, h=h: wo[:, h, p])
                                  for h in range(GQ)], a, b)
                if b == products("wo", i):
                    ins.then_inc(wo_done, 1)

            FIRST = next(n for n in range(len(FILL)) if valid(n, "first"))

            def fill(it, turn, parts):
                for n, a, b in parts:
                    if not valid(n, turn):
                        continue
                    kind, t, g, _s = FILL[n]
                    if a == 0 and turn == "first" and n == FIRST:
                        pe.wait_ge(q_cos, GQ)
                    if a == 0 and (before := bank_before(n, turn)):
                        bank_taken(before[0], before[1], it + before[2])
                    if kind == "pv":
                        values(it + g, t, n % 2, a, b)
                    elif kind == "wo":
                        project(it + g, t, n % 2, a, b)
                    else:
                        queries(it + g, int(kind == "q1"), t, n % 2, a, b)

            def turn_of(it, turn):
                for step in range(CELLS):
                    parts = SPREAD[step]
                    here, cell = cell_at(step, it, turn), cell_at(step - LAG, it, turn)
                    if step == 0:
                        fill(it, turn, parts)
                        parts = []
                    ts = pieces(cell[1]) if cell else []
                    shares = cut(parts, SHARES[len(ts)])
                    for job in PE_ORDER[part_of(step)]:
                        if job == "scores":
                            if here:
                                scores(*here)
                        elif job == "fill":
                            if shares:
                                fill(it, turn, shares.pop(0))
                        elif job < len(ts):
                            transposes(*cell, ts[job])

            for k in range(DC - 1):
                pe.wait_ge(x0_in[k], 16)
                if k == 0:
                    pe.wait_ge(w_lo, 1 + WL0)
                head_products(0, 0, 3 * k, 3 * k + 3)
            pe.wait_ge(xs_in, 16)
            head_products(0, 0, 3 * DC - 3, 3 * DC).then_inc(q_mm, 1)
            for h in range(1, GQ):
                if h >= 2:
                    pe.wait_ge(q_cos, h - 1)
                queries(0, 0, h, h % 2, 0, products("q0", h))
            turns(pe, turn_of)


class LayerNorm:

    def __init__(self, nc, sb, sem, name, tile):
        self.nc, self.tile = nc, tile
        self.stats = sb(f"{name}_stats", [P, 4, 6], F32)
        self.mv = sb(f"{name}_mv", [P, 4, 2], F32)
        self.var, self.sd, self.rs, self.tmp = (sb(f"{name}_{n}", [P, 4], F32) for n in ("var", "sd", "rs", "tmp"))
        self.st, self.link, self.asked, self.sqrt_done, self.done = (
            sem(f"{name}_{n}") for n in ("st", "link", "asked", "sqrt_done", "done"))

    def statistics(self, dve, g, tile_in=None):
        nc = self.nc
        for t in range(4):
            if tile_in:
                dve.wait_ge(tile_in[t], 16)
            nc.vector.bn_stats(self.stats[:, t], self.tile(t)).then_inc(self.st, 1)
        dve.wait_ge(self.st, 9 * g + 4)
        nc.vector.memset(self.tmp[:], 0.0)
        for t in range(4):
            nc.vector.bn_aggr(self.mv[:, t], self.stats[:, t]).then_inc(self.st, 1)
        dve.wait_ge(self.st, 9 * g + 8)
        nc.vector.tensor_copy(self.var[:], self.mv[:, :, 1]).then_inc(self.st, 1)
        dve.wait_ge(self.st, 9 * g + 9)
        nc.vector.tensor_scalar(self.var[:], self.var[:], EPS, None, ALU.add).then_inc(self.asked, 1)

    def square_root(self, act, g):
        act.wait_ge(self.asked, g + 1)
        self.nc.scalar.activation(self.sd[:], self.var[:], ACT.Sqrt).then_inc(self.sqrt_done, 1)

    def normalise(self, dve, g):
        nc, var, sd, rs, tmp = self.nc, self.var[:], self.sd[:], self.rs[:], self.tmp[:]
        dve.wait_ge(self.asked, g + 1)
        dve.wait_ge(self.sqrt_done, g + 1)
        nc.vector.reciprocal(rs, sd).then_inc(self.link, 1)
        dve.wait_ge(self.link, 5 * g + 1)
        nc.vector.tensor_tensor(tmp, rs, rs, ALU.mult).then_inc(self.link, 1)
        dve.wait_ge(self.link, 5 * g + 2)
        nc.vector.tensor_tensor(tmp, tmp, var, ALU.mult).then_inc(self.link, 1)
        dve.wait_ge(self.link, 5 * g + 3)
        nc.vector.tensor_scalar(tmp, tmp, -0.5, 1.5, ALU.mult, ALU.add).then_inc(self.link, 1)
        dve.wait_ge(self.link, 5 * g + 4)
        nc.vector.tensor_tensor(rs, rs, tmp, ALU.mult).then_inc(self.link, 1)
        dve.wait_ge(self.link, 5 * g + 5)
        for t in range(4):
            nc.vector.tensor_scalar(self.tile(t), self.tile(t), self.mv[:, t, 0:1], self.rs[:, t:t + 1],
                                    ALU.subtract, ALU.mult).then_inc(self.done, 1)


def stage_c(nc, w13p, s13p, w2p, s2p, shifts, y_d, x1_d, out):
    with ExitStack() as ctx:
        def sb(name, shape, dt):
            return ctx.enter_context(nc.sbuf_tensor(name, shape, dt))

        def sem(name):
            return ctx.enter_context(nc.semaphore(name))

        w1 = sb("c_w1", [P, 2, DC, F], F32R)
        w3 = sb("c_w3", [P, 2, DC, F], F32R)
        w2 = sb("c_w2", [P, 2, FT, D], F32R)
        pk = sb("c_pk", [P, 2, 3, 512], I32)
        sl = sb("c_sl", [P, 2, 3, 512], F32)
        sh = sb("c_sh", [P, 5, 2], I32)
        ident = sb("c_ident", [P, P], F32)
        nop = sb("c_nop", [P, 1], F32)
        yb = sb("c_yb", [P, 4, D], F32)
        xs = sb("c_xs", [P, 2, 2, DC, TB], F32R)
        hb = sb("c_hb", [P, 2, TB], F32)
        hs = sb("c_hs", [P, 2, 2, TB], F32R)
        ab = [[ctx.enter_context(nc.psum_tensor(f"c_{n}{i}", [P, TB], F32)) for n in "ab"] for i in range(2)]
        yps = [ctx.enter_context(nc.psum_tensor(f"c_y{i}", [P, D], F32)) for i in range(4)]

        x1_tiles = sl[:].rearrange("p b m d -> p (b m) d")
        norm1 = LayerNorm(nc, sb, sem, "c_n1", lambda t: yb[:, t])
        norm2 = LayerNorm(nc, sb, sem, "c_n2", lambda t: sl[:, t // 3, t % 3])

        ids, sh_in = sem("c_ids"), sem("c_sh_in")
        pk_in = [sem("c_pk_in0"), sem("c_pk_in1")]
        shifted, unpacked, w_hi, w_lo = sem("c_shifted"), sem("c_unpacked"), sem("c_w_hi"), sem("c_w_lo")
        y_in, x1_out, x1_in, o_out = sem("c_y_in"), sem("c_x1_out"), sem("c_x1_in"), sem("c_o_out")
        y0_in = [sem(f"c_y0_in{t}") for t in range(3)] + [y_in]
        t_done, t_hi, t_lo = sem("c_t_done"), sem("c_t_hi"), sem("c_t_lo")
        a_done, b_done, ab_free = sem("c_a_done"), sem("c_b_done"), sem("c_ab_free")
        silu_done, h_hi, h_lo, h_used = sem("c_silu_done"), sem("c_h_hi"), sem("c_h_lo"), sem("c_h_used")
        y_done, z_done = sem("c_y_done"), sem("c_z_done")

        HLO0, HU0, Z0 = 2, 2, 1
        LOADS = 5

        TURN = (("t", (0, 1)), ("t", (2,)), ("t", (3,)))
        AHEAD = len(TURN)

        def items(last):
            out_ = []
            for f in range(FT):
                if f >= 6 and f < 6 + len(TURN) and not last:
                    out_.append(TURN[f - 6])
                out_.append(("f", f))
            return out_

        PER = len(items(False))

        def before(n, index):
            return AHEAD + PER * n + index

        def bank_pair(n, tiles):
            index = TURN.index(("t", tiles)) if type(n) is int and n == 0 else items(False).index(("t", tiles))
            return ab[index % 2]

        def width(f):
            return min(P, F - f * P)

        def reuse(f):
            return 1 if f == 0 else 2

        blocks_of_y = y_d.rearrange("b (h i) p d -> (b h) i p d", i=4)
        block = ctx.enter_context(nc.Block())

        @block.sync
        def _(sp):
            def load_y(n):
                sp.dma_start(yb[:], blocks_of_y[n].rearrange("i p d -> p i d")).then_inc(y_in, 16)

            def store_x1(n):
                sp.wait_ge(t_done, 4 * n + 4)
                sp.dma_start(x1_d[n].rearrange("i p d -> p i d"), yb[:]).then_inc(x1_out, 16)

            def next_y(n):
                sp.wait_ge(x1_out, 16 * n)
                load_y(n)

            def load_x1(n):
                sp.dma_start(x1_tiles[:, 0:4], x1_d[n].rearrange("i p d -> p i d")).then_inc(x1_in, 16)

            def store_out(n):
                sp.wait_ge(norm2.done, 4 * n + 4)
                sp.dma_start(out[n].rearrange("i p d -> p i d"), x1_tiles[:, 0:4]).then_inc(o_out, 16)

            def weights(f):
                if f >= 2:
                    sp.wait_ge(w_lo, 3 * (f - 1))
                n, b = width(f), f % 2
                at, size = 2 * DC * P * f, 2 * DC * n
                sp.dma_start(pk[:, b, 0:2, 0:DC * n], w13p[:, at:at + size].rearrange("p (m c) -> p m c", m=2))\
                    .then_inc(pk_in[b], 16)
                for half in range(2):
                    sp.dma_start(sl[64 * half:64 * half + 64, b, 0:2, 0:DC * n],
                                 s13p[half:half + 1, at:at + size].rearrange("p (m c) -> p m c", m=2)
                                 .broadcast_to((64, 2, DC * n))).then_inc(pk_in[b], 16)
                sp.dma_start(pk[0:n, b, 2], w2p[f * P:f * P + n]).then_inc(pk_in[b], 16)
                sp.dma_start(sl[0:n, b, 2], s2p[f * P:f * P + n]).then_inc(pk_in[b], 16)

            for t in range(4):
                sp.dma_start(yb[:, t], blocks_of_y[0, t]).then_inc(y0_in[t], 16)
            sp.dma_start(sh[:], shifts).then_inc(sh_in, 16)
            for f in range(FT):
                weights(f)
                if f == 1:
                    store_x1(0)
                if f == 2:
                    next_y(1)
            store_x1(1)
            sp.wait_ge(w_lo, 3 * FT)
            load_x1(0)

            def block_io(n, last):
                if not last:
                    next_y(n + 1)
                store_out(n - 1)
                sp.wait_ge(o_out, 16 * n)
                load_x1(n)
                if not last:
                    store_x1(n + 1)

            with sp.Fori(1, NBLK - 1) as n:
                block_io(n, False)
            block_io(NBLK - 1, True)
            for t in (0, 2):
                sp.wait_ge(norm2.done, 4 * (NBLK - 1) + t + 2)
                sp.dma_start(out[NBLK - 1, t:t + 2].rearrange("i p d -> p i d"), x1_tiles[:, t:t + 2])\
                    .then_inc(o_out, 16)
            sp.wait_ge(x1_out, 16 * NBLK)
            sp.wait_ge(o_out, 16 * (NBLK + 1))

        def split_views(m, f, p):
            n, b = width(f), f % 2
            if m < 2:
                w = (w1, w3)[m]
                return w[:, p, :, f * P:f * P + n], sl[:, b, m, 0:DC * n].rearrange("p (k c) -> p k c", k=DC)
            return w2[0:n, p, f].rearrange("p (m c) -> p c m", c=4), sl[0:n, b, 2].rearrange("p (c m) -> p c m", c=4)

        @block.gpsimd
        def _(pool):
            nc.gpsimd.memset(ident[:], 0.0).then_inc(ids, 1)
            pool.wait_ge(ids, 1)
            nc.gpsimd.affine_select(out=ident[:], in_=ident[:], compare_op=ALU.not_equal, fill=1.0,
                                    base=0, pattern=[[-1, P]], channel_multiplier=1).then_inc(ids, 1)
            for f in range(FT):
                for m in range(3):
                    pool.wait_ge(w_hi, 3 * f + m + 1)
                    lo, src = split_views(m, f, LO)
                    nc.gpsimd.tensor_tensor(lo, src, split_views(m, f, HI)[0], ALU.subtract).then_inc(w_lo, 1)

        @block.scalar
        def _(act):
            def weights_hi(f, ms=(0, 1, 2)):
                for m in ms:
                    act.wait_ge(unpacked, 3 * f + m + 1)
                    hi, src = split_views(m, f, HI)
                    nc.scalar.activation(hi, src, ACT.Copy).then_inc(w_hi, 1)

            def transposed_hi(n, tiles):
                act.wait_ge(t_done, 4 * n + tiles[-1] + 1)
                if type(n) is not int:
                    nc.scalar.copy(nop[:], ident[:, 0:1])
                for j, t in enumerate(tiles):
                    nc.scalar.activation(xs[:, n % 2, HI, :, t * P:(t + 1) * P],
                                         bank_pair(n, tiles)[j][:].rearrange("p (k t) -> p k t", k=DC),
                                         ACT.Copy).then_inc(t_hi, 1)

            def hidden(n, index, f):
                k, w = FT * n + f, width(f)
                act.wait_ge(a_done, k + 1)
                act.wait_ge(h_lo, k - reuse(f) + 1 + HLO0)
                nc.scalar.activation(hb[0:w, f % 2], ab[index % 2][0][0:w], ACT.Silu).then_inc(silu_done, 1)
                act.wait_ge(h_used, k - reuse(f) + 1 + HU0)
                act.wait_ge(ab_free, before(n, index) + 1)
                nc.scalar.activation(hs[0:w, f % 2, HI], hb[0:w, f % 2], ACT.Copy).then_inc(h_hi, 1)

            def block_of(n, first, last):
                for index, (kind, what) in enumerate(items(last)):
                    if kind == "t":
                        transposed_hi(n + 1, what)
                        continue
                    hidden(n, index, what)
                    if first and what + 2 < FT:
                        weights_hi(what + 2)
                    if what == 0 and not first:
                        norm2.square_root(act, n - 1)
                    if what == 2 and not last:
                        norm1.square_root(act, n + 1)

            norm1.square_root(act, 0)
            transposed_hi(0, TURN[0][1])
            transposed_hi(0, TURN[1][1])
            weights_hi(0, (0, 1))
            transposed_hi(0, TURN[2][1])
            weights_hi(0, (2,))
            weights_hi(1)
            block_of(0, True, False)
            with act.Fori(1, NBLK - 1) as n:
                block_of(n, False, False)
            block_of(NBLK - 1, False, True)
            norm2.square_root(act, NBLK - 1)

        @block.vector
        def _(dve):
            dve.sem_inc(h_lo, HLO0)
            dve.sem_inc(z_done, Z0)

            def multiply(f, m, rows, cols):
                v = sl[0:rows, f % 2, m, 0:cols]
                nc.vector.tensor_tensor(v, pk[0:rows, f % 2, m, 0:cols], v, ALU.mult).then_inc(unpacked, 1)

            def unpack_up(f):
                n, b = width(f), f % 2
                dve.wait_ge(pk_in[b], 16 * LOADS * (f // 2 + 1))
                for m in range(2):
                    v = pk[:, b, m, 0:DC * n]
                    nc.vector.tensor_scalar(v, v, sh[:, 0, 0:1], sh[:, 0, 1:2], ALU.logical_shift_left,
                                            ALU.arith_shift_right).then_inc(shifted, 1)
                for m in range(2):
                    dve.wait_ge(shifted, 6 * f + 1 + m)
                    multiply(f, m, P, DC * n)

            def unpack_down(f):
                n, b = width(f), f % 2
                for c in range(4):
                    v = pk[0:n, b, 2, c * P:(c + 1) * P]
                    nc.vector.tensor_scalar(v, v, sh[0:n, 1 + c, 0:1], sh[0:n, 1 + c, 1:2], ALU.logical_shift_left,
                                            ALU.arith_shift_right).then_inc(shifted, 1)
                dve.wait_ge(shifted, 6 * f + 6)
                multiply(f, 2, n, D)

            def transposed_lo(n, tiles):
                for j, t in enumerate(tiles):
                    dve.wait_ge(t_hi, 4 * n + t + 1)
                    nc.vector.tensor_tensor(xs[:, n % 2, LO, :, t * P:(t + 1) * P],
                                            bank_pair(n, tiles)[j][:].rearrange("p (k t) -> p k t", k=DC),
                                            xs[:, n % 2, HI, :, t * P:(t + 1) * P], ALU.subtract)\
                        .then_inc(ab_free if t == tiles[-1] else t_lo, 1)

            def gate(n, index, f):
                k, w = FT * n + f, width(f)
                dve.wait_ge(silu_done, k + 1)
                dve.wait_ge(b_done, k + 1)
                nc.vector.tensor_tensor(hb[0:w, f % 2], ab[index % 2][1][0:w], hb[0:w, f % 2], ALU.mult)\
                    .then_inc(ab_free, 1)

            def hidden_lo(n, f):
                w = width(f)
                dve.wait_ge(h_hi, FT * n + f + 1)
                nc.vector.tensor_tensor(hs[0:w, f % 2, LO], hb[0:w, f % 2], hs[0:w, f % 2, HI], ALU.subtract)\
                    .then_inc(h_lo, 1)

            def residual(n):
                dve.wait_ge(x1_in, 16 * n + 16)
                for t in range(4):
                    if t < 3:
                        dve.wait_ge(y_done, 3 * n + t + 1)
                    else:
                        dve.wait_ge(h_used, FT * (n + 1) + HU0)
                    nc.vector.tensor_tensor(norm2.tile(t), yps[t][:], norm2.tile(t), ALU.add).then_inc(z_done, 1)

            def statistics2(n):
                dve.wait_ge(z_done, 4 * n + 4 + Z0)
                nc.vector.memset(norm2.tmp[:], 0.0)
                norm2.statistics(dve, n)

            def statistics1(n):
                dve.wait_ge(y_in, 16 * n + 16)
                nc.vector.memset(norm1.tmp[:], 0.0)
                norm1.statistics(dve, n)

            def block_of(n, first, last):
                for index, (kind, what) in enumerate(items(last)):
                    if kind == "t":
                        transposed_lo(n + 1, what)
                        continue
                    gate(n, index, what)
                    if what == 0 and not first:
                        residual(n - 1)
                    hidden_lo(n, what)
                    if first and what + 2 < FT:
                        unpack_up(what + 2)
                        unpack_down(what + 2)
                    if what == 0 and not first:
                        statistics2(n - 1)
                    if what == 1 and not first:
                        norm2.normalise(dve, n - 1)
                    if what == 2 and not last:
                        statistics1(n + 1)
                    if what == 3 and not last:
                        norm1.normalise(dve, n + 1)

            norm1.statistics(dve, 0, y0_in)
            norm1.normalise(dve, 0)
            dve.wait_ge(sh_in, 16)
            unpack_up(0)
            for _, tiles in TURN:
                transposed_lo(0, tiles)
            unpack_down(0)
            unpack_up(1)
            unpack_down(1)
            block_of(0, True, False)
            with dve.Fori(1, NBLK - 1) as n:
                block_of(n, False, False)
            block_of(NBLK - 1, False, True)
            residual(NBLK - 1)
            statistics2(NBLK - 1)
            norm2.normalise(dve, NBLK - 1)

        @block.tensor
        def _(pe):
            pe.sem_inc(h_used, HU0)

            def transposes(n, tiles):
                pe.wait_ge(norm1.done, 4 * n + tiles[-1] + 1)
                for j, t in enumerate(tiles):
                    for k in range(DC):
                        last = nc.tensor.transpose(bank_pair(n, tiles)[j][:, k * P:(k + 1) * P],
                                                   yb[:, t, k * P:(k + 1) * P], ident[:])
                    last.then_inc(t_done, 1)

            def up(n, index, f):
                w = width(f)
                cols = slice(f * P, f * P + w)
                for m, (wt, done) in enumerate(((w1, a_done), (w3, b_done))):
                    pe.wait_ge(w_lo, 3 * f + m + 1)
                    three_pass(nc, ab[index % 2][m][0:w],
                               [(lambda p, k=k: wt[:, p, k, cols], lambda p, k=k: xs[:, n % 2, p, k])
                                for k in range(DC)]).then_inc(done, 1)

            def item(n, index, kind, what):
                pe.wait_ge(ab_free, before(n, index) - 1)
                if kind == "t":
                    transposes(n + 1, what)
                else:
                    up(n, index, what)

            def down(n, f):
                w = width(f)
                pe.wait_ge(w_lo, 3 * f + 3)
                pe.wait_ge(h_lo, FT * n + f + 1 + HLO0)
                if f == 0:
                    pe.wait_ge(z_done, 4 * n + Z0)
                for t in range(4):
                    for k, (a, b) in enumerate(PASSES):
                        last = nc.tensor.matmul(yps[t][:], hs[0:w, f % 2, a, t * P:(t + 1) * P], w2[0:w, b, f],
                                                start=(f == 0 and k == 0), stop=(f == FT - 1 and k == 2))
                    if f == FT - 1 and t < 3:
                        last.then_inc(y_done, 1)
                last.then_inc(h_used, 1)

            def block_of(n, last):
                todo = list(enumerate(items(last)))[1:]
                for f in range(FT):
                    while todo:
                        index, (kind, what) = todo.pop(0)
                        item(n, index, kind, what)
                        if kind == "f":
                            break
                    if f == FT - 1 and not last:
                        item(n + 1, 0, "f", 0)
                    down(n, f)

            pe.wait_ge(ids, 2)
            for index, (_, tiles) in enumerate(TURN):
                if index >= 2:
                    pe.wait_ge(ab_free, index - 1)
                transposes(0, tiles)
            pe.wait_ge(ab_free, AHEAD)
            up(0, 0, 0)
            with pe.Fori(0, NBLK - 1) as n:
                block_of(n, False)
            block_of(NBLK - 1, True)


def kernel(L0_attn_hidden_states, L0_attn_Wq, L0_attn_Wkr, L0_attn_Wdk, L0_attn_Wupk, L0_attn_Wupv, L0_attn_Wo,
           L0_ffn_w1, L0_ffn_s1, L0_ffn_w2, L0_ffn_s2, L0_ffn_w3, L0_ffn_s3):
    import concourse.bacc as bacc
    from concourse.bass_utils import run_bass_kernel_spmd

    x = np.asarray(L0_attn_hidden_states)

    def chunked(wT, n):
        return wT.reshape(DC, P, n).transpose(1, 0, 2)

    def quads(w):
        w = np.asarray(w).reshape(2, 4, 2, 32, D).transpose(0, 2, 1, 3, 4).reshape(512, D)
        return chunked(w.T, 512)

    def packed_up(w):
        w = np.asarray(w).reshape(F, 4, 64).transpose(2, 1, 0)
        return np.concatenate([w, w])

    def scales_up(s):
        return np.asarray(s).reshape(F, 4, 2).transpose(2, 1, 0)

    def by_tile(w1, w3):
        both = np.stack([w1, w3], axis=1)
        return np.concatenate([both[..., f * P:(f + 1) * P].reshape(len(both), -1) for f in range(FT)], axis=1)

    d = np.arange(D).reshape(P, 4).T.reshape(-1)
    flat = F * d[None, :] + np.arange(F)[:, None]
    w2p = np.asarray(L0_ffn_w2)[flat // P, flat % 64]
    s2p = np.asarray(L0_ffn_s2)[flat // 64]

    inv_freq = 1.0 / 10000.0 ** (np.arange(0, HD, 2, dtype=np.float32) / HD)
    emb = np.outer(np.arange(S, dtype=np.float32), inv_freq)
    emb = np.concatenate([emb, emb], axis=-1)
    cosT = np.cos(emb).astype(np.float32).T
    sinT = np.sin(emb).astype(np.float32).T.copy()
    sinT[:HD // 2] *= -1
    shifts = np.zeros((P, 5, 2), np.int32)
    p = np.arange(P)
    for k in range(5):
        low = (p if k == 0 else (F % P * (k - 1) + p) % P) >= 64
        shifts[:, k, 0] = np.where(low, 28, 0)
        shifts[:, k, 1] = np.where(low, 28, 4)

    arrays = {
        "x": x,
        "xT": x.reshape(NBLK, TB, DC, P).transpose(0, 3, 2, 1),
        "wqT": np.asarray(L0_attn_Wq).reshape(HEADS, HD, DC, P).transpose(0, 3, 2, 1),
        "wkrT": quads(L0_attn_Wkr),
        "wdkT": chunked(np.asarray(L0_attn_Wdk).T, C),
        "wupkT": quads(L0_attn_Wupk),
        "wupvT": chunked(np.asarray(L0_attn_Wupv).T, KV * HD),
        "woT": np.asarray(L0_attn_Wo).T.reshape(HEADS, HD, D),
        "w13p": by_tile(packed_up(L0_ffn_w1), packed_up(L0_ffn_w3)),
        "s13p": by_tile(scales_up(L0_ffn_s1), scales_up(L0_ffn_s3)),
        "w2p": w2p, "s2p": s2p,
        "cosT": cosT, "sinT": sinT, "shifts": shifts,
    }
    nc = bacc.Bacc("TRN2", target_bir_lowering=False, num_devices=1)
    feeds, args = {}, []
    for name, a in arrays.items():
        a = np.ascontiguousarray(a)
        feeds[f"in_{name}"] = a
        args.append(nc.dram_tensor(f"in_{name}", a.shape, mybir.dt.from_np(a.dtype), kind="ExternalInput").ap())
    args.append(nc.dram_tensor("out", (NBLK, 4, P, D), F32, kind="ExternalOutput").ap())
    program(nc, *args)
    result = run_bass_kernel_spmd(nc, [feeds], core_ids=[0])
    return result.results[0]["out"].reshape(B, S, D)
```
